# Optimizing a Trainium2 kernel written in Bass

```python
import numpy as np
import jax
import jax.numpy as jnp

def _softmax(x, axis=-1):
    return jax.nn.softmax(x, axis=axis)

def _gelu(x):
    return jax.nn.gelu(x, approximate=True)

def _silu(x):
    return jax.nn.silu(x)

def _sigmoid(x):
    return jax.nn.sigmoid(x)

def _layernorm(x, axis=-1, eps=1e-05):
    m = jnp.mean(x, axis=axis, keepdims=True)
    v = jnp.var(x, axis=axis, keepdims=True)
    return (x - m) / jnp.sqrt(v + eps)

def _scatter_add(tgt, idx, src, axis=0):
    return tgt.at[idx].add(src)

def _segment_sum(src, seg, n):
    return jax.ops.segment_sum(src, seg, n)
kernel_name = 'mk_xattn_seq_d4_seqx_r4_cf1757'

def setup_inputs(seed: int=0):
    np.random.seed(seed)
    _w = jnp.asarray

    def _rec_inputs():
        import jax
        import jax.numpy as jnp
        _rk = jax.random.key(seed)
        x = -0.0005207 + 1.001 * jax.random.normal(jax.random.fold_in(_rk, 1), (32, 100, 256), jnp.float32)
        _lenS = 100 - jax.random.randint(jax.random.fold_in(_rk, 7), (32,), 0, max(1, 100 // 4) + 1, jnp.int32)
        _lenS2 = 361 - jax.random.randint(jax.random.fold_in(_rk, 8), (32,), 0, max(1, 361 // 4) + 1, jnp.int32)
        _ctx_1024P = jax.random.normal(jax.random.fold_in(_rk, 12), (32, 16, 256), jnp.float32)
        _ctx_1024c = jax.random.dirichlet(jax.random.fold_in(_rk, 512), 0.3 * jnp.ones((16,), jnp.float32), (32, 361))
        _ctx_1024t = jnp.einsum('bsk,bkd->bsd', _ctx_1024c, _ctx_1024P)
        _ctx_1024t = _ctx_1024t * jax.lax.rsqrt(jnp.mean(jnp.square(_ctx_1024t)) + 1e-12) * 0.953939
        ctx_1024 = -0.000514642 + 1.00011 * (_ctx_1024t + 0.3 * jax.random.normal(jax.random.fold_in(_rk, 612), (32, 361, 256), jnp.float32))
        _validS = jnp.arange(100)[None, :] < _lenS[:, None]
        _validS2 = jnp.arange(361)[None, :] < _lenS2[:, None]
        _causal = jnp.tril(jnp.ones((100, 100), dtype=bool))
        mask_1x1xSxS2_ff0 = jnp.where(jnp.ones((1, 1, 100, 361), dtype=bool), 0.0, -1000000000.0).astype(jnp.float32)
        mask_1xSxS2_bk1 = jnp.broadcast_to(_validS2[0:1, None, :], (1, 100, 361))
        mask_Bx1xSxS2_ff0 = jnp.where(jnp.ones((32, 1, 100, 361), dtype=bool), 0.0, -1000000000.0).astype(jnp.float32)
        return (x, ctx_1024, mask_1x1xSxS2_ff0, mask_1xSxS2_bk1, mask_Bx1xSxS2_ff0)
    x, ctx_1024, mask_1x1xSxS2_ff0, mask_1xSxS2_bk1, mask_Bx1xSxS2_ff0 = _rec_inputs()

    def _L0_xattn_setup():
        import jax, jax.numpy as jnp
        import numpy as np
        B, Q, C, H, N, D, F = (1, 512, 512, 256, 16, 64, 1024)
        R = Q + C
        EPS = 1e-12
        NEG = 1e+30

        def _layernorm(x, g, b):
            m = jnp.mean(x, axis=-1, keepdims=True)
            v = jnp.mean(jnp.square(x - m), axis=-1, keepdims=True)
            return (x - m) * jax.lax.rsqrt(v + EPS) * g + b

        def _rel_shift(x, klen):
            b, n, q, r = x.shape
            x = x.reshape(b, n, r, q)[:, :, 1:, :].reshape(b, n, q, r - 1)
            return x[:, :, :, :klen]
        key = jax.random.key(seed)
        ks = jax.random.split(key, 16)
        s = 0.02
        return dict(content_stream=jax.random.normal(ks[0], (B, Q, H), jnp.float32), content_mask=jnp.zeros((B, 1, Q, C), jnp.float32), context=jax.random.normal(ks[1], (B, C, H), jnp.float32), position_encoding=jax.random.normal(ks[2], (B, R, H), jnp.float32), content_bias=jax.random.normal(ks[3], (N, D), jnp.float32) * s, position_bias=jax.random.normal(ks[4], (N, D), jnp.float32) * s, segment_encoding=jax.random.normal(ks[5], (2, N, D), jnp.float32) * s, segment_matrix=jax.random.randint(ks[6], (B, Q, C), 0, 2).astype(bool), segment_bias=jax.random.normal(ks[7], (N, D), jnp.float32) * s, Wq=jax.random.normal(ks[8], (H, N, D), jnp.float32) * s, Wk=jax.random.normal(ks[9], (H, N, D), jnp.float32) * s, Wv=jax.random.normal(ks[10], (H, N, D), jnp.float32) * s, Wr=jax.random.normal(ks[11], (H, N, D), jnp.float32) * s, Wo=jax.random.normal(ks[12], (H, N, D), jnp.float32) * s, ln1_gamma=jnp.ones((H,), jnp.float32), ln1_beta=jnp.zeros((H,), jnp.float32), W1=jax.random.normal(ks[13], (H, F), jnp.float32) * s, b1=jnp.zeros((F,), jnp.float32), W2=jax.random.normal(ks[14], (F, H), jnp.float32) * s, b2=jnp.zeros((H,), jnp.float32), ln2_gamma=jnp.ones((H,), jnp.float32), ln2_beta=jnp.zeros((H,), jnp.float32))
    _L0_xattn_all = _L0_xattn_setup()
    _L0_xattn_in = {k: v for k, v in _L0_xattn_all.items() if k in ('position_encoding', 'content_bias', 'position_bias', 'segment_encoding', 'segment_bias', 'Wq', 'Wk', 'Wv', 'Wr', 'Wo', 'ln1_gamma', 'ln1_beta', 'W1', 'b1', 'W2', 'b2', 'ln2_gamma', 'ln2_beta')}
    del _L0_xattn_all

    def _L1_xattn_setup():
        import jax, jax.numpy as jnp
        import numpy as np
        B, N, DIM = (2, 512, 256)
        HEADS, DH = (16, 64)
        SEG = 128
        NPM = 16
        NM = 16
        DFF = int(DIM * 4 * 2 / 3)
        EPS = 1.1920929e-07

        def rms_norm(x, w):
            return x * jax.lax.rsqrt(jnp.mean(x * x, axis=-1, keepdims=True) + EPS) * w
        key = jax.random.key(seed)
        ks = jax.random.split(key, 10)
        p = lambda i, shape: jax.random.normal(ks[i], shape, jnp.float32) * 0.02
        return {'x': jax.random.normal(ks[0], (B, N, DIM), jnp.float32), 'mem_out': jax.random.normal(ks[1], (B, N, DIM), jnp.float32), 'attn_norm_w': jnp.ones((DIM,), jnp.float32), 'to_qkv_w': p(2, (DIM, 3 * HEADS * DH)), 'to_out_w': p(3, (HEADS * DH, DIM)), 'persist_mem': jax.random.normal(ks[4], (HEADS, NPM, DH), jnp.float32), 'mem_pool_norm_w': jnp.ones((DIM,), jnp.float32), 'to_mem_tokens_w': p(5, (DIM, DIM)), 'ff_norm_w': jnp.ones((DIM,), jnp.float32), 'ff_w1': p(6, (DIM, 2 * DFF)), 'ff_b1': jnp.zeros((2 * DFF,), jnp.float32), 'ff_w2': p(7, (DFF, DIM)), 'ff_b2': jnp.zeros((DIM,), jnp.float32)}
    _L1_xattn_all = _L1_xattn_setup()
    _L1_xattn_in = {k: v for k, v in _L1_xattn_all.items() if k in ('attn_norm_w', 'to_qkv_w', 'to_out_w', 'persist_mem', 'mem_pool_norm_w', 'to_mem_tokens_w', 'ff_norm_w', 'ff_w1', 'ff_b1', 'ff_w2', 'ff_b2')}
    del _L1_xattn_all

    def _L2_xattn_setup():
        import jax, jax.numpy as jnp
        import numpy as np
        import math
        H, NH, NKV, HD, FF = (256, 16, 4, 64, 1024)
        B, S = (2, 512)
        EPS, THETA = (1e-06, 10000.0)

        def _rmsnorm(x, w, eps=EPS):
            v = jnp.mean(x.astype(jnp.float32) ** 2, axis=-1, keepdims=True)
            return (x.astype(jnp.float32) * jax.lax.rsqrt(v + eps)).astype(x.dtype) * w

        def _rope_tables(seq_len, head_dim, theta=THETA):
            inv_freq = 1.0 / theta ** (jnp.arange(0, head_dim, 2, dtype=jnp.float32) / head_dim)
            freqs = jnp.arange(seq_len, dtype=jnp.float32)[:, None] * inv_freq[None, :]
            emb = jnp.concatenate([freqs, freqs], axis=-1)
            return (jnp.cos(emb), jnp.sin(emb))

        def _rotate_half(x):
            x1, x2 = jnp.split(x, 2, axis=-1)
            return jnp.concatenate([-x2, x1], axis=-1)

        def _apply_rope(x, cos, sin):
            return x * cos[None, None] + _rotate_half(x) * sin[None, None]
        key = jax.random.key(seed)
        ks = jax.random.split(key, 12)
        std = 0.02
        return {'hidden_states': jax.random.normal(ks[0], (B, S, H), jnp.float32), 'kv_states': jax.random.normal(ks[1], (B, S, H), jnp.float32), 'attention_mask': jnp.zeros((B, 1, S, S), jnp.float32), 'ln1_w': jnp.ones((H,), jnp.float32), 'ln2_w': jnp.ones((H,), jnp.float32), 'Wq': jax.random.normal(ks[2], (H, NH * HD), jnp.float32) * std, 'Wk': jax.random.normal(ks[3], (H, NKV * HD), jnp.float32) * std, 'Wv': jax.random.normal(ks[4], (H, NKV * HD), jnp.float32) * std, 'Wo': jax.random.normal(ks[5], (NH * HD, H), jnp.float32) * std, 'Wgate': jax.random.normal(ks[6], (H, FF), jnp.float32) * std, 'Wup': jax.random.normal(ks[7], (H, FF), jnp.float32) * std, 'Wdown': jax.random.normal(ks[8], (FF, H), jnp.float32) * std}
    _L2_xattn_all = _L2_xattn_setup()
    _L2_xattn_in = {k: v for k, v in _L2_xattn_all.items() if k in ('ln1_w', 'ln2_w', 'Wq', 'Wk', 'Wv', 'Wo', 'Wgate', 'Wup', 'Wdown')}
    del _L2_xattn_all

    def _L3_xattn_setup():
        import jax, jax.numpy as jnp
        import numpy as np
        D_MODEL = 256
        NUM_HEADS = 16
        HEAD_DIM = D_MODEL // NUM_HEADS
        EPS = 1e-06

        def rmsnorm(x, w):
            xf = x.astype(jnp.float32)
            n = xf * jax.lax.rsqrt(jnp.mean(xf * xf, axis=-1, keepdims=True) + EPS)
            return (n * w.astype(jnp.float32)).astype(x.dtype)
        key = jax.random.key(seed)
        ks = jax.random.split(key, 8)
        B, S, K = (4, 512, 512)
        s = 1.0 / np.sqrt(D_MODEL)
        return {'x': jax.random.normal(ks[0], (B, S, D_MODEL), jnp.float32), 'kv': jax.random.normal(ks[1], (B, K, D_MODEL), jnp.float32), 'wq': jax.random.normal(ks[2], (D_MODEL, D_MODEL), jnp.float32) * s, 'wk': jax.random.normal(ks[3], (D_MODEL, D_MODEL), jnp.float32) * s, 'wv': jax.random.normal(ks[4], (D_MODEL, D_MODEL), jnp.float32) * s, 'wo': jax.random.normal(ks[5], (D_MODEL, D_MODEL), jnp.float32) * s, 'bo': jnp.zeros((D_MODEL,), jnp.float32), 'gq': jnp.ones((D_MODEL,), jnp.float32), 'gkv': jnp.ones((D_MODEL,), jnp.float32)}
    _L3_xattn_all = _L3_xattn_setup()
    _L3_xattn_in = {k: v for k, v in _L3_xattn_all.items() if k in ('wq', 'wk', 'wv', 'wo', 'bo', 'gq', 'gkv')}
    del _L3_xattn_all
    return {'x': x, 'ctx_1024': ctx_1024, 'mask_1x1xSxS2_ff0': mask_1x1xSxS2_ff0, 'mask_1xSxS2_bk1': mask_1xSxS2_bk1, 'mask_Bx1xSxS2_ff0': mask_Bx1xSxS2_ff0, 'L0_xattn_position_encoding': _L0_xattn_in['position_encoding'], 'L0_xattn_content_bias': _L0_xattn_in['content_bias'], 'L0_xattn_position_bias': _L0_xattn_in['position_bias'], 'L0_xattn_segment_encoding': _L0_xattn_in['segment_encoding'], 'L0_xattn_segment_bias': _L0_xattn_in['segment_bias'], 'L0_xattn_Wq': _L0_xattn_in['Wq'], 'L0_xattn_Wk': _L0_xattn_in['Wk'], 'L0_xattn_Wv': _L0_xattn_in['Wv'], 'L0_xattn_Wr': _L0_xattn_in['Wr'], 'L0_xattn_Wo': _L0_xattn_in['Wo'], 'L0_xattn_ln1_gamma': _L0_xattn_in['ln1_gamma'], 'L0_xattn_ln1_beta': _L0_xattn_in['ln1_beta'], 'L0_xattn_W1': _L0_xattn_in['W1'], 'L0_xattn_b1': _L0_xattn_in['b1'], 'L0_xattn_W2': _L0_xattn_in['W2'], 'L0_xattn_b2': _L0_xattn_in['b2'], 'L0_xattn_ln2_gamma': _L0_xattn_in['ln2_gamma'], 'L0_xattn_ln2_beta': _L0_xattn_in['ln2_beta'], 'L1_xattn_attn_norm_w': _L1_xattn_in['attn_norm_w'], 'L1_xattn_to_qkv_w': _L1_xattn_in['to_qkv_w'], 'L1_xattn_to_out_w': _L1_xattn_in['to_out_w'], 'L1_xattn_persist_mem': _L1_xattn_in['persist_mem'], 'L1_xattn_mem_pool_norm_w': _L1_xattn_in['mem_pool_norm_w'], 'L1_xattn_to_mem_tokens_w': _L1_xattn_in['to_mem_tokens_w'], 'L1_xattn_ff_norm_w': _L1_xattn_in['ff_norm_w'], 'L1_xattn_ff_w1': _L1_xattn_in['ff_w1'], 'L1_xattn_ff_b1': _L1_xattn_in['ff_b1'], 'L1_xattn_ff_w2': _L1_xattn_in['ff_w2'], 'L1_xattn_ff_b2': _L1_xattn_in['ff_b2'], 'L2_xattn_ln1_w': _L2_xattn_in['ln1_w'], 'L2_xattn_ln2_w': _L2_xattn_in['ln2_w'], 'L2_xattn_Wq': _L2_xattn_in['Wq'], 'L2_xattn_Wk': _L2_xattn_in['Wk'], 'L2_xattn_Wv': _L2_xattn_in['Wv'], 'L2_xattn_Wo': _L2_xattn_in['Wo'], 'L2_xattn_Wgate': _L2_xattn_in['Wgate'], 'L2_xattn_Wup': _L2_xattn_in['Wup'], 'L2_xattn_Wdown': _L2_xattn_in['Wdown'], 'L3_xattn_wq': _L3_xattn_in['wq'], 'L3_xattn_wk': _L3_xattn_in['wk'], 'L3_xattn_wv': _L3_xattn_in['wv'], 'L3_xattn_wo': _L3_xattn_in['wo'], 'L3_xattn_bo': _L3_xattn_in['bo'], 'L3_xattn_gq': _L3_xattn_in['gq'], 'L3_xattn_gkv': _L3_xattn_in['gkv']}

def reference(x, ctx_1024, mask_1x1xSxS2_ff0, mask_1xSxS2_bk1, mask_Bx1xSxS2_ff0, L0_xattn_position_encoding, L0_xattn_content_bias, L0_xattn_position_bias, L0_xattn_segment_encoding, L0_xattn_segment_bias, L0_xattn_Wq, L0_xattn_Wk, L0_xattn_Wv, L0_xattn_Wr, L0_xattn_Wo, L0_xattn_ln1_gamma, L0_xattn_ln1_beta, L0_xattn_W1, L0_xattn_b1, L0_xattn_W2, L0_xattn_b2, L0_xattn_ln2_gamma, L0_xattn_ln2_beta, L1_xattn_attn_norm_w, L1_xattn_to_qkv_w, L1_xattn_to_out_w, L1_xattn_persist_mem, L1_xattn_mem_pool_norm_w, L1_xattn_to_mem_tokens_w, L1_xattn_ff_norm_w, L1_xattn_ff_w1, L1_xattn_ff_b1, L1_xattn_ff_w2, L1_xattn_ff_b2, L2_xattn_ln1_w, L2_xattn_ln2_w, L2_xattn_Wq, L2_xattn_Wk, L2_xattn_Wv, L2_xattn_Wo, L2_xattn_Wgate, L2_xattn_Wup, L2_xattn_Wdown, L3_xattn_wq, L3_xattn_wk, L3_xattn_wv, L3_xattn_wo, L3_xattn_bo, L3_xattn_gq, L3_xattn_gkv):
    import jax
    import jax.numpy as jnp

    def _L0_xattn_ref(content_stream, content_mask, context, position_encoding, content_bias, position_bias, segment_encoding, segment_matrix, segment_bias, Wq, Wk, Wv, Wr, Wo, ln1_gamma, ln1_beta, W1, b1, W2, b2, ln2_gamma, ln2_beta):
        import jax, jax.numpy as jnp
        import numpy as np
        B, Q, C, H, N, D, F = (1, 512, 512, 256, 16, 64, 1024)
        R = Q + C
        EPS = 1e-12
        NEG = 1e+30

        def _layernorm(x, g, b):
            m = jnp.mean(x, axis=-1, keepdims=True)
            v = jnp.mean(jnp.square(x - m), axis=-1, keepdims=True)
            return (x - m) * jax.lax.rsqrt(v + EPS) * g + b

        def _rel_shift(x, klen):
            b, n, q, r = x.shape
            x = x.reshape(b, n, r, q)[:, :, 1:, :].reshape(b, n, q, r - 1)
            return x[:, :, :, :klen]
        q = jnp.einsum('bqh,hnd->bqnd', content_stream, Wq)
        k = jnp.einsum('bch,hnd->bcnd', context, Wk)
        v = jnp.einsum('bch,hnd->bcnd', context, Wv)
        r = jnp.einsum('brh,hnd->brnd', position_encoding, Wr)
        ac = jnp.einsum('bqnd,bcnd->bnqc', q + content_bias, k)
        bd = _rel_shift(jnp.einsum('bqnd,brnd->bnqr', q + position_bias, r), k.shape[1])
        ef = jnp.einsum('bqnd,snd->bnqs', q + segment_bias, segment_encoding)
        ef = jnp.where(segment_matrix[:, None], ef[..., 1:], ef[..., :1])
        scores = (ac + bd + ef) / jnp.sqrt(jnp.float32(D))
        scores = scores - NEG * content_mask
        probs = jax.nn.softmax(scores, axis=-1)
        attn = jnp.einsum('bnqc,bcnd->bqnd', probs, v)
        attn_out = jnp.einsum('bqnd,hnd->bqh', attn, Wo)
        ffn_in = _layernorm(attn_out + content_stream, ln1_gamma, ln1_beta)
        ffn_out = jax.nn.relu(ffn_in @ W1 + b1) @ W2 + b2
        return _layernorm(ffn_out + ffn_in, ln2_gamma, ln2_beta)

    def _L1_xattn_ref(x, mem_out, attn_norm_w, to_qkv_w, to_out_w, persist_mem, mem_pool_norm_w, to_mem_tokens_w, ff_norm_w, ff_w1, ff_b1, ff_w2, ff_b2):
        import jax, jax.numpy as jnp
        import numpy as np
        B, N, DIM = (2, 512, 256)
        HEADS, DH = (16, 64)
        SEG = 128
        NPM = 16
        NM = 16
        DFF = int(DIM * 4 * 2 / 3)
        EPS = 1.1920929e-07

        def rms_norm(x, w):
            return x * jax.lax.rsqrt(jnp.mean(x * x, axis=-1, keepdims=True) + EPS) * w
        b, n, _ = x.shape
        split_heads = lambda t: t.reshape(b, -1, HEADS, DH).transpose(0, 2, 1, 3)
        pooled = rms_norm(mem_out.mean(axis=1), mem_pool_norm_w)
        mem_tok = jnp.broadcast_to((pooled @ to_mem_tokens_w)[:, None, :], (b, NM, DIM))
        _, k_c, v_c = jnp.split(mem_tok @ to_qkv_w, 3, axis=-1)
        k_extra, v_extra = (split_heads(k_c), split_heads(v_c))
        xn = rms_norm(x, attn_norm_w)
        q, k, v = jnp.split(xn @ to_qkv_w, 3, axis=-1)
        q, k, v = (split_heads(q), split_heads(k), split_heads(v))
        pos = jnp.arange(n)
        inv = 1.0 / 10000.0 ** (jnp.arange(0, DH, 2, dtype=jnp.float32) / DH)
        ang = jnp.repeat(pos[:, None].astype(jnp.float32) * inv[None, :], 2, axis=-1)
        cos, sin = (jnp.cos(ang), jnp.sin(ang))

        def rope(t):
            z = t.reshape(t.shape[:-1] + (-1, 2))
            rh = jnp.stack([-z[..., 1], z[..., 0]], axis=-1).reshape(t.shape)
            return t * cos + rh * sin
        q, k = (rope(q), rope(k))
        pm = jnp.broadcast_to(persist_mem[None], (b, HEADS, NPM, DH))
        kf = jnp.concatenate([k_extra, pm, k], axis=2)
        vf = jnp.concatenate([v_extra, pm, v], axis=2)
        P = NPM + NM
        ki = jnp.arange(kf.shape[2])[None, :]
        qi = pos[:, None]
        causal = qi >= ki - P
        seg = qi // SEG == (ki - P) // SEG
        mask = causal & seg | (ki < P)
        scores = jnp.einsum('bhid,bhjd->bhij', q, kf) * DH ** (-0.5)
        scores = jnp.where(mask[None, None], scores, -1e+30)
        probs = jax.nn.softmax(scores, axis=-1)
        o = jnp.einsum('bhij,bhjd->bhid', probs, vf)
        attn_out = o.transpose(0, 2, 1, 3).reshape(b, n, HEADS * DH) @ to_out_w
        x = x + attn_out
        h = rms_norm(x, ff_norm_w) @ ff_w1 + ff_b1
        a, g = jnp.split(h, 2, axis=-1)
        x = x + jax.nn.silu(g) * a @ ff_w2 + ff_b2
        return x

    def _L2_xattn_ref(hidden_states, kv_states, attention_mask, ln1_w, ln2_w, Wq, Wk, Wv, Wo, Wgate, Wup, Wdown):
        import jax, jax.numpy as jnp
        import numpy as np
        import math
        H, NH, NKV, HD, FF = (256, 16, 4, 64, 1024)
        B, S = (2, 512)
        EPS, THETA = (1e-06, 10000.0)

        def _rmsnorm(x, w, eps=EPS):
            v = jnp.mean(x.astype(jnp.float32) ** 2, axis=-1, keepdims=True)
            return (x.astype(jnp.float32) * jax.lax.rsqrt(v + eps)).astype(x.dtype) * w

        def _rope_tables(seq_len, head_dim, theta=THETA):
            inv_freq = 1.0 / theta ** (jnp.arange(0, head_dim, 2, dtype=jnp.float32) / head_dim)
            freqs = jnp.arange(seq_len, dtype=jnp.float32)[:, None] * inv_freq[None, :]
            emb = jnp.concatenate([freqs, freqs], axis=-1)
            return (jnp.cos(emb), jnp.sin(emb))

        def _rotate_half(x):
            x1, x2 = jnp.split(x, 2, axis=-1)
            return jnp.concatenate([-x2, x1], axis=-1)

        def _apply_rope(x, cos, sin):
            return x * cos[None, None] + _rotate_half(x) * sin[None, None]
        bsz, q_len, _ = hidden_states.shape
        k_len = kv_states.shape[1]
        residual = hidden_states
        h = _rmsnorm(hidden_states, ln1_w)
        kv = _rmsnorm(kv_states, ln1_w)
        q = (h @ Wq).reshape(bsz, q_len, NH, HD).transpose(0, 2, 1, 3)
        k = (kv @ Wk).reshape(bsz, k_len, NKV, HD).transpose(0, 2, 1, 3)
        v = (kv @ Wv).reshape(bsz, k_len, NKV, HD).transpose(0, 2, 1, 3)
        cos_q, sin_q = _rope_tables(q_len, HD)
        cos_k, sin_k = _rope_tables(k_len, HD)
        q = _apply_rope(q, cos_q, sin_q)
        k = _apply_rope(k, cos_k, sin_k)
        groups = NH // NKV
        k = jnp.repeat(k, groups, axis=1)
        v = jnp.repeat(v, groups, axis=1)
        scores = jnp.einsum('bhqd,bhkd->bhqk', q, k) / math.sqrt(HD)
        scores = scores + attention_mask
        probs = jax.nn.softmax(scores.astype(jnp.float32), axis=-1).astype(q.dtype)
        attn = jnp.einsum('bhqk,bhkd->bhqd', probs, v)
        attn = attn.transpose(0, 2, 1, 3).reshape(bsz, q_len, NH * HD)
        attn = attn @ Wo
        hidden = residual + attn
        residual = hidden
        x = _rmsnorm(hidden, ln2_w)
        x = jax.nn.silu(x @ Wgate) * (x @ Wup) @ Wdown
        return residual + x

    def _L3_xattn_ref(x, kv, wq, wk, wv, wo, bo, gq, gkv):
        import jax, jax.numpy as jnp
        import numpy as np
        D_MODEL = 256
        NUM_HEADS = 16
        HEAD_DIM = D_MODEL // NUM_HEADS
        EPS = 1e-06

        def rmsnorm(x, w):
            xf = x.astype(jnp.float32)
            n = xf * jax.lax.rsqrt(jnp.mean(xf * xf, axis=-1, keepdims=True) + EPS)
            return (n * w.astype(jnp.float32)).astype(x.dtype)
        B, S, _ = x.shape
        K = kv.shape[1]
        xn = rmsnorm(x, gq)
        kvn = rmsnorm(kv, gkv)
        q = (xn @ wq.T).reshape(B, S, NUM_HEADS, HEAD_DIM)
        k = (kvn @ wk.T).reshape(B, K, NUM_HEADS, HEAD_DIM)
        v = (kvn @ wv.T).reshape(B, K, NUM_HEADS, HEAD_DIM)
        scale = HEAD_DIM ** (-0.5)
        scores = jnp.einsum('bshd,bkhd->bhsk', q, k) * scale
        attn = jax.nn.softmax(scores, axis=-1)
        o = jnp.einsum('bhsk,bkhd->bshd', attn, v).reshape(B, S, D_MODEL)
        out = o @ wo.T + bo
        return xn + out
    x = _L0_xattn_ref(x, mask_1x1xSxS2_ff0, ctx_1024, L0_xattn_position_encoding, L0_xattn_content_bias, L0_xattn_position_bias, L0_xattn_segment_encoding, mask_1xSxS2_bk1, L0_xattn_segment_bias, L0_xattn_Wq, L0_xattn_Wk, L0_xattn_Wv, L0_xattn_Wr, L0_xattn_Wo, L0_xattn_ln1_gamma, L0_xattn_ln1_beta, L0_xattn_W1, L0_xattn_b1, L0_xattn_W2, L0_xattn_b2, L0_xattn_ln2_gamma, L0_xattn_ln2_beta)
    x = _L1_xattn_ref(x, ctx_1024, L1_xattn_attn_norm_w, L1_xattn_to_qkv_w, L1_xattn_to_out_w, L1_xattn_persist_mem, L1_xattn_mem_pool_norm_w, L1_xattn_to_mem_tokens_w, L1_xattn_ff_norm_w, L1_xattn_ff_w1, L1_xattn_ff_b1, L1_xattn_ff_w2, L1_xattn_ff_b2)
    x = _L2_xattn_ref(x, ctx_1024, mask_Bx1xSxS2_ff0, L2_xattn_ln1_w, L2_xattn_ln2_w, L2_xattn_Wq, L2_xattn_Wk, L2_xattn_Wv, L2_xattn_Wo, L2_xattn_Wgate, L2_xattn_Wup, L2_xattn_Wdown)
    x = _L3_xattn_ref(x, ctx_1024, L3_xattn_wq, L3_xattn_wk, L3_xattn_wv, L3_xattn_wo, L3_xattn_bo, L3_xattn_gq, L3_xattn_gkv)
    return x

_drawn_inputs = setup_inputs


def setup_inputs(seed=0):
    import zlib

    import numpy as np

    out = dict(_drawn_inputs(seed))
    spreads = {'L0_xattn_ln1_gamma': (1.0, 0.2),
     'L0_xattn_ln1_beta': (0.0, 0.1),
     'L0_xattn_b1': (0.0, 0.1),
     'L0_xattn_b2': (0.0, 0.1),
     'L0_xattn_ln2_gamma': (1.0, 0.2),
     'L0_xattn_ln2_beta': (0.0, 0.1),
     'L1_xattn_attn_norm_w': (1.0, 0.6),
     'L1_xattn_mem_pool_norm_w': (1.0, 0.6),
     'L1_xattn_ff_norm_w': (1.0, 0.6),
     'L1_xattn_ff_b1': (0.0, 0.7),
     'L1_xattn_ff_b2': (0.0, 0.1),
     'L2_xattn_ln1_w': (1.0, 0.6),
     'L2_xattn_ln2_w': (1.0, 0.6),
     'L3_xattn_bo': (0.0, 0.1),
     'L3_xattn_gq': (1.0, 0.2),
     'L3_xattn_gkv': (1.0, 0.2)}
    factors = {'L0_xattn_position_encoding': 8.0,
     'L0_xattn_content_bias': 50.945,
     'L0_xattn_position_bias': 8.0,
     'L0_xattn_segment_encoding': 64.0,
     'L0_xattn_segment_bias': 200.0,
     'L0_xattn_Wq': 8.0,
     'L0_xattn_Wk': 8.0,
     'L0_xattn_Wr': 8.0,
     'L1_xattn_to_mem_tokens_w': 4.026,
     'L2_xattn_Wq': 8.0,
     'L2_xattn_Wk': 8.0}
    for name, (base, spread) in spreads.items():
        noise = np.random.default_rng([zlib.crc32(name.encode()), seed]).standard_normal(out[name].shape)
        drawn = base * np.exp(spread * noise) if base else spread * noise
        out[name] = jnp.asarray(drawn.astype(out[name].dtype))
    for name, factor in factors.items():
        out[name] = (out[name] * factor).astype(out[name].dtype)
    return out
```

```python
from contextlib import ExitStack

import numpy as np

import concourse.bass as bass
from concourse import mybir

F32 = mybir.dt.float32
F32R = mybir.dt.float32r
U8 = mybir.dt.uint8
ALU = mybir.AluOpType
ACT = mybir.ActivationFunctionType
AX = mybir.AxisListType

B, T, C, H = 32, 100, 361, 256
P = 128
KT = H // P
CT = 121
NCT = 3
CP = CT * NCT
CE = 362
NR = C + T - 1
UH = 8
UNITS = 2 * B
NEG = -1e30


class Signal:

    def __init__(self, nc, name, window, per, full, by=1):
        self.sem = nc.alloc_semaphore(name)
        self.window, self.per, self.full, self.by = window, per, full, by

    def at(self, u, i=None):
        i = self.per - 1 if i is None else i
        first, last = self.window
        if isinstance(u, int):
            before = self.per * max(0, min(u - 1, last) - first + 1)
            return self.by * (before + (i + 1 if first <= u <= last else 0))
        before = self.per * (self.full - first)
        return u * (self.per * self.by) + self.by * (before - self.full * self.per + i + 1)


def runs(window, u):
    return not isinstance(u, int) or window[0] <= u <= window[1]


def starts(u):
    return isinstance(u, int) and u == -1


def row(ap, i):
    if isinstance(i, int):
        return ap[i]
    names = " ".join(f"d{k}" for k in range(1, len(ap.shape)))
    rest = tuple(slice(None) for _ in ap.shape[1:])
    first = names.split()[0]
    return ap[(bass.ds(i, 1),) + rest].rearrange(f"a {names} -> (a {first}) " + " ".join(names.split()[1:]))


W_N, W_A, W_W, W_O = (-1, UNITS - 2), (0, UNITS - 1), (1, UNITS), (2, UNITS + 1)
A_FULL = 4


class Layer:

    def __init__(self, n, d, keys, key_tiles, aux):
        self.n, self.d = n, d
        self.dv = d + 2
        self.keys = keys
        self.key_tiles = key_tiles
        self.sw = key_tiles[-1][0] + key_tiles[-1][1]
        self.ncols = keys + keys % 2
        self.aux = aux
        self.ot = UH * d // P


LAYERS = [
    Layer(0, 64, C, [(0, CT), (CT, CT), (2 * CT, CT)],
          [["Q", "V"], ["V", "OT"], ["V", "G"], ["WO", "G"], ["K", "G", "G"], ["K", "G"], ["K", "G"], ["K", "G", "G"]]),
    Layer(1, 64, T + 32, [(0, T), (T, 32)],
          [["Q"], ["K"], ["V"], ["OT"], [], ["WO"], [], []]),
    Layer(2, 64, C, [(0, CT), (CT, CT), (2 * CT, CT)],
          [["Q"], ["K"], ["V"], ["OT"], [], ["WO"], [], []]),
    Layer(3, 16, C, [(0, CT), (CT, CT), (2 * CT, CT)],
          [["Q"], ["K"], ["K"], ["V"], ["OT"], [], ["WO"], []]),
]
AUX_WINDOW = {"Q": W_N, "K": W_N, "G": W_N, "V": W_A, "OT": W_O, "WO": W_O}


def attention(nc, ctx, L, W, io):
    n = L.n

    def sb(name, shape, dt=F32):
        return ctx.enter_context(nc.sbuf_tensor(f"a{n}_{name}", shape, dt))

    def sig(name, window, per, by=1):
        return Signal(nc, f"a{n}_{name}", window, per, A_FULL, by)

    S = [sb(f"scores{p}", [T, UH, L.sw]) for p in range(2)]
    V = [sb(f"values{p}", [CT, len(L.key_tiles), UH, L.dv]) for p in range(2)]
    PT = [sb(f"probsT{p}", [P, len(L.key_tiles) * T]) for p in range(2)]
    mx = [sb(f"rowmax{p}", [T, UH]) for p in range(2)]
    nb = [sb(f"expbias{p}", [T, UH]) for p in range(2)]
    rec = sb("recip", [T, 2, 4])
    On = sb("attn", [T, UH * L.d])
    OTs = sb("attnT", [P, L.ot * T])
    xres = sb("residual", [T, H])
    Yacc, Yout = sb("yacc", [T, H]), sb("yout", [T, H])
    xT = sb("queriesT", [P, KT, T])
    if n == 0:
        Kst = [sb(f"kstack{p}", [P, UH, CE], F32R) for p in range(2)]
        Qc = [sb(f"qc_hi{p}", [P, UH, T], F32R) for p in range(2)]
        Lc = [sb(f"qc_lo{p}", [P, UH // 2, T], F32R) for p in range(2)]
        Qp, Lp = sb("qp_hi", [P, UH, T], F32R), sb("qp_lo", [P, UH // 2, T], F32R)
        qcf, qpf = sb("qc", [P, 4, T]), sb("qp", [P, 4, T])
        e0 = [sb(f"seg0_{p}", [T, UH]) for p in range(2)]
        de = [sb(f"segd_{p}", [T, UH]) for p in range(2)]
        mtot = sb("maxtotal", [T, UH])
        Gs = [sb(f"relpos{g}", [T, 4, NR]) for g in range(2)]
        craw, chi, clo = sb("ctx", [P, KT, CE + 2]), sb("ctx_hi", [P, KT, CE + 2], F32R), sb("ctx_lo", [P, KT, CE + 2], F32R)
    if n == 1:
        Kn = [sb(f"keys{p}", [P, 4, L.keys]) for p in range(2)]
        qf = [sb(f"queries{p}", [P, 4, T]) for p in range(2)]
        xTv = sb("valuesT", [P, KT, T])
        qsw, qcos = sb("rope_swapped", [P, 4, T]), sb("rope_cos", [P, 4, T])
        ksw, kcos = sb("rope_kswapped", [P, 4, T]), sb("rope_kcos", [P, 4, T])
        Vx = [sb(f"extra_values{p}", [32, UH, L.dv]) for p in range(2)]
    if n == 2:
        Kst = [sb(f"kstack{p}", [P, 2, CE], F32R) for p in range(2)]
        Qh = [sb(f"q_hi{p}", [P, UH, T], F32R) for p in range(2)]
        Ql = [sb(f"q_lo{p}", [P, UH, T], F32R) for p in range(2)]
        qf, kf = sb("queries", [P, 4, T]), sb("keys", [P, CE])
        qsw, qcos = sb("rope_swapped", [P, 4, T]), sb("rope_cos", [P, 4, T])
        ksw, kcos = sb("rope_kswapped", [P, C]), sb("rope_kcos", [P, C])
        mask = [sb(f"mask{p}", [T, C]) for p in range(2)]
    if n == 3:
        Kst = [sb(f"kstack{p}", [P, 2, CE], F32R) for p in range(2)]
        khi = sb("k_hi", [P, 2, C], F32R)
        Qh = [sb(f"q_hi{p}", [P, 2, T], F32R) for p in range(2)]
        Ql = [sb(f"q_lo{p}", [P, 2, T], F32R) for p in range(2)]
    if n >= 2:
        cK, cV = sb("ctx_k", [P, KT, CE + 2]), sb("ctx_v", [P, KT, CE + 2])

    ps = [ctx.enter_context(nc.psum_tensor(f"a{n}_ps{k}", [P, 512], F32)) for k in range(8)]
    ac, aux, ptb, ob = ps[0:2], ps[2:4], ps[4:6], ps[6:8]

    setup = nc.alloc_semaphore(f"a{n}_setup")
    extras = nc.alloc_semaphore(f"a{n}_extras")
    sp_gate = nc.alloc_semaphore(f"a{n}_sp_gate")
    gate = nc.alloc_semaphore(f"a{n}_gate")
    ac_mm = sig("ac_mm", W_A, UH)
    scored = sig("scored", W_A, UH)
    biased = sig("biased", W_A, 1)
    maxed = sig("maxed", W_A, 1)
    probs = sig("probs", W_W, UH)
    pt_mm = sig("pt_mm", W_W, UH)
    pt_even = sig("pt_even", W_W, UH // 2)
    pt_odd = sig("pt_odd", W_W, UH // 2)
    pv_mm = sig("pv_mm", W_W, UH)
    recd = sig("recd", W_W, 2)
    normed = sig("normed", W_W, 2)
    count = {k: sum(s.count(k) for s in L.aux) for k in AUX_WINDOW}
    aux_mm = {k: sig(f"{k}_mm", AUX_WINDOW[k], c) for k, c in count.items() if c}
    done = {k: sig(f"{k}_done", AUX_WINDOW[k], c) for k, c in count.items() if c}
    batch_sem = {k: nc.alloc_semaphore(f"a{n}_{k}") for k in ("xT_in", "res_in", "y_out", "ctxK_in", "ctxV_in")}
    if n == 0:
        qf_done = sig("qf_done", W_N, 2)
        qhi = sig("qhi", W_N, 2)
        qlo = sig("qlo", W_N, 2)
        segd = sig("segd", W_N, 1)
        khi_done = sig("khi", W_N, 4)
        split_hi = nc.alloc_semaphore("a0_split_hi")
        split_lo = nc.alloc_semaphore("a0_split_lo")
        g_out = [sig(f"g_out{g}", W_N, 1, 16) for g in range(2)]
        b_in = [sig(f"b_in{g}", W_N, 1, 16) for g in range(2)]
        b_add = [sig(f"b_add{g}", W_N, 1) for g in range(2)]
    if n in (1, 2):
        swp = {k: sig(f"{k}_swapped", W_N, 1) for k in "QK"}
        cosd = {k: sig(f"{k}_cos", W_N, 1) for k in "QK"}
        sind = {k: sig(f"{k}_sin", W_N, 1) for k in "QK"}
        roped = {k: sig(f"{k}_roped", W_N, 1) for k in "QK"}
    if n == 1:
        vx_in = [nc.alloc_semaphore(f"a1_vx{p}") for p in range(2)]
        kx_done = sig("kx_done", W_N, 1)
    if n == 2:
        m_in = [nc.alloc_semaphore(f"a2_mask{p}") for p in range(2)]
        qhi2 = sig("qhi", W_N, 1)
        khi2 = sig("khi", W_N, 1)
        qlo2 = sig("qlo", W_N, 1)
    if n == 3:
        khi3 = sig("khi", W_N, 2)
        qhi3 = sig("qhi", W_N, 1)

    flat = [(s, k) for s, ks in enumerate(L.aux) for k in ks]
    order = []
    seen = {}
    for at, (_, k) in enumerate(flat):
        order.append((k, seen.get(k, 0), at % 2))
        seen[k] = seen.get(k, 0) + 1
    slot_uses = [[m for m, (s, _) in enumerate(flat) if s == i] for i in range(UH)]

    def bank_free(pe, u, m):
        v, q = u, m
        while True:
            q -= 1
            if q < 0:
                v, q = v - 1, len(order) - 1
            if isinstance(v, int) and v < -1:
                return
            k, i, bank = order[q]
            if bank == order[m][2] and runs(AUX_WINDOW[k], v):
                pe.wait_ge(done[k].sem, done[k].at(v, i))
                return

    def batch_of(j, par, ahead):
        return j + (par + ahead) // 2

    def loop(e, step):
        step(-1, -1, 1)
        for u in range(0, A_FULL):
            step(u, u // 2, u % 2)
        with e.Fori(A_FULL // 2, UNITS // 2 - 1) as j:
            step(2 * j, j, 0)
            step(2 * j + 1, j, 1)
        for u in range(UNITS - 2, UNITS + 2):
            step(u, u // 2, u % 2)

    heads = lambda i: slice(64 * (i % 2), 64 * (i % 2) + 64)
    block = ctx.enter_context(nc.Block())

    @block.tensor
    def _(pe):
        def mm3(out, w, x, first, last):
            pe.matmul(out, w[0], x[0], start=first, stop=False)
            pe.matmul(out, w[0], x[1], start=False, stop=False)
            return pe.matmul(out, w[1], x[0], start=False, stop=last)

        def project(u, j, par, m):
            k, i, bank = order[m]
            out = aux[bank]
            npar, nbatch = 1 - par, batch_of(j, par, 1)
            bank_free(pe, u, m)
            if k == "Q":
                pe.wait_ge(batch_sem["xT_in"], 16 * nbatch + 16)
                if n == 3:
                    for t in range(2):
                        for kk in range(KT):
                            mm = pe.matmul(out[:, t * T:(t + 1) * T], W["wq"][:, kk, (2 * npar + t) * P:(2 * npar + t + 1) * P],
                                           xT[:, kk, :], start=(kk == 0), stop=(kk == KT - 1))
                else:
                    for t in range(4):
                        for kk in range(KT):
                            mm = pe.matmul(out[:, t * T:(t + 1) * T], W["wq"][:, kk, (4 * npar + t) * P:(4 * npar + t + 1) * P],
                                           xT[:, kk, :], start=(kk == 0), stop=(kk == KT - 1))
                if n == 0:
                    seg = out[0:T, 4 * T:4 * T + 2 * UH]
                    for kk in range(KT):
                        pe.matmul(seg, xT[:, kk, :], W["we"][:, kk, npar, :], start=(kk == 0), stop=False)
                    mm = pe.matmul(seg, W["ones"][0:1, 0:T], W["ce"][0:1, npar, :], start=False, stop=True)
            if k == "K":
                if n == 0:
                    if i == 0 and par == 1:
                        pe.wait_ge(split_hi, nbatch + 1)
                        pe.wait_ge(split_lo, nbatch + 1)
                    c0 = (4 * npar + i) * P
                    for kk in range(KT):
                        mm = mm3(out[:, 0:CE], [w[:, kk, c0:c0 + P] for w in W["wk"]],
                                 [chi[:, kk, 0:CE], clo[:, kk, 0:CE]], kk == 0, kk == KT - 1)
                if n == 1:
                    for t in range(4):
                        for kk in range(KT):
                            mm = pe.matmul(out[:, t * T:(t + 1) * T], W["wk"][:, kk, (4 * npar + t) * P:(4 * npar + t + 1) * P],
                                           xT[:, kk, :], start=(kk == 0), stop=(kk == KT - 1))
                if n >= 2:
                    pe.wait_ge(batch_sem["ctxK_in"], 16 * nbatch + 16)
                    c0 = (npar if n == 2 else 2 * npar + i) * P
                    for kk in range(KT):
                        mm = pe.matmul(out[:, 0:C], W["wk"][:, kk, c0:c0 + P], cK[:, kk, 0:C], start=(kk == 0), stop=(kk == KT - 1))
            if k == "G":
                if i == 0:
                    pe.wait_ge(qhi.sem, qhi.at(u, 0))
                    pe.wait_ge(qlo.sem, qlo.at(u, 0))
                h = UH * npar + i
                pe.matmul(out[0:T, 0:NR], Qp[:, i, :], W["rst"][:, h, 0:NR], start=True, stop=False)
                mm = pe.matmul(out[0:T, 0:NR], Lp[heads(i), i // 2, :], W["rst"][heads(i), h, 0:NR], start=False, stop=True)
            if k == "V":
                if n == 0:
                    c0 = 512 * par
                    for kk in range(KT):
                        mm = mm3(out[0:CT, :], [x[:, kk, CT * i:CT * i + CT] for x in (chi, clo)],
                                 [w[:, kk, c0:c0 + 512] for w in W["wv"]], kk == 0, kk == KT - 1)
                if n == 1:
                    pe.wait_ge(batch_sem["ctxV_in"], 16 * j + 16)
                    for kk in range(KT):
                        mm = pe.matmul(out[0:T, :], xTv[:, kk, :], W["wv"][:, kk, 512 * par:512 * par + 512],
                                       start=(kk == 0), stop=(kk == KT - 1))
                if n >= 2:
                    pe.wait_ge(batch_sem["ctxV_in"], 16 * j + 16)
                    for t in range(NCT):
                        for kk in range(KT):
                            mm = pe.matmul(out[0:CT, t * P:(t + 1) * P], cV[:, kk, CT * t:CT * t + CT],
                                           W["wv"][:, kk, P * par:P * par + P], start=(kk == 0), stop=(kk == KT - 1))
            if k == "OT":
                pe.wait_ge(normed.sem, normed.at(u - 1))
                for q in range(L.ot):
                    mm = pe.transpose(out[:, q * T:(q + 1) * T], On[:, q * P:(q + 1) * P], W["ident"][0:T, 0:T])
            if k == "WO":
                pe.wait_ge(done["OT"].sem, done["OT"].at(u))
                for q in range(L.ot):
                    mm = pe.matmul(out[0:T, 0:H], OTs[:, q * T:(q + 1) * T], W["wo"][:, L.ot * par + q, :],
                                   start=(q == 0), stop=(q == L.ot - 1))
            mm.then_inc(aux_mm[k].sem, 1)

        def scores(u, par, i):
            if i >= 2:
                pe.wait_ge(scored.sem, scored.at(u, i - 2))
            else:
                pe.wait_ge(scored.sem, scored.at(u - 1, UH - 2 + i))
            out = ac[i % 2][0:T, 0:L.ncols]
            if n == 0:
                if i == 0:
                    pe.wait_ge(qhi.sem, qhi.at(u - 1, 1))
                    pe.wait_ge(qlo.sem, qlo.at(u - 1, 1))
                if i % 2 == 0:
                    pe.wait_ge(done["K"].sem, done["K"].at(u - 1, i // 2))
                pe.matmul(out, Qc[par][:, i, :], Kst[par][:, i, :], start=True, stop=False)
                mm = pe.matmul(out, Lc[par][heads(i), i // 2, :], Kst[par][heads(i), i, :], start=False, stop=True)
            if n == 1:
                if i == 0:
                    pe.wait_ge(roped["Q"].sem, roped["Q"].at(u - 1))
                    pe.wait_ge(roped["K"].sem, roped["K"].at(u - 1))
                    pe.wait_ge(kx_done.sem, kx_done.at(u - 1))
                mm = pe.matmul(out, qf[par][heads(i), i // 2, :], Kn[par][heads(i), i // 2, :], start=True, stop=True)
            if n == 2:
                if i == 0:
                    pe.wait_ge(qhi2.sem, qhi2.at(u - 1))
                    pe.wait_ge(qlo2.sem, qlo2.at(u - 1))
                    pe.wait_ge(done["K"].sem, done["K"].at(u - 1))
                kv = i // 4
                pe.matmul(out, Qh[par][:, i, :], Kst[par][:, kv, :], start=True, stop=False)
                mm = pe.matmul(out, Ql[par][heads(kv), i, :], Kst[par][heads(kv), kv, :], start=False, stop=True)
            if n == 3:
                if i == 0:
                    pe.wait_ge(done["Q"].sem, done["Q"].at(u - 1))
                if i % 4 == 0:
                    pe.wait_ge(done["K"].sem, done["K"].at(u - 1, i // 4))
                r = slice(32 * (i % 4), 32 * (i % 4) + 32)
                pe.matmul(out, Qh[par][r, i // 4, :], Kst[par][r, i // 4, :], start=True, stop=False)
                mm = pe.matmul(out, Ql[par][r, i // 4, :], Kst[par][r, i // 4, :], start=False, stop=True)
            mm.then_inc(ac_mm.sem, 1)

        def moved(u, i):
            s = pt_odd if i % 2 else pt_even
            pe.wait_ge(s.sem, s.at(u, i // 2))

        def transposes(u, par, i):
            wpar = 1 - par
            pe.wait_ge(probs.sem, probs.at(u, i))
            if i >= 2:
                moved(u, i - 2)
            else:
                moved(u - 1, UH - 2 + i)
            for t, (c0, cn) in enumerate(L.key_tiles):
                mm = pe.transpose(ptb[i % 2][0:cn, t * T:(t + 1) * T], S[wpar][:, i, c0:c0 + cn], W["ident"][0:T, 0:T])
            mm.then_inc(pt_mm.sem, 1)

        def weigh(u, j, par, i):
            wpar = 1 - par
            moved(u, i)
            if i == 0:
                pe.wait_ge(done["V"].sem, done["V"].at(u - 1))
                if n == 1:
                    pe.wait_ge(vx_in[wpar], 16 * batch_of(j, par, -1) + 16)
            if i % 4 == 0:
                pe.wait_ge(normed.sem, normed.at(u - 1, i // 4))
            out = ob[i // 4][0:T, (i % 4) * L.dv:(i % 4 + 1) * L.dv]
            last = len(L.key_tiles) - 1
            for t, (c0, cn) in enumerate(L.key_tiles):
                v = Vx[wpar][:, i, :] if n == 1 and t == 1 else V[wpar][0:cn, t, i // 4 if n == 2 else i, :]
                mm = pe.matmul(out, PT[i % 2][0:cn, t * T:(t + 1) * T], v, start=(t == 0), stop=(t == last))
            mm.then_inc(pv_mm.sem, 1)

        def step(u, j, par):
            if starts(u):
                pe.wait_ge(setup, 1)
                if n == 1:
                    pe.wait_ge(extras, 32)
            for i in range(UH):
                if runs(W_A, u):
                    scores(u, par, i)
                for m in slot_uses[i]:
                    if runs(AUX_WINDOW[order[m][0]], u):
                        project(u, j, par, m)
                if runs(W_W, u):
                    transposes(u, par, i)
                    if i > 0:
                        weigh(u, j, par, i - 1)
            if runs(W_W, u):
                weigh(u, j, par, UH - 1)

        loop(pe, step)

    @block.vector
    def _(dve):
        def rope(u, par, k, m):
            _, _, bank = order[m]
            npar = 1 - par
            tile, swapped, cosb = (qf, qsw, qcos) if k == "Q" else ((Kn if n == 1 else kf), ksw, kcos)
            wide = n == 1 or k == "Q"
            src = aux[bank][:, 0:4 * T].rearrange("p (t q) -> p t q", t=4) if wide else aux[bank][:, 0:C]
            cos = W["cosq" if k == "Q" else "cosk"]
            cos = cos[:, None, 0:T].to_broadcast([P, 4, T]) if wide else cos[:, 0:C]
            cosv = cosb[:, :, :] if wide else cosb[:, :]
            dve.wait_ge(roped[k].sem, roped[k].at(u - 1))
            dve.tensor_tensor(cosv, src, cos, ALU.mult).then_inc(cosd[k].sem, 1)

        def rope_sum(u, par, k):
            npar = 1 - par
            if k == "Q":
                dst = qf[npar][:, :, :] if n == 1 else qf[:, :, :]
                a, b = qcos[:, :, :], qsw[:, :, :]
            elif n == 1:
                dst, a, b = Kn[npar][:, :, 0:T], kcos[:, :, :], ksw[:, :, :]
            else:
                dst, a, b = kf[:, 0:C], kcos[:, :], ksw[:, :]
            dve.wait_ge(cosd[k].sem, cosd[k].at(u))
            dve.wait_ge(sind[k].sem, sind[k].at(u))
            if n == 1:
                dve.wait_ge(ac_mm.sem, ac_mm.at(u - 1))
            elif k == "Q":
                dve.wait_ge(qlo2.sem, qlo2.at(u - 1))
                dve.wait_ge(qhi2.sem, qhi2.at(u - 1))
            else:
                dve.wait_ge(khi2.sem, khi2.at(u - 1))
                dve.wait_ge(done["K"].sem, done["K"].at(u - 1))
            dve.tensor_tensor(dst, a, b, ALU.add).then_inc(roped[k].sem, 1)

        def split_queries(u, par):
            npar = 1 - par
            for s, (full, hi, lo) in enumerate(((qpf, Qp, Lp), (qcf, Qc[npar], Lc[npar]))):
                dve.wait_ge(qhi.sem, qhi.at(u, s))
                if s == 0:
                    dve.wait_ge(aux_mm["G"].sem, aux_mm["G"].at(u - 1))
                else:
                    dve.wait_ge(ac_mm.sem, ac_mm.at(u - 1))
                dve.wait_ge(qf_done.sem, qf_done.at(u, s))
                for r in range(2):
                    rr = slice(64 * r, 64 * r + 64)
                    ins = dve.tensor_tensor(lo[rr, :, :], full[rr, :, :], hi[rr, r:UH:2, :].bitcast(F32), ALU.subtract)
                ins.then_inc(qlo.sem, 1)

        def evacuate(u, j, par, m):
            k, i, bank = order[m]
            src = aux[bank]
            npar = 1 - par
            if k == "Q" and n == 0:
                dve.wait_ge(aux_mm["Q"].sem, aux_mm["Q"].at(u))
                q4 = src[:, 0:4 * T].rearrange("p (t q) -> p t q", t=4)
                for s, (dst, bias) in enumerate(((qpf, W["pb"]), (qcf, W["cb"]))):
                    dve.wait_ge(qhi.sem, qhi.at(u - 1, s))
                    dve.wait_ge(qlo.sem, qlo.at(u - 1, s))
                    bb = bias[:, 4 * npar:4 * npar + 4, None].to_broadcast([P, 4, T])
                    dve.scalar_tensor_tensor(dst[:, :, :], q4, 0.125, bb, ALU.mult, ALU.add).then_inc(qf_done.sem, 1)
                dve.tensor_copy(e0[npar][:, :], src[0:T, 4 * T:4 * T + UH]).then_inc(segd.sem, 1)
                dve.wait_ge(segd.sem, segd.at(u))
                dve.tensor_tensor(de[npar][:, :], src[0:T, 4 * T + UH:4 * T + 2 * UH], e0[npar][:, :], ALU.subtract)\
                   .then_inc(done["Q"].sem, 1)
            if k == "G":
                dve.wait_ge(aux_mm["G"].sem, aux_mm["G"].at(u, i))
                if i % 4 == 0:
                    dve.wait_ge(g_out[i // 4].sem, g_out[i // 4].at(u - 1))
                if i == 0:
                    dve.wait_ge(done["Q"].sem, done["Q"].at(u))
                dve.scalar_tensor_tensor(Gs[i // 4][:, i % 4, :], W["segm"][:, :], de[npar][:, i:i + 1], src[0:T, 0:NR],
                                         ALU.mult, ALU.add).then_inc(done["G"].sem, 1)
            if k == "K" and n == 0:
                dve.wait_ge(khi_done.sem, khi_done.at(u, i))
                dve.tensor_tensor(Kst[npar][64:128, 2 * i, :], src[0:64, 0:CE], Kst[npar][0:64, 2 * i, :].bitcast(F32), ALU.subtract)
                dve.tensor_tensor(Kst[npar][0:64, 2 * i + 1, :], src[64:128, 0:CE],
                                  Kst[npar][64:128, 2 * i + 1, :].bitcast(F32), ALU.subtract).then_inc(done["K"].sem, 1)
            if k == "K" and n == 3:
                dve.wait_ge(khi3.sem, khi3.at(u, i))
                dve.scalar_tensor_tensor(Kst[npar][:, i, 0:C], khi[:, i, :].bitcast(F32), W["neg"][:, 0:1], src[:, 0:C],
                                         ALU.mult, ALU.add).then_inc(done["K"].sem, 1)
            if k == "Q" and n == 3:
                dve.wait_ge(qhi3.sem, qhi3.at(u))
                dve.scalar_tensor_tensor(Ql[npar][:, :, :], src[:, 0:2 * T].rearrange("p (t q) -> p t q", t=2), 0.25,
                                         Qh[npar][:, :, :].bitcast(F32), ALU.mult, ALU.subtract).then_inc(done["Q"].sem, 1)
            if k in "QK" and n in (1, 2):
                dve.wait_ge(aux_mm[k].sem, aux_mm[k].at(u))
                rope(u, par, k, m)
                dve.wait_ge(swp[k].sem, swp[k].at(u))
                if n == 1 and k == "K":
                    dve.wait_ge(ac_mm.sem, ac_mm.at(u - 1))
                    nbatch = batch_of(j, par, 1)
                    at = slice(nbatch, nbatch + 1) if isinstance(nbatch, int) else bass.ds(nbatch, 1)
                    mem = W["memk"][:, at, 4 * npar:4 * npar + 4].rearrange("p a t -> p t a")
                    dve.tensor_copy(Kn[npar][:, :, T:T + 16], mem.to_broadcast([P, 4, 16])).then_inc(kx_done.sem, 1)
                rope_sum(u, par, k)
                dve.wait_ge(roped[k].sem, roped[k].at(u))
                if n == 1:
                    dve.sem_inc(done[k].sem, 1)
                if n == 2 and k == "Q":
                    dve.sem_inc(done[k].sem, 1)
                    dve.wait_ge(qhi2.sem, qhi2.at(u))
                    for g in range(2):
                        for r in range(2):
                            rr, dd = slice(64 * r, 64 * r + 64), slice(64 * g, 64 * g + 64)
                            ins = dve.tensor_tensor(Ql[npar][dd, 4 * g + r:4 * g + 4:2, :], qf[rr, 2 * g:2 * g + 2, :],
                                                    Qh[npar][rr, 4 * g + r:4 * g + 4:2, :].bitcast(F32), ALU.subtract)
                    ins.then_inc(qlo2.sem, 1)
                if n == 2 and k == "K":
                    dve.wait_ge(khi2.sem, khi2.at(u))
                    dve.tensor_tensor(Kst[npar][64:128, 0, 0:C], kf[0:64, 0:C], Kst[npar][0:64, 0, 0:C].bitcast(F32), ALU.subtract)
                    dve.tensor_tensor(Kst[npar][0:64, 1, 0:C], kf[64:128, 0:C], Kst[npar][64:128, 1, 0:C].bitcast(F32),
                                      ALU.subtract).then_inc(done["K"].sem, 1)
            if k == "WO":
                dve.wait_ge(aux_mm["WO"].sem, aux_mm["WO"].at(u))
                if par == 0:
                    dve.wait_ge(batch_sem["res_in"], 16 * (j - 1) + 16)
                    dve.tensor_tensor(Yacc[:, :], src[0:T, 0:H], xres[:, :], ALU.add).then_inc(done["WO"].sem, 1)
                else:
                    dve.wait_ge(done["WO"].sem, done["WO"].at(u - 1))
                    dve.wait_ge(batch_sem["y_out"], 16 * (j - 1))
                    dve.tensor_tensor(Yout[:, :], src[0:T, 0:H], Yacc[:, :], ALU.add).then_inc(done["WO"].sem, 1)

        def score(u, j, par, i):
            dve.wait_ge(ac_mm.sem, ac_mm.at(u, i))
            if i == 0:
                dve.wait_ge(biased.sem, biased.at(u - 1))
                if n != 0:
                    dve.wait_ge(pt_mm.sem, pt_mm.at(u - 1))
                if n == 2:
                    dve.wait_ge(m_in[par], 16 * j + 16)
            if n == 0 and i % 4 == 0:
                dve.wait_ge(b_add[i // 4].sem, b_add[i // 4].at(u - 1))
            dst, m = S[par][:, i, 0:L.keys], mx[par][:, i:i + 1]
            src = ac[i % 2][0:T, 0:L.keys]
            if n == 3:
                dve.tensor_scalar(dst, src, 1.0, None, ALU.mult, ALU.max, accum_out=m).then_inc(scored.sem, 1)
                return
            add = {0: dst, 1: W["mask"][:, :] if n == 1 else None, 2: mask[par][:, :] if n == 2 else None}[n]
            dve.sem_inc(gate, 1)
            dve.tensor_tensor_reduce(out=dst, in0=src, in1=add, scale=1.0, scalar=-3.0e38, op0=ALU.add, op1=ALU.max,
                                     accum_out=m).then_inc(scored.sem, 1)

        def exp_bias(u, par):
            dve.wait_ge(scored.sem, scored.at(u))
            dve.wait_ge(probs.sem, probs.at(u - 1))
            if n == 0:
                dve.tensor_tensor(mtot[:, :], mx[par][:, :], e0[par][:, :], ALU.add).then_inc(maxed.sem, 1)
                dve.wait_ge(maxed.sem, maxed.at(u))
                dve.tensor_tensor(nb[par][:, :], e0[par][:, :], mtot[:, :], ALU.subtract).then_inc(biased.sem, 1)
            else:
                dve.tensor_scalar(nb[par][:, :], mx[par][:, :], -1.0, None, ALU.mult).then_inc(biased.sem, 1)

        def move_even(u, i):
            dve.wait_ge(pt_mm.sem, pt_mm.at(u, i))
            dve.wait_ge(pv_mm.sem, pv_mm.at(u, i - 2) if i >= 2 else pv_mm.at(u - 1, UH - 2 + i))
            for a, b, c in pieces:
                ins = dve.tensor_copy(PT[i % 2][0:a, b:c], ptb[i % 2][0:a, b:c])
            ins.then_inc(pt_even.sem, 1)

        def normalise(u, g):
            dve.wait_ge(pv_mm.sem, pv_mm.at(u, 4 * g + 3))
            o = ob[g][0:T, 0:4 * L.dv].rearrange("p (h d) -> p h d", h=4)
            dve.wait_ge(normed.sem, normed.at(u - 1, g))
            dve.reciprocal(rec[:, g, :], o[:, :, L.d]).then_inc(recd.sem, 1)
            dve.wait_ge(recd.sem, recd.at(u, g))
            if runs(W_O, u):
                dve.wait_ge(aux_mm["OT"].sem, aux_mm["OT"].at(u))
            dst = On[:, 4 * g * L.d:4 * (g + 1) * L.d].rearrange("p (h d) -> p h d", h=4)
            dve.tensor_tensor(dst, o[:, :, 0:L.d], rec[:, g, :, None].to_broadcast([T, 4, L.d]), ALU.mult)\
               .then_inc(normed.sem, 1)

        pieces = [(CT, 0, NCT * T)] if n != 1 else [(T, 0, T), (32, T, 2 * T)]
        dve.memset(PT[0][:, :], 0.0)
        for p in range(2):
            dve.memset(S[p][:, :, :], 0.0)
            dve.memset(V[p][:, :, :, :], 0.0)
        if n == 0:
            dve.memset(clo[:, :, :].bitcast(F32), 0.0)
            dve.memset(chi[:, :, :].bitcast(F32), 0.0)
            dve.memset(craw[:, :, :], 0.0)
        if n >= 2:
            dve.memset(cK[:, :, :], 0.0)
            dve.memset(cV[:, :, :], 0.0)
            for p in range(2):
                dve.memset(Kst[p][:, :, :].bitcast(F32), 0.0)
        dve.drain()
        for p in range(2):
            dve.memset(V[p][:, :, :, L.d:L.d + 1], 1.0)
        if n == 1:
            for p in range(2):
                dve.memset(Vx[p][:, :, :], 0.0)
            dve.drain()
            for p in range(2):
                dve.memset(Vx[p][:, :, L.d:L.d + 1], 1.0)
                dve.tensor_copy(Kn[p][:, :, T + 16:T + 32], W["perk"][:, 4 * p:4 * p + 4, :])
        dve.drain().then_inc(setup, 1)

        def step(u, j, par):
            for i in range(UH):
                if runs(W_A, u):
                    score(u, j, par, i)
                if n == 0 and i == 1 and runs(W_N, u):
                    split_queries(u, par)
                for m in slot_uses[i]:
                    if runs(AUX_WINDOW[order[m][0]], u):
                        evacuate(u, j, par, m)
                if runs(W_W, u):
                    if i % 2 == 0:
                        move_even(u, i)
                    if i == 5:
                        normalise(u, 0)
            if runs(W_A, u):
                exp_bias(u, par)
            if runs(W_W, u):
                normalise(u, 1)

        loop(dve, step)

    @block.scalar
    def _(act):
        def softmax(u, par, i):
            wpar = 1 - par
            if i == 0:
                act.wait_ge(biased.sem, biased.at(u - 1))
            s = S[wpar][:, i, 0:L.keys]
            act.activation(s, s, ACT.Exp, bias=nb[wpar][:, i:i + 1], scale=1.0).then_inc(probs.sem, 1)

        def evacuate(u, j, par, m):
            k, i, bank = order[m]
            src = aux[bank]
            npar = 1 - par
            if k == "Q" and n == 0:
                for s, (full, hi) in enumerate(((qpf, Qp), (qcf, Qc[npar]))):
                    act.wait_ge(qf_done.sem, qf_done.at(u, s))
                    if s == 0:
                        act.wait_ge(aux_mm["G"].sem, aux_mm["G"].at(u - 1))
                    else:
                        act.wait_ge(ac_mm.sem, ac_mm.at(u - 1))
                    for r in range(2):
                        for d in range(2):
                            ins = act.copy(hi[64 * d:64 * d + 64, r:UH:2, :], full[64 * r:64 * r + 64, :, :])
                    ins.then_inc(qhi.sem, 1)
            if k == "K" and n == 0:
                act.wait_ge(aux_mm["K"].sem, aux_mm["K"].at(u, i))
                if i == 0:
                    act.wait_ge(ac_mm.sem, ac_mm.at(u - 1))
                act.copy(Kst[npar][0:64, 2 * i, :], src[0:64, 0:CE])
                act.copy(Kst[npar][64:128, 2 * i + 1, :], src[64:128, 0:CE]).then_inc(khi_done.sem, 1)
            if k == "K" and n == 3:
                act.wait_ge(aux_mm["K"].sem, aux_mm["K"].at(u, i))
                act.wait_ge(done["K"].sem, done["K"].at(u - 1, i))
                if i == 0:
                    act.wait_ge(ac_mm.sem, ac_mm.at(u - 1))
                act.copy(khi[:, i, :], src[:, 0:C]).then_inc(khi3.sem, 1)
            if k == "Q" and n == 3:
                act.wait_ge(aux_mm["Q"].sem, aux_mm["Q"].at(u))
                act.wait_ge(ac_mm.sem, ac_mm.at(u - 1))
                act.activation(Qh[npar][:, :, :], src[:, 0:2 * T].rearrange("p (t q) -> p t q", t=2), ACT.Copy, scale=0.25)\
                   .then_inc(qhi3.sem, 1)
            if k in "QK" and n in (1, 2):
                act.wait_ge(cosd[k].sem, cosd[k].at(u))
                act.wait_ge(roped[k].sem, roped[k].at(u - 1))
                for r in range(4):
                    o = 32 * (r ^ 1)
                    if n == 1 or k == "Q":
                        dst = (qsw if k == "Q" else ksw)[32 * r:32 * r + 32, :, :]
                        sv = src[o:o + 32, 0:4 * T].rearrange("p (t q) -> p t q", t=4)
                    else:
                        dst, sv = ksw[32 * r:32 * r + 32, :], src[o:o + 32, 0:C]
                    ins = act.copy(dst, sv)
                ins.then_inc(swp[k].sem, 1)
                if n == 2 and k == "Q":
                    act.wait_ge(roped["Q"].sem, roped["Q"].at(u))
                    act.wait_ge(ac_mm.sem, ac_mm.at(u - 1))
                    for r in range(2):
                        for d in range(2):
                            ins = act.copy(Qh[npar][64 * d:64 * d + 64, r:UH:2, :], qf[64 * r:64 * r + 64, :, :])
                    ins.then_inc(qhi2.sem, 1)
                if n == 2 and k == "K":
                    act.wait_ge(roped["K"].sem, roped["K"].at(u))
                    act.copy(Kst[npar][0:64, 0, 0:C], kf[0:64, 0:C])
                    act.copy(Kst[npar][64:128, 1, 0:C], kf[64:128, 0:C]).then_inc(khi2.sem, 1)
            if k == "V":
                act.wait_ge(aux_mm["V"].sem, aux_mm["V"].at(u, i))
                if i == 0:
                    act.wait_ge(pv_mm.sem, pv_mm.at(u - 1))
                if n == 0:
                    dst = V[par][:, i, :, 0:L.d]
                    sv = src[0:CT, :].rearrange("p (h d) -> p h d", h=UH)
                elif n == 1:
                    dst = V[par][0:T, 0, :, 0:L.d]
                    sv = src[0:T, :].rearrange("p (h d) -> p h d", h=UH)
                if n < 2:
                    act.copy(dst, sv).then_inc(done["V"].sem, 1)
                elif n == 2:
                    for kv in range(2):
                        sv = src[0:CT, 0:NCT * P].rearrange("p (t h d) -> p t h d", t=NCT, h=2)[:, :, kv, :]
                        ins = act.copy(V[par][:, :, kv, 0:L.d], sv)
                    ins.then_inc(done["V"].sem, 1)
                else:
                    for t in range(NCT):
                        sv = src[0:CT, t * P:(t + 1) * P].rearrange("p (h d) -> p h d", h=UH)
                        ins = act.copy(V[par][:, t, :, 0:L.d], sv)
                    ins.then_inc(done["V"].sem, 1)
            if k == "OT":
                act.wait_ge(aux_mm["OT"].sem, aux_mm["OT"].at(u))
                act.wait_ge(aux_mm["WO"].sem, aux_mm["WO"].at(u - 1))
                act.copy(OTs[:, :], src[:, 0:L.ot * T]).then_inc(done["OT"].sem, 1)

        def split(j):
            act.wait_ge(batch_sem["ctxK_in"], 16 * (j + 1) + 16)
            act.copy(chi[:, :, 0:CE], craw[:, :, 0:CE]).then_inc(split_hi, 1)

        def move_odd(u, i):
            act.wait_ge(pt_mm.sem, pt_mm.at(u, i))
            act.wait_ge(pv_mm.sem, pv_mm.at(u, i - 2) if i >= 2 else pv_mm.at(u - 1, UH - 2 + i))
            for a, b, c in ([(CT, 0, NCT * T)] if n != 1 else [(T, 0, T), (32, T, 2 * T)]):
                ins = act.copy(PT[i % 2][0:a, b:c], ptb[i % 2][0:a, b:c])
            ins.then_inc(pt_odd.sem, 1)

        def step(u, j, par):
            if starts(u):
                act.wait_ge(setup, 1)
                if n == 0:
                    split(-1)
            if runs(W_W, u):
                softmax(u, par, 0)
            for i in range(UH):
                if runs(W_W, u) and i + 1 < UH:
                    softmax(u, par, i + 1)
                if n == 0 and i == 3 and par == 1 and runs((0, UNITS - 3), u):
                    act.wait_ge(aux_mm["V"].sem, aux_mm["V"].at(u))
                    split(j)
                for m in slot_uses[i]:
                    if runs(AUX_WINDOW[order[m][0]], u):
                        evacuate(u, j, par, m)
                if runs(W_W, u) and i % 2 == 1:
                    move_odd(u, i)

        loop(act, step)

    @block.gpsimd
    def _(pool):
        def step(u, j, par):
            if n == 0:
                if starts(u):
                    pool.wait_ge(setup, 1)
                if starts(u) or (par == 1 and runs((0, UNITS - 3), u)):
                    pool.wait_ge(split_hi, j + 2)
                    pool.tensor_tensor(clo[:, :, 0:CE], craw[:, :, 0:CE], chi[:, :, 0:CE].bitcast(F32), ALU.subtract)\
                        .then_inc(split_lo, 1)
                if runs(W_N, u):
                    npar = 1 - par
                    for g in range(2):
                        pool.wait_ge(b_in[g].sem, b_in[g].at(u))
                        s = S[npar][:, 4 * g:4 * g + 4, 0:C]
                        pool.tensor_tensor(s, s, W["cmask"][:, None, :].to_broadcast([T, 4, C]), ALU.add).then_inc(b_add[g].sem, 1)
            if n in (1, 2) and runs(W_N, u):
                if starts(u):
                    pool.wait_ge(setup, 1)
                for k in "QK":
                    pool.wait_ge(swp[k].sem, swp[k].at(u))
                    sin = W["sinq" if k == "Q" else "sink"]
                    if n == 1 or k == "Q":
                        t = (qsw if k == "Q" else ksw)[:, :, :]
                        sv = sin[:, None, 0:T].to_broadcast([P, 4, T])
                    else:
                        t, sv = ksw[:, :], sin[:, 0:C]
                    pool.tensor_tensor(t, t, sv, ALU.mult).then_inc(sind[k].sem, 1)

        if n != 3:
            loop(pool, step)

    @block.sync
    def _(sp):
        def load_ctx(dst, src, s):
            sp.dma_start(dst[:, :, 0:io["ctx_cols"]], src).then_inc(s, 16)

        ctx_src = lambda b: row(io["ctxT"], b).rearrange("(k p) c -> p k c", k=KT)
        xT_src = lambda b: row(io["xT"], b).rearrange("(k p) q -> p k q", k=KT)

        def step(u, j, par):
            npar = 1 - par
            if starts(u):
                sp.dma_start(xT[:, :, :], xT_src(0)).then_inc(batch_sem["xT_in"], 16)
                sp.wait_ge(setup, 1)
                if n == 1:
                    for p in range(2):
                        sp.dma_start(Vx[p][16:32, :, 0:L.d], io["perv"][:, UH * p:UH * p + UH, :]).then_inc(extras, 16)
                    sp.dma_start(xTv[:, :, :], xT_src(0)).then_inc(batch_sem["ctxV_in"], 16)
                if n == 0:
                    load_ctx(craw, ctx_src(0), batch_sem["ctxK_in"])
                if n >= 2:
                    load_ctx(cK, ctx_src(0), batch_sem["ctxK_in"])
                    load_ctx(cV, ctx_src(0), batch_sem["ctxV_in"])
            nextb = (0, UNITS - 4)
            if par == 0 and runs(nextb, u):
                ctx_next, xT_next = ctx_src(j + 1) if n != 1 else None, xT_src(j + 1)
                last = aux_mm["K"] if n == 1 else aux_mm["Q"]
                sp.wait_ge(last.sem, last.at(u))
                sp.dma_start(xT[:, :, :], xT_next).then_inc(batch_sem["xT_in"], 16)
                if n == 0:
                    sp.wait_ge(split_lo, j + 1)
                    load_ctx(craw, ctx_next, batch_sem["ctxK_in"])
                if n >= 2:
                    sp.wait_ge(aux_mm["K"].sem, aux_mm["K"].at(u))
                    load_ctx(cK, ctx_next, batch_sem["ctxK_in"])
            if n == 2 and runs(W_A, u):
                src = row(io["mask"], j)
                sp.wait_ge(scored.sem, scored.at(u - 2))
                sp.dma_start(mask[par][:, :], src).then_inc(m_in[par], 16)
            if n == 1 and runs(W_A, u):
                src = row(io["memv"], j)[par * 512:par * 512 + 512].rearrange("(o h d) -> o h d", o=1, h=UH).to_broadcast([16, UH, L.d])
                sp.wait_ge(pv_mm.sem, pv_mm.at(u - 1))
                sp.dma_start(Vx[par][0:16, :, 0:L.d], src).then_inc(vx_in[par], 16)
            if par == 1 and n >= 1 and runs((0, UNITS - 3), u):
                src = xT_src(j + 1) if n == 1 else ctx_src(j + 1)
                sp.wait_ge(aux_mm["V"].sem, aux_mm["V"].at(u))
                if n == 1:
                    sp.dma_start(xTv[:, :, :], src).then_inc(batch_sem["ctxV_in"], 16)
                else:
                    load_ctx(cV, src, batch_sem["ctxV_in"])
            if par == 1 and runs((0, UNITS - 1), u):
                src = row(io["res"], j)
                sp.wait_ge(done["WO"].sem, done["WO"].at(u - 1))
                sp.dma_start(xres[:, :], src).then_inc(batch_sem["res_in"], 16)
            if par == 1 and runs(W_O, u):
                dst = row(io["y"], j - 1)
                sp.wait_ge(done["WO"].sem, done["WO"].at(u))
                sp.dma_start(dst, Yout[:, :]).then_inc(batch_sem["y_out"], 16)
            if n == 0 and runs(W_N, u):
                for g in range(2):
                    sp.wait_ge(b_in[g].sem, b_in[g].at(u - 1))
                    sp.sem_inc(sp_gate, 1)
                    sp.wait_ge(done["G"].sem, done["G"].at(u, 4 * g + 3))
                    sp.dma_start(io["gscr"][g], Gs[g][:, :, :]).then_inc(g_out[g].sem, 16)
                    sp.wait_ge(g_out[g].sem, g_out[g].at(u))
                    if runs(W_W, u):
                        sp.sem_inc(sp_gate, 1)
                        sp.wait_ge(pt_mm.sem, pt_mm.at(u, 4 * g + 3))
                    skew = bass.AP(tensor=io["gscr"][g].tensor, offset=io["gscr"][g].offset + T - 1,
                                   ap=[[4 * NR - 1, T], [NR, 4], [1, C]])
                    sp.dma_start(S[npar][:, 4 * g:4 * g + 4, 0:C], skew).then_inc(b_in[g].sem, 16)

        loop(sp, step)
        sp.wait_ge(batch_sem["y_out"], 16 * B)



def context_pass(nc, ctx, ident, io):
    def sb(name, shape, dt=F32):
        return ctx.enter_context(nc.sbuf_tensor(f"c_{name}", shape, dt))

    EVERY = (0, B - 1)
    FULL = 2

    def sig(name, per, by=1):
        return Signal(nc, f"c_{name}", EVERY, per, FULL, by)

    X = [sb(f"ctx{p}", [CT, NCT, H]) for p in range(2)]
    bn = sb("bn", [CT, NCT, 6])
    mv = sb("mv", [CT, NCT, 2])
    ms, ms2, sd, rs = (sb(k, [CT, NCT]) for k in ("ms", "ms2", "sd", "rs"))
    XT = [sb(f"ctxT{p}", [P, KT, CP]) for p in range(2)]
    means = sb("means", [P, KT, B])
    eps, ones = sb("eps", [P, 1]), sb("ones", [CT, 2])
    ps = [ctx.enter_context(nc.psum_tensor(f"c_ps{k}", [P, 512], F32)) for k in range(6)]
    setup = nc.alloc_semaphore("c_setup")
    loaded = [nc.alloc_semaphore(f"c_in{p}") for p in range(2)]
    stored = [nc.alloc_semaphore(f"c_out{p}") for p in range(2)]
    gate = nc.alloc_semaphore("c_gate")
    m_out = nc.alloc_semaphore("c_means_out")
    summed, stats, mean2, meansq = sig("summed", 1), sig("stats", 1), sig("mean2", 1), sig("meansq", 1)
    aggr, rooted, inv = sig("aggr", 1), sig("rooted", 1), sig("inv", 1)
    scaled, turned, moved, mcopied = sig("scaled", 1), sig("turned", KT), sig("moved", KT), sig("mcopied", 1)
    block = ctx.enter_context(nc.Block())

    def loop(e, step):
        for b in range(FULL):
            step(b, b // 2, b % 2)
        with e.Fori(FULL // 2, B // 2) as j:
            step(2 * j, j, 0)
            step(2 * j + 1, j, 1)

    @block.sync
    def _(sp):
        sp.wait_ge(setup, 1)

        def load(b, j, p):
            src = row(io["ctx"], b)
            sp.wait_ge(turned.sem, turned.at(b - 2))
            sp.dma_start(X[p][:, 0:2, :], src[0:2 * CT, :].rearrange("(t p) h -> p t h", t=2)).then_inc(loaded[p], 16)
            sp.dma_start(X[p][0:C - 2 * CT, 2, :], src[2 * CT:C, :]).then_inc(loaded[p], 16)

        for b in range(FULL):
            load(b, b // 2, b % 2)
        with sp.Fori(FULL // 2, B // 2) as j:
            load(2 * j, j, 0)
            load(2 * j + 1, j, 1)
        sp.wait_ge(mcopied.sem, B)
        sp.dma_start(io["means"].rearrange("k p b -> p k b"), means[:, :, :]).then_inc(m_out, 16)
        for s in stored:
            sp.wait_ge(s, 16 * (B // 2))
        sp.wait_ge(m_out, 16)

    @block.vector
    def _(dve):
        for p in range(2):
            dve.memset(X[p][:, :, :], 0.0)
        dve.memset(eps[:, :], 1e-6)
        dve.memset(ones[:, :], 1.0 / C)
        dve.drain().then_inc(setup, 1)

        def step(b, j, p):
            dve.wait_ge(loaded[p], 32 * j + 32)
            for t in range(NCT):
                ins = dve.bn_stats(bn[:, t, :], X[p][:, t, :])
            ins.then_inc(stats.sem, 1)
            dve.wait_ge(stats.sem, stats.at(b))
            dve.sem_inc(gate, 1)
            for t in range(NCT):
                ins = dve.bn_aggr(mv[:, t, :], bn[:, t, :])
            ins.then_inc(aggr.sem, 1)
            dve.wait_ge(aggr.sem, aggr.at(b))
            dve.tensor_tensor(ms2[:, :], mv[:, :, 0], mv[:, :, 0], ALU.mult).then_inc(mean2.sem, 1)
            dve.wait_ge(mean2.sem, mean2.at(b))
            dve.wait_ge(rooted.sem, rooted.at(b - 1))
            dve.tensor_tensor(ms[:, :], ms2[:, :], mv[:, :, 1], ALU.add).then_inc(meansq.sem, 1)
            dve.wait_ge(rooted.sem, rooted.at(b))
            dve.reciprocal(rs[:, :], sd[:, :]).then_inc(inv.sem, 1)
            dve.wait_ge(inv.sem, inv.at(b))
            dve.wait_ge(summed.sem, summed.at(b))
            for t in range(NCT):
                ins = dve.tensor_scalar(X[p][:, t, :], X[p][:, t, :], rs[:, t:t + 1], None, ALU.mult)
            ins.then_inc(scaled.sem, 1)
            dve.wait_ge(turned.sem, turned.at(b, 0))
            if not isinstance(b, int) or b >= 2:
                dve.wait_ge(stored[p], 16 * j)
            dve.tensor_copy(XT[p][:, 0, :], ps[2 * p][:, 0:CP]).then_inc(moved.sem, 1)
            at = slice(b, b + 1) if isinstance(b, int) else bass.ds(b, 1)
            dve.tensor_copy(means[:, :, at].rearrange("p k a -> p (k a)"), ps[4][:, 0:2 * KT:2]).then_inc(mcopied.sem, 1)

        loop(dve, step)

    @block.scalar
    def _(act):
        act.wait_ge(setup, 1)

        def step(b, j, p):
            dst = row(io["ctxnT"], b).rearrange("(k p) c -> p k c", k=KT)
            act.wait_ge(meansq.sem, meansq.at(b))
            act.wait_ge(inv.sem, inv.at(b - 1))
            act.activation(sd[:, :], ms[:, :], ACT.Sqrt, bias=eps[0:CT, 0:1]).then_inc(rooted.sem, 1)
            act.wait_ge(moved.sem, moved.at(b, 0))
            act.wait_ge(turned.sem, turned.at(b, 1))
            if not isinstance(b, int) or b >= 2:
                act.wait_ge(stored[p], 16 * j)
            act.copy(XT[p][:, 1, :], ps[2 * p + 1][:, 0:CP]).then_inc(moved.sem, 1)
            act.wait_ge(moved.sem, moved.at(b))
            act.dma_start(dst, XT[p][:, :, :]).then_inc(stored[p], 16)

        loop(act, step)

    @block.tensor
    def _(pe):
        pe.wait_ge(setup, 1)

        def step(b, j, p):
            pe.wait_ge(loaded[p], 32 * j + 32)
            pe.wait_ge(mcopied.sem, mcopied.at(b - 1))
            for k in range(KT):
                for t in range(NCT):
                    mm = pe.matmul(ps[4][:, 2 * k:2 * k + 2], X[p][:, t, k * P:(k + 1) * P], ones[:, :], start=(t == 0), stop=(t == NCT - 1))
            mm.then_inc(summed.sem, 1)
            pe.wait_ge(scaled.sem, scaled.at(b))
            pe.wait_ge(moved.sem, moved.at(b - 2))
            for k in range(KT):
                for t in range(NCT):
                    mm = pe.transpose(ps[2 * p + k][:, t * CT:(t + 1) * CT], X[p][:, t, k * P:(k + 1) * P], ident[0:CT, 0:CT])
                mm.then_inc(turned.sem, 1)

        loop(pe, step)


GB = 4
NG = B // GB
GT = GB * T
F_PRE, F_MID, F_POST = (-1, NG - 2), (0, NG - 1), (1, NG)
F_FULL = 2


def feed_forward(nc, ctx, n, ident, W, io, eps_pre, eps_post, eps_next, ftiles):
    gated = n != 0
    NF = len(ftiles)

    def sb(name, shape, dt=F32):
        return ctx.enter_context(nc.sbuf_tensor(f"f{n}_{name}", shape, dt))

    def sig(name, window, per, by=1):
        return Signal(nc, f"f{n}_{name}", window, per, F_FULL, by)

    Yin = sb("y", [T, GB, H])
    Xn = sb("norm", [T, GB, H])
    Xs = sb("affine", [T, GB, H])
    XT = [sb(f"xT_{k}", [P, KT, GT], F32R) for k in ("hi", "lo")]
    R = sb("resid", [T, GB, H])
    Z = sb("z", [T, GB, H])
    Zn, Zs = sb("znorm", [T, GB, H]), sb("zaffine", [T, GB, H])
    Zx = sb("znext", [T, GB, H])
    Zg = sb("zgain", [T, GB, H])
    ZT = sb("zT", [P, KT, GT])
    hf = [sb(f"hidden{p}", [P, GT]) for p in range(2)]
    sg = [sb(f"silu{p}", [P, GT]) for p in range(2)]
    Hh, Hl = sb("h_hi", [P, NF, GT], F32R), sb("h_lo", [P, NF, GT], F32R)
    st = {k: {"bn": sb(f"{k}_bn", [T, GB, 6]), "mv": sb(f"{k}_mv", [T, GB, 2]), "m2": sb(f"{k}_m2", [T, GB]),
              "v": sb(f"{k}_v", [T, GB]), "sd": sb(f"{k}_sd", [T, GB]), "rs": sb(f"{k}_rs", [T, GB])} for k in ("pre", "post", "next")}
    epst = sb("eps", [P, 3])
    ps = [ctx.enter_context(nc.psum_tensor(f"f{n}_ps{k}", [P, 512], F32)) for k in range(8)]
    hb, fb, tb = ps[0:4], ps[4:6], ps[6:8]

    setup = nc.alloc_semaphore(f"f{n}_setup")
    gate, pool_gate = (nc.alloc_semaphore(f"f{n}_{k}") for k in ("gate", "pool_gate"))
    y_in = sig("y_in", F_PRE, 1, 16)
    z_out = sig("z_out", F_POST, 1, 16)
    zt_out = [sig(f"zt_out{k}", F_POST, 1, 16) for k in range(KT)]
    norms = {"pre": F_PRE, "next": F_POST}
    if n == 0:
        norms["post"] = F_POST
    N = {k: {s: sig(f"{k}_{s}", w, 1) for s in ("bn", "mv", "m2", "v", "sd", "rs", "out", "g", "b")} for k, w in norms.items()}
    p_mm, p_hi, p_lo = sig("p_mm", F_PRE, KT), sig("p_hi", F_PRE, KT), sig("p_lo", F_PRE, KT)
    q_mm, q_done = sig("q_mm", F_POST, KT), sig("q_done", F_POST, KT)
    h_mm, h_act, h_val = sig("h_mm", F_MID, NF), sig("h_act", F_MID, NF), sig("h_val", F_MID, NF)
    h_hi, h_lo = sig("h_hi", F_MID, NF), sig("h_lo", F_MID, NF)
    o_mm, o_done = sig("o_mm", F_MID, GB), sig("o_done", F_MID, GB)
    resid, base, gbase = sig("resid", F_PRE, 1), sig("base", F_PRE, 1), sig("zg", F_POST, 1)
    zg2 = sig("zg2", F_POST, 1)
    block = ctx.enter_context(nc.Block())

    def loop(e, step):
        for s in range(-1, F_FULL):
            step(s)
        with e.Fori(F_FULL, NG - 1) as s:
            step(s)
        for s in range(NG - 1, NG + 1):
            step(s)

    wide = lambda ap: ap[:, None, :].to_broadcast([T, GB, H])
    pre_in = Xs if n == 0 else Xn

    @block.tensor
    def _(pe):
        def step(s):
            if isinstance(s, int) and s == -1:
                pe.wait_ge(setup, 1)
            if runs(F_MID, s):
                for f, (f0, fn) in enumerate(ftiles):
                    if f == 0:
                        pe.wait_ge(p_lo.sem, p_lo.at(s - 1))
                    banks = [hb[(2 * f) % 4], hb[(2 * f + 1) % 4]] if gated else [hb[f % 4]]
                    back = 2 if gated else 4
                    pe.wait_ge(h_val.sem, h_val.at(s, f - back) if f >= back else h_val.at(s - 1, NF - back + f))
                    for g, bank in enumerate(banks):
                        c0 = g * W["f"] + f0
                        for k in range(KT):
                            for a, (wi, xi) in enumerate(((0, 0), (0, 1), (1, 0))):
                                mm = pe.matmul(bank[0:fn, 0:GT], W["w1"][wi][:, k, c0:c0 + fn], XT[xi][:, k, :],
                                               start=(k == 0 and a == 0), stop=(k == KT - 1 and a == 2))
                    mm.then_inc(h_mm.sem, 1)
            if runs(F_PRE, s):
                last = N["pre"]["b"] if n == 0 else N["pre"]["out"]
                pe.wait_ge(last.sem, last.at(s))
                pe.wait_ge(q_done.sem, q_done.at(s - 1))
                for k in range(KT):
                    for t in range(GB):
                        mm = pe.transpose(tb[k][:, t * T:(t + 1) * T], pre_in[:, t, k * P:(k + 1) * P], ident[0:T, 0:T])
                    mm.then_inc(p_mm.sem, 1)
            if runs(F_MID, s):
                for t in range(GB):
                    pe.wait_ge(o_done.sem, o_done.at(s, t - 2) if t >= 2 else o_done.at(s - 1, GB - 2 + t))
                    for f, (f0, fn) in enumerate(ftiles):
                        if t == 0:
                            pe.wait_ge(h_lo.sem, h_lo.at(s, f))
                        for a, (hh, wi) in enumerate(((Hh, 0), (Hh, 1), (Hl, 0))):
                            mm = pe.matmul(fb[t % 2][0:T, 0:H], hh[0:fn, f, t * T:(t + 1) * T], W["w2"][wi][0:fn, f, :],
                                           start=(f == 0 and a == 0), stop=(f == NF - 1 and a == 2))
                    mm.then_inc(o_mm.sem, 1)
            if runs(F_POST, s):
                pe.wait_ge(N["next"]["out"].sem, N["next"]["out"].at(s))
                pe.wait_ge(p_lo.sem, p_lo.at(s))
                for k in range(KT):
                    for t in range(GB):
                        mm = pe.transpose(tb[k][:, t * T:(t + 1) * T], Zx[:, t, k * P:(k + 1) * P], ident[0:T, 0:T])
                    mm.then_inc(q_mm.sem, 1)

        loop(pe, step)

    @block.vector
    def _(dve):
        for c, e in enumerate((eps_pre, eps_post, eps_next)):
            dve.memset(epst[:, c:c + 1], e)
        dve.drain().then_inc(setup, 1)

        def norm(s, k, src, dst, centred):
            a, g = st[k], N[k]
            for t in range(GB):
                ins = dve.bn_stats(a["bn"][:, t, :], src[:, t, :])
            ins.then_inc(g["bn"].sem, 1)
            dve.wait_ge(g["bn"].sem, g["bn"].at(s))
            dve.sem_inc(gate, 1)
            for t in range(GB):
                ins = dve.bn_aggr(a["mv"][:, t, :], a["bn"][:, t, :])
            ins.then_inc(g["mv"].sem, 1)
            dve.wait_ge(g["mv"].sem, g["mv"].at(s))
            dve.tensor_tensor(a["m2"][:, :], a["mv"][:, :, 0], a["mv"][:, :, 0], ALU.mult).then_inc(g["m2"].sem, 1)
            dve.wait_ge(g["m2"].sem, g["m2"].at(s))
            if centred:
                dve.tensor_copy(a["v"][:, :], a["mv"][:, :, 1]).then_inc(g["v"].sem, 1)
            else:
                dve.tensor_tensor(a["v"][:, :], a["m2"][:, :], a["mv"][:, :, 1], ALU.add).then_inc(g["v"].sem, 1)
            dve.wait_ge(g["sd"].sem, g["sd"].at(s))
            dve.reciprocal(a["rs"][:, :], a["sd"][:, :]).then_inc(g["rs"].sem, 1)
            dve.wait_ge(g["rs"].sem, g["rs"].at(s))
            for t in range(GB):
                if centred:
                    ins = dve.tensor_scalar(dst[:, t, :], src[:, t, :], a["mv"][:, t, 0:1], a["rs"][:, t:t + 1], ALU.subtract, ALU.mult)
                else:
                    ins = dve.tensor_scalar(dst[:, t, :], src[:, t, :], a["rs"][:, t:t + 1], None, ALU.mult)
            ins.then_inc(g["out"].sem, 1)

        def step(s):
            if runs(F_PRE, s):
                dve.wait_ge(y_in.sem, y_in.at(s))
                if n == 0:
                    dve.wait_ge(N["pre"]["g"].sem, N["pre"]["g"].at(s - 1))
                else:
                    dve.wait_ge(p_mm.sem, p_mm.at(s - 1))
                norm(s, "pre", Yin, Xn, n == 0)
            if runs(F_MID, s):
                for f, (f0, fn) in enumerate(ftiles):
                    dve.wait_ge(h_act.sem, h_act.at(s, f))
                    if gated:
                        dve.wait_ge(h_mm.sem, h_mm.at(s, f))
                        dve.wait_ge(h_hi.sem, h_hi.at(s, f - 2) if f >= 2 else h_hi.at(s - 1, NF - 2 + f))
                        dve.wait_ge(h_lo.sem, h_lo.at(s, f - 2) if f >= 2 else h_lo.at(s - 1, NF - 2 + f))
                        dve.scalar_tensor_tensor(hf[f % 2][0:fn, :], hb[(2 * f) % 4][0:fn, 0:GT], W["b1"][0:fn, f:f + 1],
                                                 sg[f % 2][0:fn, :], ALU.add, ALU.mult).then_inc(h_val.sem, 1)
                        dve.wait_ge(h_val.sem, h_val.at(s, f))
                    if f == 0:
                        dve.wait_ge(o_mm.sem, o_mm.at(s - 1))
                    dve.tensor_copy(Hh[0:fn, f, :], hf[f % 2][0:fn, :]).then_inc(h_hi.sem, 1)
                    dve.wait_ge(h_hi.sem, h_hi.at(s, f))
                    dve.tensor_tensor(Hl[0:fn, f, :], hf[f % 2][0:fn, :], Hh[0:fn, f, :].bitcast(F32), ALU.subtract).then_inc(h_lo.sem, 1)
            if runs(F_PRE, s):
                for k in range(KT):
                    dve.wait_ge(p_hi.sem, p_hi.at(s, k))
                    dve.tensor_tensor(XT[1][:, k, :], tb[k][:, 0:GT], XT[0][:, k, :].bitcast(F32), ALU.subtract).then_inc(p_lo.sem, 1)
            if runs(F_POST, s):
                dve.wait_ge(o_done.sem, o_done.at(s - 1))
                if n == 0:
                    dve.wait_ge(N["post"]["g"].sem, N["post"]["g"].at(s - 1))
                    norm(s, "post", Z, Zn, True)
                    dve.wait_ge(N["post"]["b"].sem, N["post"]["b"].at(s))
                dve.wait_ge(q_mm.sem, q_mm.at(s - 1))
                if n == 2:
                    dve.wait_ge(gbase.sem, gbase.at(s - 1))
                norm(s, "next", Zs if n == 0 else Z, Zx, False)
            if runs(F_MID, s):
                for t in range(GB):
                    dve.wait_ge(o_mm.sem, o_mm.at(s, t))
                    if t == 0:
                        dve.wait_ge(resid.sem, resid.at(s - 1))
                        if n == 0:
                            dve.wait_ge(N["post"]["out"].sem, N["post"]["out"].at(s))
                        else:
                            dve.wait_ge(N["next"]["out"].sem, N["next"]["out"].at(s))
                        if n == 1:
                            dve.wait_ge(z_out.sem, z_out.at(s))
                    dve.tensor_tensor(Z[:, t, :], fb[t % 2][0:T, 0:H], R[:, t, :], ALU.add).then_inc(o_done.sem, 1)

        loop(dve, step)

    @block.scalar
    def _(act):
        act.wait_ge(setup, 1)

        def root(s, k):
            c = ("pre", "post", "next").index(k)
            act.wait_ge(N[k]["v"].sem, N[k]["v"].at(s))
            act.wait_ge(N[k]["rs"].sem, N[k]["rs"].at(s - 1))
            act.activation(st[k]["sd"][:, :], st[k]["v"][:, :], ACT.Sqrt, bias=epst[0:T, c:c + 1]).then_inc(N[k]["sd"].sem, 1)

        def step(s):
            if runs(F_PRE, s):
                root(s, "pre")
            if runs(F_MID, s):
                for f, (f0, fn) in enumerate(ftiles):
                    act.wait_ge(h_mm.sem, h_mm.at(s, f))
                    if gated:
                        act.wait_ge(h_val.sem, h_val.at(s, f - 2) if f >= 2 else h_val.at(s - 1, NF - 2 + f))
                        act.activation(sg[f % 2][0:fn, :], hb[(2 * f + 1) % 4][0:fn, 0:GT], ACT.Silu, bias=W["bg"][0:fn, f:f + 1])\
                           .then_inc(h_act.sem, 1)
                    else:
                        act.wait_ge(h_lo.sem, h_lo.at(s, f - 2) if f >= 2 else h_lo.at(s - 1, NF - 2 + f))
                        act.activation(hf[f % 2][0:fn, :], hb[f % 4][0:fn, 0:GT], ACT.Relu, bias=W["b1"][0:fn, f:f + 1])\
                           .then_inc(h_act.sem, 1)
                        act.wait_ge(h_act.sem, h_act.at(s, f))
                        act.sem_inc(h_val.sem, 1)
            if runs(F_PRE, s):
                for k in range(KT):
                    act.wait_ge(p_mm.sem, p_mm.at(s, k))
                    if k == 0:
                        act.wait_ge(h_mm.sem, h_mm.at(s))
                    act.copy(XT[0][:, k, :], tb[k][:, 0:GT]).then_inc(p_hi.sem, 1)
            if runs(F_POST, s):
                if n == 0:
                    root(s, "post")
                root(s, "next")
                for k in range(KT):
                    act.wait_ge(q_mm.sem, q_mm.at(s, k))
                    act.wait_ge(zt_out[k].sem, zt_out[k].at(s - 1))
                    act.copy(ZT[:, k, :], tb[k][:, 0:GT]).then_inc(q_done.sem, 1)

        loop(act, step)

    @block.gpsimd
    def _(pool):
        def step(s):
            if runs(F_PRE, s):
                if n == 0:
                    g = N["pre"]
                    pool.wait_ge(g["out"].sem, g["out"].at(s))
                    pool.tensor_tensor(Xn[:, :, :], Xn[:, :, :], wide(W["gamma1"]), ALU.mult).then_inc(base.sem, 1)
                    pool.wait_ge(base.sem, base.at(s))
                    pool.wait_ge(p_mm.sem, p_mm.at(s - 1))
                    pool.wait_ge(resid.sem, resid.at(s - 1))
                    pool.tensor_tensor(Xs[:, :, :], Xn[:, :, :], wide(W["beta1"]), ALU.add).then_inc(g["b"].sem, 1)
                    pool.wait_ge(g["b"].sem, g["b"].at(s))
                    pool.sem_inc(g["g"].sem, 1)
            if runs(F_POST, s) and n == 0:
                g = N["post"]
                pool.wait_ge(g["out"].sem, g["out"].at(s))
                pool.tensor_tensor(Zn[:, :, :], Zn[:, :, :], wide(W["gamma2"]), ALU.mult).then_inc(gbase.sem, 1)
                pool.wait_ge(gbase.sem, gbase.at(s))
                pool.wait_ge(z_out.sem, z_out.at(s - 1))
                pool.wait_ge(N["next"]["out"].sem, N["next"]["out"].at(s - 1))
                pool.tensor_tensor(Zs[:, :, :], Zn[:, :, :], wide(W["beta2"]), ALU.add).then_inc(g["b"].sem, 1)
                pool.wait_ge(g["b"].sem, g["b"].at(s))
                pool.sem_inc(g["g"].sem, 1)
            if runs(F_POST, s) and n == 2:
                pool.wait_ge(N["next"]["out"].sem, N["next"]["out"].at(s))
                pool.wait_ge(z_out.sem, z_out.at(s - 1))
                pool.tensor_tensor(Zg[:, :, :], Zx[:, :, :], wide(W["gq"]), ALU.mult).then_inc(gbase.sem, 1)
                pool.wait_ge(gbase.sem, gbase.at(s))
                pool.tensor_tensor(Zg[:, :, :], Zg[:, :, :], wide(W["bo"]), ALU.add).then_inc(zg2.sem, 1)
            if runs(F_PRE, s):
                if n == 0:
                    src = Xs
                    pool.wait_ge(o_done.sem, o_done.at(s))
                else:
                    src = Yin
                    pool.wait_ge(o_done.sem, o_done.at(s))
                    pool.wait_ge(y_in.sem, y_in.at(s))
                pool.sem_inc(pool_gate, 1)
                if n == 2:
                    pool.tensor_copy(R[:, :, :], src[:, :, :]).then_inc(resid.sem, 1)
                else:
                    pool.tensor_tensor(R[:, :, :], src[:, :, :], wide(W["b2"]), ALU.add).then_inc(resid.sem, 1)

        loop(pool, step)

    @block.sync
    def _(sp):
        def group(ap, s):
            return row(ap.rearrange("(g t) p h -> g p t h", t=GB), s)

        def step(s):
            if runs(F_PRE, s):
                src = group(io["y"], s + 1)
                last = N["pre"]["out"]
                sp.wait_ge(last.sem, last.at(s - 1))
                if n != 0:
                    sp.wait_ge(resid.sem, resid.at(s - 1))
                sp.dma_start(Yin[:, :, :], src).then_inc(y_in.sem, 16)
            if runs(F_POST, s):
                dst = group(io["x_next"], s - 1)
                dstT = row(io["xT_next"].rearrange("(g t) (k p) q -> g p k t q", t=GB, k=KT), s - 1)
                zsrc, zr = {0: (Zs, N["post"]["b"] if n == 0 else None), 1: (Z, None), 2: (Zg, zg2)}[n]
                if n == 1:
                    sp.wait_ge(o_done.sem, o_done.at(s - 1))
                else:
                    sp.wait_ge(zr.sem, zr.at(s))
                sp.dma_start(dst, zsrc[:, :, :]).then_inc(z_out.sem, 16)
                sp.wait_ge(q_done.sem, q_done.at(s))
                sp.dma_start(dstT[:, 0], ZT[:, 0, :].rearrange("p (t q) -> p t q", t=GB)).then_inc(zt_out[0].sem, 16)
                sp.dma_start(dstT[:, 1], ZT[:, 1, :].rearrange("p (t q) -> p t q", t=GB)).then_inc(zt_out[1].sem, 16)

        loop(sp, step)
        sp.wait_ge(z_out.sem, z_out.at(NG))
        for k in range(KT):
            sp.wait_ge(zt_out[k].sem, zt_out[k].at(NG))


def prepare(nc, name, loads, scales=(), splits=()):
    loaded = nc.alloc_semaphore(f"{name}_loaded")
    scaled = nc.alloc_semaphore(f"{name}_scaled")
    high = nc.alloc_semaphore(f"{name}_high")

    with nc.Block() as block:
        @block.sync
        def _(sp):
            for dst, src in loads:
                sp.dma_start(dst, src).then_inc(loaded, 16)
            sp.wait_ge(loaded, 16 * len(loads))

        @block.vector
        def _(dve):
            dve.wait_ge(loaded, 16 * len(loads))
            for src, dst, gain in scales:
                for k in range(src.shape[1]):
                    ins = dve.tensor_scalar(dst[:, k, :], src[:, k, :], gain[:, k:k + 1], None, ALU.mult)
                ins.then_inc(scaled, 1)
            if scales and splits:
                dve.wait_ge(scaled, len(scales))
            for q, (full, hi, lo) in enumerate(splits):
                dve.wait_ge(high, q + 1)
                dve.tensor_tensor(lo, full, hi.bitcast(F32), ALU.subtract)

        @block.scalar
        def _(act):
            act.wait_ge(loaded, 16 * len(loads))
            if scales and splits:
                act.wait_ge(scaled, len(scales))
            for full, hi, lo in splits:
                act.copy(hi, full).then_inc(high, 1)


def rows(ap):
    return ap.rearrange("(k p) c -> p k c", p=P)


def spread(ap, n):
    return ap.rearrange("(o h) -> o h", o=1).to_broadcast([n, ap.shape[0]])


def tiles(nc, ctx, name, shapes):
    made = {}
    for k, shape in shapes.items():
        if shape[0] == "pair":
            made[k] = [ctx.enter_context(nc.sbuf_tensor(f"{name}_{k}_{h}", list(shape[1:]), F32R)) for h in ("hi", "lo")]
        else:
            made[k] = ctx.enter_context(nc.sbuf_tensor(f"{name}_{k}", list(shape), F32))
    return made


def setup_layer0(nc, ctx, io):
    W = tiles(nc, ctx, "w0", {
        "wq": (P, KT, 1024), "wk": ("pair", P, KT, 1024), "wv": ("pair", P, KT, 1024), "wo": (P, 8, H),
        "we": (P, KT, 2, 2 * UH), "ce": (1, 2, 2 * UH), "ones": (1, P), "pb": (P, 8), "cb": (P, 8),
        "segm": (T, NR), "cmask": (T, C), "ident": (P, P)})
    W["rst"] = ctx.enter_context(nc.sbuf_tensor("w0_relpos", [P, 16, NR], F32R))
    with ExitStack() as tmp:
        raw = tiles(nc, tmp, "s0", {"wk": (P, KT, 1024), "wv": (P, KT, 1024)})
        prepare(nc, "s0a", [
            (W["wq"][:, :, :], rows(io["L0_Wq"])), (raw["wk"][:, :, :], rows(io["L0_Wk"])), (raw["wv"][:, :, :], rows(io["L0_Wv"])),
            (W["wo"][:, :, :], rows(io["L0_WoT"])), (W["ident"][:, :], io["ident"])],
            splits=[(raw[k][:, kk, :], W[k][0][:, kk, :], W[k][1][:, kk, :]) for k in ("wk", "wv") for kk in range(KT)])
    with ExitStack() as tmp:
        t = tiles(nc, tmp, "t0", {"wr": (P, KT, 1024), "pos": (P, KT, NR), "wqT": (P, 8, H), "E": (P, 8, 4), "sb": (P, 8),
                                  "rawp": (P, 8), "rawc": (P, 8), "seg": (T, C), "zero": (T, NR), "mask": (T, C)})
        seg8 = tmp.enter_context(nc.sbuf_tensor("t0_seg8", [T, C], U8))
        ps = [tmp.enter_context(nc.psum_tensor(f"t0_ps{k}", [P, 512], F32)) for k in range(4)]
        loaded, zeroed, sflt = (nc.alloc_semaphore(f"t0_{k}") for k in ("loaded", "zeroed", "seg_float"))
        dz, dsk, dld = (nc.alloc_semaphore(f"t0_{k}") for k in ("seg_cleared", "seg_skewed", "seg_back"))
        r_mm, r_hi, r_lo = (nc.alloc_semaphore(f"t0_{k}") for k in ("r_mm", "r_hi", "r_lo"))
        e_mm = nc.alloc_semaphore("t0_e_mm")
        loads = [(t["wr"][:, :, :], rows(io["L0_Wr"])), (t["pos"][:, :, :], rows(io["L0_posT"])),
                 (t["wqT"][:, :, :], rows(io["L0_WqT"])), (t["E"][:, :, :], io["L0_segE"]), (t["sb"][:, :], io["L0_segb"]),
                 (t["rawp"][:, :], io["L0_posb"]), (t["rawc"][:, :], io["L0_contb"]), (seg8[:, :], io["seg"]),
                 (t["mask"][:, :], io["cmask"])]
        with nc.Block() as block:
            @block.sync
            def _(sp):
                for dst, src in loads:
                    sp.dma_start(dst, src).then_inc(loaded, 16)
                sp.wait_ge(zeroed, 1)
                sp.dma_start(io["segscr"], t["zero"][:, :]).then_inc(dz, 16)
                sp.wait_ge(dz, 16)
                sp.wait_ge(sflt, 1)
                skew = bass.AP(tensor=io["segscr"].tensor, offset=io["segscr"].offset + T - 1, ap=[[NR - 1, T], [1, C]])
                sp.dma_start(skew, t["seg"][:, :]).then_inc(dsk, 16)
                sp.wait_ge(dsk, 16)
                sp.dma_start(W["segm"][:, :], io["segscr"]).then_inc(dld, 16)
                sp.wait_ge(dld, 16)

            @block.vector
            def _(dve):
                dve.memset(t["zero"][:, :], 0.0).then_inc(zeroed, 1)
                dve.memset(W["ones"][:, :], 1.0)
                dve.wait_ge(loaded, 16 * len(loads))
                dve.tensor_copy(t["seg"][:, :], seg8[:, :]).then_inc(sflt, 1)
                dve.tensor_scalar(W["cmask"][:, :], t["mask"][:, :], NEG, None, ALU.mult)
                dve.tensor_scalar(W["pb"][:, :], t["rawp"][:, :], 0.125, None, ALU.mult)
                dve.tensor_scalar(W["cb"][:, :], t["rawc"][:, :], 0.125, None, ALU.mult)
                for q in range(8):
                    src, even, odd = ps[q % 2], 2 * q, 2 * q + 1
                    dve.wait_ge(r_hi, q + 1)
                    dve.tensor_tensor(W["rst"][64:128, even, :], src[0:64, 0:NR], W["rst"][0:64, even, :].bitcast(F32), ALU.subtract)
                    dve.tensor_tensor(W["rst"][0:64, odd, :], src[64:128, 0:NR], W["rst"][64:128, odd, :].bitcast(F32),
                                      ALU.subtract).then_inc(r_lo, 1)

            @block.scalar
            def _(act):
                for q in range(8):
                    act.wait_ge(r_mm, q + 1)
                    act.copy(W["rst"][0:64, 2 * q, :], ps[q % 2][0:64, 0:NR])
                    act.copy(W["rst"][64:128, 2 * q + 1, :], ps[q % 2][64:128, 0:NR]).then_inc(r_hi, 1)
                act.wait_ge(e_mm, 1)
                for s in range(2):
                    for k in range(KT):
                        src = ps[2][:, k * 32:k * 32 + 32].rearrange("p (n q s r) -> p n q s r", n=2, q=4, s=2)[:, :, :, s, :]
                        dst = W["we"][:, k, :, s * UH:(s + 1) * UH].rearrange("p n (q r) -> p n q r", q=4)
                        act.activation(dst, src, ACT.Copy, scale=0.125)
                    src = ps[3][0:1, 0:32].rearrange("p (n q s r) -> p n q s r", n=2, q=4, s=2)[:, :, :, s, :]
                    dst = W["ce"][0:1, :, s * UH:(s + 1) * UH].rearrange("p n (q r) -> p n q r", q=4)
                    act.activation(dst, src, ACT.Copy, scale=0.125)

            @block.tensor
            def _(pe):
                pe.wait_ge(loaded, 16 * len(loads))
                for q in range(8):
                    if q >= 2:
                        pe.wait_ge(r_lo, q - 1)
                    for k in range(KT):
                        mm = pe.matmul(ps[q % 2][:, 0:NR], t["wr"][:, k, q * P:(q + 1) * P], t["pos"][:, k, :], start=(k == 0), stop=(k == KT - 1))
                    mm.then_inc(r_mm, 1)
                for q in range(8):
                    for k in range(KT):
                        pe.matmul(ps[2][:, k * 32 + q * 4:k * 32 + q * 4 + 4], t["wqT"][:, q, k * P:(k + 1) * P], t["E"][:, q, :],
                                  start=True, stop=True)
                    mm = pe.matmul(ps[3][0:1, q * 4:q * 4 + 4], t["sb"][:, q:q + 1], t["E"][:, q, :], start=True, stop=True)
                mm.then_inc(e_mm, 1)
    return W


def setup_layer1(nc, ctx, io):
    W = tiles(nc, ctx, "w1", {
        "wq": (P, KT, 1024), "wk": (P, KT, 1024), "wv": (P, KT, 1024), "wo": (P, 8, H), "ident": (P, P), "gain": (P, KT),
        "cosq": (P, T), "sinq": (P, T), "cosk": (P, T), "sink": (P, T), "mask": (T, T + 32),
        "memk": (P, B, 8), "perk": (P, 8, 16)})
    with ExitStack() as tmp:
        t = tiles(nc, tmp, "t1", {"wk": (P, KT, 1024), "wv": (P, KT, 1024), "wm": (P, KT, H), "means": (P, KT, B), "pw": (P, KT),
                                  "sq": (P, KT, B), "avg": (P, P), "sd": (P, B), "rs": (P, B), "pool": (P, KT, B),
                                  "tok": (P, KT, B), "memv": (B, 1024), "eps": (P, 1)})
        ps = [tmp.enter_context(nc.psum_tensor(f"t1_ps{k}", [P, 512], F32)) for k in range(5)]
        names = ("loaded", "ready", "squared", "ms_mm", "rooted", "inv", "pooled", "gained", "tok_mm", "tok_sb", "kv_mm", "v_sb", "v_out")
        s = {k: nc.alloc_semaphore(f"t1_{k}") for k in names}
        loads = [(W["wq"][:, :, :], rows(io["L1_Wq"])), (t["wk"][:, :, :], rows(io["L1_Wk"])), (t["wv"][:, :, :], rows(io["L1_Wv"])),
                 (W["wo"][:, :, :], rows(io["L1_Wo"])), (W["ident"][:, :], io["ident"]), (W["gain"][:, :], io["L1_gain"]),
                 (W["cosq"][:, :], io["cos8"][:, 0:T]), (W["sinq"][:, :], io["sin8"][:, 0:T]),
                 (W["cosk"][:, :], io["cos"][:, 0:T]), (W["sink"][:, :], io["sin"][:, 0:T]), (W["mask"][:, :], io["causal"]),
                 (W["perk"][:, :, :], io["L1_perk"]), (t["wm"][:, :, :], rows(io["L1_Wm"])),
                 (t["means"][:, :, :], io["means"].rearrange("k p b -> p k b")), (t["pw"][:, :], io["L1_poolw"])]
        with nc.Block() as block:
            @block.sync
            def _(sp):
                for dst, src in loads:
                    sp.dma_start(dst, src).then_inc(s["loaded"], 16)
                sp.wait_ge(s["v_sb"], 2)
                sp.dma_start(io["memv"], t["memv"][:, :]).then_inc(s["v_out"], 16)
                sp.wait_ge(s["v_out"], 16)

            @block.vector
            def _(dve):
                dve.memset(t["avg"][:, :], 1.0 / H)
                dve.memset(t["eps"][:, :], 1.1920929e-07)
                dve.drain().then_inc(s["ready"], 1)
                dve.wait_ge(s["loaded"], 16 * len(loads))
                dve.tensor_tensor(t["sq"][:, :, :], t["means"][:, :, :], t["means"][:, :, :], ALU.mult).then_inc(s["squared"], 1)
                dve.wait_ge(s["rooted"], 1)
                dve.reciprocal(t["rs"][:, :], t["sd"][:, :]).then_inc(s["inv"], 1)
                dve.wait_ge(s["inv"], 1)
                dve.tensor_tensor(t["pool"][:, :, :], t["means"][:, :, :], t["rs"][:, None, :].to_broadcast([P, KT, B]), ALU.mult)\
                   .then_inc(s["pooled"], 1)
                dve.wait_ge(s["pooled"], 1)
                for k in range(KT):
                    ins = dve.tensor_scalar(t["pool"][:, k, :], t["pool"][:, k, :], t["pw"][:, k:k + 1], None, ALU.mult)
                ins.then_inc(s["gained"], 1)
                for src, dst in ((W["wq"], W["wq"]), (t["wk"], W["wk"]), (t["wv"], W["wv"])):
                    for k in range(KT):
                        dve.tensor_scalar(dst[:, k, :], src[:, k, :], W["gain"][:, k:k + 1], None, ALU.mult)

            @block.scalar
            def _(act):
                act.wait_ge(s["ready"], 1)
                act.wait_ge(s["ms_mm"], 1)
                act.activation(t["sd"][:, :], ps[0][:, 0:B], ACT.Sqrt, bias=t["eps"][:, 0:1]).then_inc(s["rooted"], 1)
                act.wait_ge(s["tok_mm"], KT)
                for k in range(KT):
                    act.copy(t["tok"][:, k, :], ps[1][:, k * B:(k + 1) * B]).then_inc(s["tok_sb"], 1)
                act.wait_ge(s["kv_mm"], 1)
                act.copy(W["memk"][:, :, :].rearrange("p b t -> p t b"), ps[2][:, 0:8 * B].rearrange("p (t b) -> p t b", t=8))
                for g in range(2):
                    act.wait_ge(s["kv_mm"], 2 + g)
                    act.copy(t["memv"][:, g * 512:(g + 1) * 512], ps[3 + g][0:B, :]).then_inc(s["v_sb"], 1)

            @block.tensor
            def _(pe):
                pe.wait_ge(s["ready"], 1)
                pe.wait_ge(s["squared"], 1)
                for k in range(KT):
                    mm = pe.matmul(ps[0][:, 0:B], t["avg"][:, :], t["sq"][:, k, :], start=(k == 0), stop=(k == KT - 1))
                mm.then_inc(s["ms_mm"], 1)
                pe.wait_ge(s["gained"], 1)
                for o in range(KT):
                    for k in range(KT):
                        mm = pe.matmul(ps[1][:, o * B:(o + 1) * B], t["wm"][:, k, o * P:(o + 1) * P], t["pool"][:, k, :],
                                       start=(k == 0), stop=(k == KT - 1))
                    mm.then_inc(s["tok_mm"], 1)
                pe.wait_ge(s["tok_sb"], KT)
                for o in range(8):
                    for k in range(KT):
                        mm = pe.matmul(ps[2][:, o * B:(o + 1) * B], t["wk"][:, k, o * P:(o + 1) * P], t["tok"][:, k, :],
                                       start=(k == 0), stop=(k == KT - 1))
                mm.then_inc(s["kv_mm"], 1)
                for g in range(2):
                    for k in range(KT):
                        mm = pe.matmul(ps[3 + g][0:B, :], t["tok"][:, k, :], t["wv"][:, k, g * 512:(g + 1) * 512],
                                       start=(k == 0), stop=(k == KT - 1))
                    mm.then_inc(s["kv_mm"], 1)
    return W


def setup_layer2(nc, ctx, io):
    W = tiles(nc, ctx, "w2", {
        "wq": (P, KT, 1024), "wk": (P, KT, H), "wv": (P, KT, H), "wo": (P, 8, H), "ident": (P, P), "gain": (P, KT),
        "cosq": (P, T), "sinq": (P, T), "cosk": (P, C), "sink": (P, C)})
    prepare(nc, "s2", [
        (W["wq"][:, :, :], rows(io["L2_Wq"])), (W["wk"][:, :, :], rows(io["L2_Wk"])), (W["wv"][:, :, :], rows(io["L2_Wv"])),
        (W["wo"][:, :, :], rows(io["L2_Wo"])), (W["ident"][:, :], io["ident"]), (W["gain"][:, :], io["L2_gain"]),
        (W["cosq"][:, :], io["cos8"][:, 0:T]), (W["sinq"][:, :], io["sin8"][:, 0:T]),
        (W["cosk"][:, :], io["cos"]), (W["sink"][:, :], io["sin"])],
        scales=[(W[k], W[k], W["gain"]) for k in ("wq", "wk", "wv")])
    return W


def setup_layer3(nc, ctx, io):
    W = tiles(nc, ctx, "w3", {
        "wq": (P, KT, 512), "wk": (P, KT, 512), "wv": (P, KT, H), "wo": (P, KT, H), "ident": (P, P), "gq": (P, KT), "gkv": (P, KT),
        "neg": (P, 1)})
    prepare(nc, "s3", [
        (W["wq"][:, :, :], rows(io["L3_Wq"])), (W["wk"][:, :, :], rows(io["L3_Wk"])), (W["wv"][:, :, :], rows(io["L3_Wv"])),
        (W["wo"][:, :, :], rows(io["L3_Wo"])), (W["ident"][:, :], io["ident"]), (W["gq"][:, :], io["L3_gq"]),
        (W["gkv"][:, :], io["L3_gkv"]), (W["neg"][:, :], io["neg"])],
        scales=[(W["wq"], W["wq"], W["gq"]), (W["wk"], W["wk"], W["gkv"]), (W["wv"], W["wv"], W["gkv"])])
    return W


F_TILES = {0: [(k * P, P) for k in range(8)], 1: [(k * P, P) for k in range(5)] + [(640, 42)], 2: [(k * P, P) for k in range(8)]}


def setup_feed_forward(nc, ctx, n, io):
    ftiles = F_TILES[n]
    NF, width = len(ftiles), ftiles[-1][0] + ftiles[-1][1]
    cols = width if n == 0 else 2 * width
    shapes = {"w1": ("pair", P, KT, cols), "w2": ("pair", P, NF, H), "ident": (P, P), "b1": (P, NF), "bg": (P, NF)}
    shapes.update({0: {k: (T, H) for k in ("gamma1", "beta1", "gamma2", "beta2", "b2")},
                   1: {"b2": (T, H), "gain": (P, KT)}, 2: {"gq": (T, H), "bo": (T, H), "gain": (P, KT)}}[n])
    W = tiles(nc, ctx, f"wf{n}", shapes)
    with ExitStack() as tmp:
        raw = tiles(nc, tmp, f"sf{n}", {"w1": (P, KT, cols), "w2": (P, NF, H)})
        loads = [(W["ident"][:, :], io["ident"])]
        if n == 2:
            loads += [(raw["w1"][:, :, 0:width], rows(io["L2_Wup"])), (raw["w1"][:, :, width:cols], rows(io["L2_Wgate"]))]
        else:
            loads.append((raw["w1"][:, :, :], rows(io[f"F{n}_W1"])))
        whole = [f for f, (f0, fn) in enumerate(ftiles) if fn == P]
        nw = len(whole)
        loads.append((raw["w2"][:, 0:nw, :], rows(io[f"F{n}_W2"][0:nw * P, :])))
        for f, (f0, fn) in enumerate(ftiles):
            if fn < P:
                loads.append((raw["w2"][0:fn, f, :], io[f"F{n}_W2"][f0:f0 + fn, :]))
        if n < 2:
            for k in ["b1"] if n == 0 else ["b1", "bg"]:
                loads.append((W[k][:, :], io[f"F{n}_{k}"]))
            loads.append((W["b2"][:, :], spread(io[f"F{n}_b2"], T)))
        if n == 0:
            for k in ("gamma1", "beta1", "gamma2", "beta2"):
                loads.append((W[k][:, :], spread(io[f"F0_{k}"], T)))
        if n > 0:
            loads.append((W["gain"][:, :], io[f"F{n}_gain"]))
        if n == 2:
            loads += [(W[k][:, :], io["zeros"]) for k in ("b1", "bg")]
            loads += [(W["gq"][:, :], spread(io["L3_gq_row"], T)), (W["bo"][:, :], spread(io["L3_bo"], T))]
        splits = [(raw["w1"][:, kk, :], W["w1"][0][:, kk, :], W["w1"][1][:, kk, :]) for kk in range(KT)]
        splits.append(tuple(w[:, 0:nw, :] for w in (raw["w2"], *W["w2"])))
        for f, (f0, fn) in enumerate(ftiles):
            if fn < P:
                splits.append(tuple(w[0:fn, f, :] for w in (raw["w2"], *W["w2"])))
        prepare(nc, f"sf{n}", loads, scales=[(raw["w1"], raw["w1"], W["gain"])] if n else (), splits=splits)
    W["f"] = width
    return W, ftiles


def program(nc, io):
    dram = lambda name, shape: nc.dram_tensor(name, shape, F32).ap()
    ctxnT = dram("ctx_normT", (B, H, CP))
    means, memv = dram("ctx_means", (KT, P, B)), dram("mem_values", (B, 1024))
    segscr = dram("seg_skew", (T, NR))
    relpos = [dram(f"relpos_skew{g}", (T, 4, NR)) for g in range(2)]
    y = dram("attn_out", (B, T, H))
    x = [dram(f"x_{n}", (B, T, H)) for n in range(3)]
    xT = [dram(f"x_normT_{n}", (B, H, T)) for n in range(3)]
    io = dict(io, means=means, memv=memv, segscr=segscr)

    with nc.cleanup_on_exit(), ExitStack() as ctx:
        ident = ctx.enter_context(nc.sbuf_tensor("c_ident", [P, P], F32))
        prepare(nc, "sc", [(ident[:, :], io["ident"])])
        context_pass(nc, ctx, ident, dict(ctx=io["ctx"], ctxnT=ctxnT, means=means))

    setups = [setup_layer0, setup_layer1, setup_layer2, setup_layer3]
    streams = [dict(ctxT=io["ctxT"], ctx_cols=C, xT=io["xT"], res=io["x"], y=y, gscr=relpos),
               dict(xT=xT[0], res=x[0], y=y, memv=memv, perv=io["L1_perv"]),
               dict(ctxT=ctxnT, ctx_cols=CP, xT=xT[1], res=x[1], y=y, mask=io["mask"]),
               dict(ctxT=ctxnT, ctx_cols=CP, xT=xT[2], res=x[2], y=io["out"])]
    guards = [(1e-12, 1e-12, 1.1920929e-07), (1.1920929e-07, 1e-6, 1e-6), (1e-6, 1e-6, 1e-6)]
    for n, L in enumerate(LAYERS):
        with nc.cleanup_on_exit(), ExitStack() as ctx:
            W = setups[n](nc, ctx, io)
            attention(nc, ctx, L, W, streams[n])
        if n < 3:
            with nc.cleanup_on_exit(), ExitStack() as ctx:
                W, ftiles = setup_feed_forward(nc, ctx, n, io)
                feed_forward(nc, ctx, n, W["ident"], W, dict(y=y, x_next=x[n], xT_next=xT[n]), *guards[n], ftiles)


def kernel(**inputs):
    import numpy as _np
    import concourse.bacc as _bacc
    from concourse import mybir as _mybir
    from concourse.bass_utils import run_bass_kernel_spmd as _run

    a = {k.replace("_xattn", ""): _np.asarray(v) for k, v in inputs.items()}
    f32 = _np.float32
    pairs = _np.concatenate([h * 64 + _np.r_[0:64:2, 1:64:2] for h in range(16)])
    qkv = a["L1_to_qkv_w"]
    per_row = lambda v: v.reshape(KT, P).T
    per_unit = lambda v: _np.pad(v, (0, -len(v) % P)).reshape(-1, P).T
    E = _np.zeros((P, 8, 4), a["L0_segment_encoding"].dtype)
    for s in range(2):
        for r in range(2):
            E[64 * r:64 * r + 64, :, 2 * s + r] = a["L0_segment_encoding"][s].reshape(8, 2, 64)[:, r, :].T
    doubled = lambda w: _np.repeat(w.T.reshape(H, 16, 1, 16), 2, axis=2).reshape(H, 512)
    freq = (f32(1.0) / f32(10000.0) ** (_np.arange(0, 64, 2, dtype=f32) / f32(64)))[_np.arange(P) % 32]
    angle = _np.arange(C, dtype=f32)[None, :] * freq[:, None]
    side = _np.where(_np.arange(P) // 32 % 2 == 0, f32(-1), f32(1))[:, None]
    cos, sin = _np.cos(angle).astype(f32), (_np.sin(angle) * side).astype(f32)
    causal = _np.concatenate([_np.where(_np.arange(T)[:, None] >= _np.arange(T)[None, :], f32(0), f32(NEG)), _np.zeros((T, 32), f32)], 1)
    arrays = {
        "ident": _np.eye(P, dtype=f32), "zeros": _np.zeros((P, 8), f32),
        "neg": _np.where(_np.arange(P) % 32 >= 16, f32(-1), f32(0))[:, None],
        "cos": cos, "sin": sin, "cos8": (cos / 8).astype(f32), "sin8": (sin / 8).astype(f32), "causal": causal.astype(f32),
        "x": a["x"], "xT": a["x"].transpose(0, 2, 1), "ctx": a["ctx_1024"], "ctxT": a["ctx_1024"].transpose(0, 2, 1),
        "cmask": a["mask_1x1xSxS2_ff0"][0, 0], "seg": a["mask_1xSxS2_bk1"][0], "mask": a["mask_Bx1xSxS2_ff0"][:, 0],
        "L0_Wq": a["L0_Wq"].reshape(H, 1024), "L0_WqT": a["L0_Wq"].reshape(H, 1024).T, "L0_Wk": a["L0_Wk"].reshape(H, 1024),
        "L0_Wv": a["L0_Wv"].reshape(H, 1024), "L0_Wr": a["L0_Wr"].reshape(H, 1024), "L0_WoT": a["L0_Wo"].reshape(H, 1024).T,
        "L0_posT": a["L0_position_encoding"][0].T[:, 1:1 + NR], "L0_segE": E, "L0_segb": a["L0_segment_bias"].reshape(8, P).T,
        "L0_posb": a["L0_position_bias"].reshape(8, P).T, "L0_contb": a["L0_content_bias"].reshape(8, P).T,
        "F0_W1": a["L0_W1"], "F0_b1": per_unit(a["L0_b1"]), "F0_W2": a["L0_W2"], "F0_b2": a["L0_b2"],
        "F0_gamma1": a["L0_ln1_gamma"], "F0_beta1": a["L0_ln1_beta"], "F0_gamma2": a["L0_ln2_gamma"], "F0_beta2": a["L0_ln2_beta"],
        "L1_Wq": qkv[:, 0:1024][:, pairs], "L1_Wk": qkv[:, 1024:2048][:, pairs], "L1_Wv": qkv[:, 2048:3072],
        "L1_Wo": a["L1_to_out_w"], "L1_gain": per_row(a["L1_attn_norm_w"]), "L1_Wm": a["L1_to_mem_tokens_w"],
        "L1_poolw": per_row(a["L1_mem_pool_norm_w"]),
        "L1_perk": a["L1_persist_mem"].transpose(0, 2, 1).reshape(1024, 16)[pairs].reshape(8, P, 16).transpose(1, 0, 2),
        "L1_perv": a["L1_persist_mem"].transpose(1, 0, 2),
        "F1_W1": a["L1_ff_w1"], "F1_b1": per_unit(a["L1_ff_b1"][:682]), "F1_bg": per_unit(a["L1_ff_b1"][682:]), "F1_W2": a["L1_ff_w2"], "F1_b2": a["L1_ff_b2"], "F1_gain": per_row(a["L1_ff_norm_w"]),
        "L2_Wq": a["L2_Wq"], "L2_Wk": a["L2_Wk"], "L2_Wv": a["L2_Wv"], "L2_Wo": a["L2_Wo"], "L2_gain": per_row(a["L2_ln1_w"]),
        "L2_Wup": a["L2_Wup"], "L2_Wgate": a["L2_Wgate"], "F2_W2": a["L2_Wdown"], "F2_gain": per_row(a["L2_ln2_w"]),
        "L3_Wq": doubled(a["L3_wq"]), "L3_Wk": doubled(a["L3_wk"]), "L3_Wv": a["L3_wv"].T, "L3_Wo": a["L3_wo"].T,
        "L3_gq": per_row(a["L3_gq"]), "L3_gkv": per_row(a["L3_gkv"]), "L3_gq_row": a["L3_gq"], "L3_bo": a["L3_bo"],
    }
    arrays = {f"in_{k}": _np.ascontiguousarray(v) for k, v in arrays.items()}
    nc = _bacc.Bacc("TRN2", target_bir_lowering=False, num_devices=1)
    io = {k[3:]: nc.dram_tensor(k, v.shape, _mybir.dt.from_np(v.dtype), kind="ExternalInput").ap() for k, v in arrays.items()}
    io["out"] = nc.dram_tensor("out", (B, T, H), F32, kind="ExternalOutput").ap()
    program(nc, io)
    return _run(nc, [arrays], core_ids=[0]).results[0]["out"]
```

```python
from contextlib import ExitStack

import numpy as np

import concourse.bass as bass
from concourse import mybir

F32 = mybir.dt.float32
F32R = mybir.dt.float32r
U8 = mybir.dt.uint8
ALU = mybir.AluOpType
ACT = mybir.ActivationFunctionType
AX = mybir.AxisListType

B, T, C, H = 32, 100, 361, 256
P = 128
KT = H // P
CT = 121
NCT = 3
CP = CT * NCT
CE = 362
NR = C + T - 1
UH = 8
UNITS = 2 * B
NEG = -1e30


class Signal:

    def __init__(self, nc, name, window, per, full, by=1):
        self.sem = nc.alloc_semaphore(name)
        self.window, self.per, self.full, self.by = window, per, full, by

    def at(self, u, i=None):
        i = self.per - 1 if i is None else i
        first, last = self.window
        if isinstance(u, int):
            before = self.per * max(0, min(u - 1, last) - first + 1)
            return self.by * (before + (i + 1 if first <= u <= last else 0))
        before = self.per * (self.full - first)
        return u * (self.per * self.by) + self.by * (before - self.full * self.per + i + 1)


def runs(window, u):
    return not isinstance(u, int) or window[0] <= u <= window[1]


def starts(u):
    return isinstance(u, int) and u == -1


def row(ap, i):
    if isinstance(i, int):
        return ap[i]
    names = " ".join(f"d{k}" for k in range(1, len(ap.shape)))
    rest = tuple(slice(None) for _ in ap.shape[1:])
    first = names.split()[0]
    return ap[(bass.ds(i, 1),) + rest].rearrange(f"a {names} -> (a {first}) " + " ".join(names.split()[1:]))


W_N, W_A, W_W, W_O = (-1, UNITS - 2), (0, UNITS - 1), (1, UNITS), (2, UNITS + 1)
A_FULL = 4


class Layer:

    def __init__(self, n, d, keys, key_tiles, aux, banks, at=None):
        self.n, self.d = n, d
        self.keys = keys
        self.key_tiles = key_tiles
        self.sw = key_tiles[-1][0] + key_tiles[-1][1]
        self.ncols = keys + keys % 2
        self.aux = aux
        self.banks = banks
        self.at = at or {}
        self.ot = UH * d // P


WIDE = [(0, CT), (CT, CT), (2 * CT, CT)]
LAYERS = [
    Layer(0, 64, C, WIDE,
          {(0, 0): "Q", (0, 1): "V", (1, 0): "T", (1, 1): "V", (2, 0): "W", (2, 1): "V", (3, 0): "G", (3, 1): "G", (4, 0): "GK",
           (4, 1): "G", (5, 0): "GK", (5, 1): "G", (6, 0): "K", (6, 1): "G", (7, 0): "K", (7, 1): "G"},
          {"K": [0, 2], "V": [0, 2], "Q": [1], "T": [1], "W": [1], "G": [1]}, {"Q_own": 0, "Q_position": 1, "Q_content": 5}),
    Layer(1, 64, T + 32, [(0, T), (T, 32)],
          {(1, 0): "Q", (1, 1): "K", (3, 0): "V", (3, 1): "T", (4, 1): "W"},
          {"Q": [0], "V": [1], "W": [1], "K": [2], "T": [0]}, {"Q_sum": 5, "K_sum": 3}),
    Layer(2, 64, C, WIDE,
          {(0, 0): "Q", (2, 0): "K", (4, 0): "VT", (6, 0): "W"},
          {"Q": [2], "V": [2], "W": [1], "K": [1], "T": [1]},
          {"Q_sum": 3, "K_sum": 4, "Q_hi": 4, "K_hi": 6, "Q_lo": 5, "K_lo": 6}),
    Layer(3, 16, C, WIDE,
          {(0, 0): "Q", (1, 0): "K", (2, 0): "K", (3, 0): "V", (4, 0): "T", (5, 1): "W"},
          {"Q": [0], "K": [1, 2], "V": [0], "T": [1], "W": [2]}),
]
AUX_WINDOW = {"Q": W_N, "K": W_N, "G": W_N, "V": W_A, "T": W_O, "W": W_O}


def attention(nc, ctx, L, W, io):
    n = L.n

    def sb(name, shape, dt=F32):
        return ctx.enter_context(nc.sbuf_tensor(f"a{n}_{name}", shape, dt))

    def sig(name, window, per, by=1):
        return Signal(nc, f"a{n}_{name}", window, per, A_FULL, by)

    S = [sb(f"scores{p}", [T, UH, L.sw]) for p in range(2)]
    V = [sb(f"values{p}", [CT, len(L.key_tiles), UH, L.d]) for p in range(2)]
    PT = [sb(f"probsT{p}", [P, len(L.key_tiles) * T]) for p in range(2)]
    mx = [sb(f"rowmax{p}", [T, UH]) for p in range(2)]
    nb = [sb(f"expbias{p}", [T, UH]) for p in range(2)]
    sums = [sb(f"sums{p}", [T, UH]) for p in range(2)]
    rec = sb("recip", [T, UH])
    On = sb("attn", [T, UH * L.d])
    OTs = sb("attnT", [P, L.ot * T])
    xres = sb("residual", [T, H])
    Yacc, Yout = sb("yacc", [T, H]), sb("yout", [T, H])
    xT = sb("queriesT", [P, KT, T])
    if n == 0:
        Kst = [sb(f"kstack{p}", [P, UH, CE], F32R) for p in range(2)]
        Qc = [sb(f"qc_hi{p}", [P, UH, T], F32R) for p in range(2)]
        Lc = [sb(f"qc_lo{p}", [P, UH // 2, T], F32R) for p in range(2)]
        Qp, Lp = sb("qp_hi", [P, UH, T], F32R), sb("qp_lo", [P, UH // 2, T], F32R)
        qcf, qpf = sb("qc", [P, 4, T]), sb("qp", [P, 4, T])
        qco, qpo = sb("qc_own", [P, 4, T], F32R), sb("qp_own", [P, 4, T], F32R)
        e0 = [sb(f"seg0_{p}", [T, UH]) for p in range(2)]
        de = [sb(f"segd_{p}", [T, UH]) for p in range(2)]
        mtot = sb("maxtotal", [T, UH])
        Gs = [sb(f"relpos{g}", [T, 4, NR]) for g in range(2)]
        craw, chi, clo = sb("ctx", [P, KT, CE + 2]), sb("ctx_hi", [P, KT, CE + 2], F32R), sb("ctx_lo", [P, KT, CE + 2], F32R)
    if n == 1:
        Kn = [sb(f"keys{p}", [P, 4, L.keys]) for p in range(2)]
        qf = [sb(f"queries{p}", [P, 4, T]) for p in range(2)]
        xTv = sb("valuesT", [P, KT, T])
        qsw, qcos = sb("rope_swapped", [P, 4, T]), sb("rope_cos", [P, 4, T])
        ksw, kcos = sb("rope_kswapped", [P, 4, T]), sb("rope_kcos", [P, 4, T])
        Vx = [sb(f"extra_values{p}", [32, UH, L.d]) for p in range(2)]
    if n == 2:
        Kst = [sb(f"kstack{p}", [P, 2, CE], F32R) for p in range(2)]
        Qh = [sb(f"q_hi{p}", [P, UH, T], F32R) for p in range(2)]
        Ql = [sb(f"q_lo{p}", [P, UH, T], F32R) for p in range(2)]
        qf, kf = sb("queries", [P, 4, T]), sb("keys", [P, CE])
        qsw, qcos = sb("rope_swapped", [P, 4, T]), sb("rope_cos", [P, 4, T])
        ksw, kcos = sb("rope_kswapped", [P, C]), sb("rope_kcos", [P, C])
        mask = [sb(f"mask{p}", [T, C]) for p in range(2)]
    if n == 3:
        Kst = [sb(f"kstack{p}", [P, 2, CE], F32R) for p in range(2)]
        khi = sb("k_hi", [P, 2, C], F32R)
        Qh = [sb(f"q_hi{p}", [P, 2, T], F32R) for p in range(2)]
        Ql = [sb(f"q_lo{p}", [P, 2, T], F32R) for p in range(2)]
    if n >= 2:
        cK, cV = sb("ctx_k", [P, KT, CE + 2]), sb("ctx_v", [P, KT, CE + 2])

    ps = [ctx.enter_context(nc.psum_tensor(f"a{n}_ps{k}", [P, 512], F32)) for k in range(8)]
    ac, aux, ptb, ob = ps[0:2], ps[2:5], ps[5:7], ps[7]

    setup = nc.alloc_semaphore(f"a{n}_setup")
    extras = nc.alloc_semaphore(f"a{n}_extras")
    sp_gate = nc.alloc_semaphore(f"a{n}_sp_gate")
    gate = nc.alloc_semaphore(f"a{n}_gate")
    ac_mm = sig("ac_mm", W_A, UH)
    scored = sig("scored", W_A, UH)
    biased = sig("biased", W_A, 1)
    maxed = sig("maxed", W_A, 1)
    probs = sig("probs", W_W, UH)
    pt_mm = sig("pt_mm", W_W, UH)
    pt_even = sig("pt_even", W_W, UH // 2)
    pt_odd = sig("pt_odd", W_W, UH // 2)
    pv_mm = sig("pv_mm", W_W, UH)
    recd = sig("recd", W_W, 1)
    normed = sig("normed", W_W, 1)
    count = {k: sum(s.count(k) for s in L.aux.values()) for k in AUX_WINDOW}
    aux_mm = {k: sig(f"{k}_mm", AUX_WINDOW[k], c) for k, c in count.items() if c}
    done = {k: sig(f"{k}_done", AUX_WINDOW[k], c) for k, c in count.items() if c}
    batch_sem = {k: nc.alloc_semaphore(f"a{n}_{k}") for k in ("xT_in", "res_in", "y_out", "ctxK_in", "ctxV_in")}
    if n == 0:
        qf_done = sig("qf_done", W_N, 2)
        qhi = sig("qhi", W_N, 2)
        qown = sig("qown", W_N, 2)
        qlo = sig("qlo", W_N, 2)
        segd = sig("segd", W_N, 1)
        khi_done = sig("khi", W_N, 4)
        split_hi = nc.alloc_semaphore("a0_split_hi")
        split_lo = nc.alloc_semaphore("a0_split_lo")
        g_out = [sig(f"g_out{g}", W_N, 1, 16) for g in range(2)]
        b_in = [sig(f"b_in{g}", W_N, 1, 16) for g in range(2)]
        b_add = [sig(f"b_add{g}", W_N, 1) for g in range(2)]
    if n in (1, 2):
        swp = {k: sig(f"{k}_swapped", W_N, 1) for k in "QK"}
        cosd = {k: sig(f"{k}_cos", W_N, 1) for k in "QK"}
        sind = {k: sig(f"{k}_sin", W_N, 1) for k in "QK"}
        roped = {k: sig(f"{k}_roped", W_N, 1) for k in "QK"}
    if n == 1:
        vx_in = [nc.alloc_semaphore(f"a1_vx{p}") for p in range(2)]
        kx_done = sig("kx_done", W_N, 1)
    if n == 2:
        m_in = [nc.alloc_semaphore(f"a2_mask{p}") for p in range(2)]
        qhi2 = sig("qhi", W_N, 1)
        khi2 = sig("khi", W_N, 1)
        qlo2 = sig("qlo", W_N, 1)
    if n == 3:
        khi3 = sig("khi", W_N, 2)
        qhi3 = sig("qhi", W_N, 1)

    parts = [(i, part) for i in range(UH) for part in range(2)]
    flat = [(at, k) for at in parts for k in L.aux.get(at, "")]
    order = []
    for m, (_, k) in enumerate(flat):
        number = sum(k == other for _, other in flat[:m])
        order.append((k, number, L.banks[k][number % len(L.banks[k])]))
    uses = {at: [m for m, (other, _) in enumerate(flat) if other == at] for at in parts}
    free = dict(done, **(swp if n in (1, 2) else {}))

    def bank_free(pe, u, m):
        v, q = u, m
        while True:
            q -= 1
            if q < 0:
                v, q = v - 1, len(order) - 1
            if isinstance(v, int) and v < -1:
                return
            k, i, bank = order[q]
            if bank == order[m][2] and runs(AUX_WINDOW[k], v):
                pe.wait_ge(free[k].sem, free[k].at(v, i))
                return

    def batch_of(j, par, ahead):
        return j + (par + ahead) // 2

    def loop(e, step):
        step(-1, -1, 1)
        for u in range(0, A_FULL):
            step(u, u // 2, u % 2)
        with e.Fori(A_FULL // 2, UNITS // 2 - 1) as j:
            step(2 * j, j, 0)
            step(2 * j + 1, j, 1)
        for u in range(UNITS - 2, UNITS + 2):
            step(u, u // 2, u % 2)

    heads = lambda i: slice(64 * (i % 2), 64 * (i % 2) + 64)
    block = ctx.enter_context(nc.Block())

    @block.tensor
    def _(pe):
        def mm3(out, w, x, first, last):
            pe.matmul(out, w[0], x[0], start=first, stop=False)
            pe.matmul(out, w[0], x[1], start=False, stop=False)
            return pe.matmul(out, w[1], x[0], start=False, stop=last)

        def project(u, j, par, m):
            k, i, bank = order[m]
            out = aux[bank]
            npar, nbatch = 1 - par, batch_of(j, par, 1)
            bank_free(pe, u, m)
            if k == "Q":
                pe.wait_ge(batch_sem["xT_in"], 16 * nbatch + 16)
                if n == 3:
                    for t in range(2):
                        for kk in range(KT):
                            mm = pe.matmul(out[:, t * T:(t + 1) * T], W["wq"][:, kk, (2 * npar + t) * P:(2 * npar + t + 1) * P],
                                           xT[:, kk, :], start=(kk == 0), stop=(kk == KT - 1))
                else:
                    for t in range(4):
                        for kk in range(KT):
                            mm = pe.matmul(out[:, t * T:(t + 1) * T], W["wq"][:, kk, (4 * npar + t) * P:(4 * npar + t + 1) * P],
                                           xT[:, kk, :], start=(kk == 0), stop=(kk == KT - 1))
                if n == 0:
                    seg = out[0:T, 4 * T:4 * T + 2 * UH]
                    for kk in range(KT):
                        pe.matmul(seg, xT[:, kk, :], W["we"][:, kk, npar, :], start=(kk == 0), stop=False)
                    mm = pe.matmul(seg, W["ones"][0:1, 0:T], W["ce"][0:1, npar, :], start=False, stop=True)
            if k == "K":
                if n == 0:
                    if i == 0 and par == 1:
                        pe.wait_ge(split_hi, nbatch + 1)
                        pe.wait_ge(split_lo, nbatch + 1)
                    c0 = (4 * npar + i) * P
                    for kk in range(KT):
                        mm = mm3(out[:, 0:CE], [w[:, kk, c0:c0 + P] for w in W["wk"]],
                                 [chi[:, kk, 0:CE], clo[:, kk, 0:CE]], kk == 0, kk == KT - 1)
                if n == 1:
                    for t in range(4):
                        for kk in range(KT):
                            mm = pe.matmul(out[:, t * T:(t + 1) * T], W["wk"][:, kk, (4 * npar + t) * P:(4 * npar + t + 1) * P],
                                           xT[:, kk, :], start=(kk == 0), stop=(kk == KT - 1))
                if n >= 2:
                    pe.wait_ge(batch_sem["ctxK_in"], 16 * nbatch + 16)
                    c0 = (npar if n == 2 else 2 * npar + i) * P
                    for kk in range(KT):
                        mm = pe.matmul(out[:, 0:C], W["wk"][:, kk, c0:c0 + P], cK[:, kk, 0:C], start=(kk == 0), stop=(kk == KT - 1))
            if k == "G":
                if i == 0:
                    pe.wait_ge(qhi.sem, qhi.at(u, 0))
                    pe.wait_ge(qlo.sem, qlo.at(u, 0))
                h = UH * npar + i
                pe.matmul(out[0:T, 0:NR], Qp[:, i, :], W["rst"][:, h, 0:NR], start=True, stop=False)
                mm = pe.matmul(out[0:T, 0:NR], Lp[heads(i), i // 2, :], W["rst"][heads(i), h, 0:NR], start=False, stop=True)
            if k == "V":
                if n == 0:
                    c0 = 512 * par
                    for kk in range(KT):
                        mm = mm3(out[0:CT, :], [x[:, kk, CT * i:CT * i + CT] for x in (chi, clo)],
                                 [w[:, kk, c0:c0 + 512] for w in W["wv"]], kk == 0, kk == KT - 1)
                if n == 1:
                    pe.wait_ge(batch_sem["ctxV_in"], 16 * j + 16)
                    for kk in range(KT):
                        mm = pe.matmul(out[0:T, :], xTv[:, kk, :], W["wv"][:, kk, 512 * par:512 * par + 512],
                                       start=(kk == 0), stop=(kk == KT - 1))
                if n >= 2:
                    pe.wait_ge(batch_sem["ctxV_in"], 16 * j + 16)
                    for t in range(NCT):
                        for kk in range(KT):
                            mm = pe.matmul(out[0:CT, t * P:(t + 1) * P], cV[:, kk, CT * t:CT * t + CT],
                                           W["wv"][:, kk, P * par:P * par + P], start=(kk == 0), stop=(kk == KT - 1))
            if k == "T":
                pe.wait_ge(normed.sem, normed.at(u - 1))
                for q in range(L.ot):
                    mm = pe.transpose(out[:, q * T:(q + 1) * T], On[:, q * P:(q + 1) * P], W["ident"][0:T, 0:T])
            if k == "W":
                pe.wait_ge(done["T"].sem, done["T"].at(u))
                for q in range(L.ot):
                    mm = pe.matmul(out[0:T, 0:H], OTs[:, q * T:(q + 1) * T], W["wo"][:, L.ot * par + q, :],
                                   start=(q == 0), stop=(q == L.ot - 1))
            mm.then_inc(aux_mm[k].sem, 1)

        def scores(u, par, i):
            if i >= 2:
                pe.wait_ge(scored.sem, scored.at(u, i - 2))
            else:
                pe.wait_ge(scored.sem, scored.at(u - 1, UH - 2 + i))
            out = ac[i % 2][0:T, 0:L.ncols]
            if n == 0:
                if i == 0:
                    pe.wait_ge(qhi.sem, qhi.at(u - 1, 1))
                    pe.wait_ge(qlo.sem, qlo.at(u - 1, 1))
                if i % 2 == 0:
                    pe.wait_ge(done["K"].sem, done["K"].at(u - 1, i // 2))
                pe.matmul(out, Qc[par][:, i, :], Kst[par][:, i, :], start=True, stop=False)
                mm = pe.matmul(out, Lc[par][heads(i), i // 2, :], Kst[par][heads(i), i, :], start=False, stop=True)
            if n == 1:
                if i == 0:
                    pe.wait_ge(roped["Q"].sem, roped["Q"].at(u - 1))
                    pe.wait_ge(roped["K"].sem, roped["K"].at(u - 1))
                    pe.wait_ge(kx_done.sem, kx_done.at(u - 1))
                mm = pe.matmul(out, qf[par][heads(i), i // 2, :], Kn[par][heads(i), i // 2, :], start=True, stop=True)
            if n == 2:
                if i == 0:
                    pe.wait_ge(qhi2.sem, qhi2.at(u - 1))
                    pe.wait_ge(qlo2.sem, qlo2.at(u - 1))
                    pe.wait_ge(done["K"].sem, done["K"].at(u - 1))
                kv = i // 4
                pe.matmul(out, Qh[par][:, i, :], Kst[par][:, kv, :], start=True, stop=False)
                mm = pe.matmul(out, Ql[par][heads(kv), i, :], Kst[par][heads(kv), kv, :], start=False, stop=True)
            if n == 3:
                if i == 0:
                    pe.wait_ge(done["Q"].sem, done["Q"].at(u - 1))
                if i % 4 == 0:
                    pe.wait_ge(done["K"].sem, done["K"].at(u - 1, i // 4))
                r = slice(32 * (i % 4), 32 * (i % 4) + 32)
                pe.matmul(out, Qh[par][r, i // 4, :], Kst[par][r, i // 4, :], start=True, stop=False)
                mm = pe.matmul(out, Ql[par][r, i // 4, :], Kst[par][r, i // 4, :], start=False, stop=True)
            mm.then_inc(ac_mm.sem, 1)

        def moved(u, i):
            s = pt_odd if i % 2 else pt_even
            pe.wait_ge(s.sem, s.at(u, i // 2))

        def transposes(u, par, i):
            wpar = 1 - par
            pe.wait_ge(probs.sem, probs.at(u, i))
            if i >= 2:
                moved(u, i - 2)
            else:
                moved(u - 1, UH - 2 + i)
            for t, (c0, cn) in enumerate(L.key_tiles):
                mm = pe.transpose(ptb[i % 2][0:cn, t * T:(t + 1) * T], S[wpar][:, i, c0:c0 + cn], W["ident"][0:T, 0:T])
            mm.then_inc(pt_mm.sem, 1)

        def weigh(u, j, par, i):
            wpar = 1 - par
            moved(u, i)
            if i == 0:
                pe.wait_ge(done["V"].sem, done["V"].at(u - 1))
                if n == 1:
                    pe.wait_ge(vx_in[wpar], 16 * batch_of(j, par, -1) + 16)
                pe.wait_ge(normed.sem, normed.at(u - 1))
            out = ob[0:T, i * L.d:(i + 1) * L.d]
            last = len(L.key_tiles) - 1
            for t, (c0, cn) in enumerate(L.key_tiles):
                v = Vx[wpar][:, i, :] if n == 1 and t == 1 else V[wpar][0:cn, t, i // 4 if n == 2 else i, :]
                mm = pe.matmul(out, PT[i % 2][0:cn, t * T:(t + 1) * T], v, start=(t == 0), stop=(t == last))
            mm.then_inc(pv_mm.sem, 1)

        def products(u, j, par, i, part):
            for m in uses[i, part]:
                if runs(AUX_WINDOW[order[m][0]], u):
                    project(u, j, par, m)

        def step(u, j, par):
            if starts(u):
                pe.wait_ge(setup, 1)
                if n == 1:
                    pe.wait_ge(extras, 32)
            for i in range(UH):
                if runs(W_A, u):
                    scores(u, par, i)
                products(u, j, par, i, 0)
                if runs(W_W, u):
                    transposes(u, par, i)
                    if i > 0:
                        weigh(u, j, par, i - 1)
                products(u, j, par, i, 1)
            if runs(W_W, u):
                weigh(u, j, par, UH - 1)

        loop(pe, step)

    @block.vector
    def _(dve):
        def rope(u, par, k, m):
            _, _, bank = order[m]
            npar = 1 - par
            tile, swapped, cosb = (qf, qsw, qcos) if k == "Q" else ((Kn if n == 1 else kf), ksw, kcos)
            wide = n == 1 or k == "Q"
            src = aux[bank][:, 0:4 * T].rearrange("p (t q) -> p t q", t=4) if wide else aux[bank][:, 0:C]
            cos = W["cosq" if k == "Q" else "cosk"]
            cos = cos[:, None, 0:T].to_broadcast([P, 4, T]) if wide else cos[:, 0:C]
            cosv = cosb[:, :, :] if wide else cosb[:, :]
            dve.wait_ge(roped[k].sem, roped[k].at(u - 1))
            dve.tensor_tensor(cosv, src, cos, ALU.mult).then_inc(cosd[k].sem, 1)

        def rope_sum(u, j, par, k):
            npar = 1 - par
            if k == "Q":
                dst = qf[npar][:, :, :] if n == 1 else qf[:, :, :]
                a, b = qcos[:, :, :], qsw[:, :, :]
            elif n == 1:
                dst, a, b = Kn[npar][:, :, 0:T], kcos[:, :, :], ksw[:, :, :]
            else:
                dst, a, b = kf[:, 0:C], kcos[:, :], ksw[:, :]
            dve.wait_ge(cosd[k].sem, cosd[k].at(u))
            dve.wait_ge(sind[k].sem, sind[k].at(u))
            if n == 1:
                dve.wait_ge(ac_mm.sem, ac_mm.at(u - 1))
            elif k == "Q":
                dve.wait_ge(qlo2.sem, qlo2.at(u - 1))
                dve.wait_ge(qhi2.sem, qhi2.at(u - 1))
            else:
                dve.wait_ge(khi2.sem, khi2.at(u - 1))
                dve.wait_ge(done["K"].sem, done["K"].at(u - 1))
            dve.tensor_tensor(dst, a, b, ALU.add).then_inc(roped[k].sem, 1)
            if n == 1 and k == "K":
                nbatch = batch_of(j, par, 1)
                at = slice(nbatch, nbatch + 1) if isinstance(nbatch, int) else bass.ds(nbatch, 1)
                mem = W["memk"][:, at, 4 * npar:4 * npar + 4].rearrange("p a t -> p t a")
                dve.tensor_copy(Kn[npar][:, :, T:T + 16], mem.to_broadcast([P, 4, 16])).then_inc(kx_done.sem, 1)

        def queries_low(u, par):
            npar = 1 - par
            dve.wait_ge(roped["Q"].sem, roped["Q"].at(u))
            dve.wait_ge(ac_mm.sem, ac_mm.at(u - 1))
            dve.wait_ge(qhi2.sem, qhi2.at(u))
            for g in range(2):
                for r in range(2):
                    rr, dd = slice(64 * r, 64 * r + 64), slice(64 * g, 64 * g + 64)
                    ins = dve.tensor_tensor(Ql[npar][dd, 4 * g + r:4 * g + 4:2, :], qf[rr, 2 * g:2 * g + 2, :],
                                            Qh[npar][rr, 4 * g + r:4 * g + 4:2, :].bitcast(F32), ALU.subtract)
            ins.then_inc(qlo2.sem, 1)

        def keys_low(u, par):
            npar = 1 - par
            dve.wait_ge(roped["K"].sem, roped["K"].at(u))
            dve.wait_ge(khi2.sem, khi2.at(u))
            dve.tensor_tensor(Kst[npar][64:128, 0, 0:C], kf[0:64, 0:C], Kst[npar][0:64, 0, 0:C].bitcast(F32), ALU.subtract)
            dve.tensor_tensor(Kst[npar][0:64, 1, 0:C], kf[64:128, 0:C], Kst[npar][64:128, 1, 0:C].bitcast(F32),
                              ALU.subtract).then_inc(done["K"].sem, 1)

        def evacuate(u, j, par, m):
            k, i, bank = order[m]
            src = aux[bank]
            npar = 1 - par
            if k == "Q" and n == 0:
                dve.wait_ge(aux_mm["Q"].sem, aux_mm["Q"].at(u))
                q4 = src[:, 0:4 * T].rearrange("p (t q) -> p t q", t=4)
                for s, (dst, bias) in enumerate(((qpf, W["pb"]), (qcf, W["cb"]))):
                    dve.wait_ge(qhi.sem, qhi.at(u - 1, s))
                    dve.wait_ge(qlo.sem, qlo.at(u - 1, s))
                    bb = bias[:, 4 * npar:4 * npar + 4, None].to_broadcast([P, 4, T])
                    dve.scalar_tensor_tensor(dst[:, :, :], q4, 0.125, bb, ALU.mult, ALU.add).then_inc(qf_done.sem, 1)
                dve.tensor_copy(e0[npar][:, :], src[0:T, 4 * T:4 * T + UH]).then_inc(segd.sem, 1)
                dve.wait_ge(segd.sem, segd.at(u))
                dve.tensor_tensor(de[npar][:, :], src[0:T, 4 * T + UH:4 * T + 2 * UH], e0[npar][:, :], ALU.subtract)\
                   .then_inc(done["Q"].sem, 1)
            if k == "G":
                dve.wait_ge(aux_mm["G"].sem, aux_mm["G"].at(u, i))
                if i % 4 == 0:
                    dve.wait_ge(g_out[i // 4].sem, g_out[i // 4].at(u - 1))
                if i == 0:
                    dve.wait_ge(done["Q"].sem, done["Q"].at(u))
                dve.scalar_tensor_tensor(Gs[i // 4][:, i % 4, :], W["segm"][:, :], de[npar][:, i:i + 1], src[0:T, 0:NR],
                                         ALU.mult, ALU.add).then_inc(done["G"].sem, 1)
            if k == "K" and n == 0:
                dve.wait_ge(khi_done.sem, khi_done.at(u, i))
                dve.tensor_tensor(Kst[npar][64:128, 2 * i, :], src[0:64, 0:CE], Kst[npar][0:64, 2 * i, :].bitcast(F32), ALU.subtract)
                dve.tensor_tensor(Kst[npar][0:64, 2 * i + 1, :], src[64:128, 0:CE],
                                  Kst[npar][64:128, 2 * i + 1, :].bitcast(F32), ALU.subtract).then_inc(done["K"].sem, 1)
            if k == "K" and n == 3:
                dve.wait_ge(khi3.sem, khi3.at(u, i))
                dve.scalar_tensor_tensor(Kst[npar][:, i, 0:C], khi[:, i, :].bitcast(F32), W["neg"][:, 0:1], src[:, 0:C],
                                         ALU.mult, ALU.add).then_inc(done["K"].sem, 1)
            if k == "Q" and n == 3:
                dve.wait_ge(qhi3.sem, qhi3.at(u))
                dve.scalar_tensor_tensor(Ql[npar][:, :, :], src[:, 0:2 * T].rearrange("p (t q) -> p t q", t=2), 0.25,
                                         Qh[npar][:, :, :].bitcast(F32), ALU.mult, ALU.subtract).then_inc(done["Q"].sem, 1)
            if k in "QK" and n in (1, 2):
                dve.wait_ge(aux_mm[k].sem, aux_mm[k].at(u))
                rope(u, par, k, m)
            if k == "W":
                dve.wait_ge(aux_mm["W"].sem, aux_mm["W"].at(u))
                if par == 0:
                    dve.wait_ge(batch_sem["res_in"], 16 * (j - 1) + 16)
                    dve.tensor_tensor(Yacc[:, :], src[0:T, 0:H], xres[:, :], ALU.add).then_inc(done["W"].sem, 1)
                else:
                    dve.wait_ge(done["W"].sem, done["W"].at(u - 1))
                    dve.wait_ge(batch_sem["y_out"], 16 * (j - 1))
                    dve.tensor_tensor(Yout[:, :], src[0:T, 0:H], Yacc[:, :], ALU.add).then_inc(done["W"].sem, 1)

        def score(u, j, par, i):
            dve.wait_ge(ac_mm.sem, ac_mm.at(u, i))
            if i == 0:
                dve.wait_ge(biased.sem, biased.at(u - 1))
                if n != 0:
                    dve.wait_ge(pt_mm.sem, pt_mm.at(u - 1))
                if n == 2:
                    dve.wait_ge(m_in[par], 16 * j + 16)
            if n == 0 and i % 4 == 0:
                dve.wait_ge(b_add[i // 4].sem, b_add[i // 4].at(u - 1))
            dst, m = S[par][:, i, 0:L.keys], mx[par][:, i:i + 1]
            src = ac[i % 2][0:T, 0:L.keys]
            if n == 3:
                dve.tensor_scalar(dst, src, 1.0, None, ALU.mult, ALU.max, accum_out=m).then_inc(scored.sem, 1)
                return
            add = {0: dst, 1: W["mask"][:, :] if n == 1 else None, 2: mask[par][:, :] if n == 2 else None}[n]
            dve.sem_inc(gate, 1)
            dve.tensor_tensor_reduce(out=dst, in0=src, in1=add, scale=1.0, scalar=-3.0e38, op0=ALU.add, op1=ALU.max,
                                     accum_out=m).then_inc(scored.sem, 1)

        def exp_bias(u, par):
            dve.wait_ge(scored.sem, scored.at(u))
            dve.wait_ge(probs.sem, probs.at(u - 1))
            if n == 0:
                dve.tensor_tensor(mtot[:, :], mx[par][:, :], e0[par][:, :], ALU.add).then_inc(maxed.sem, 1)
                dve.wait_ge(maxed.sem, maxed.at(u))
                dve.tensor_tensor(nb[par][:, :], e0[par][:, :], mtot[:, :], ALU.subtract).then_inc(biased.sem, 1)
            else:
                dve.tensor_scalar(nb[par][:, :], mx[par][:, :], -1.0, None, ALU.mult).then_inc(biased.sem, 1)

        def move_even(u, i):
            dve.wait_ge(pt_mm.sem, pt_mm.at(u, i))
            dve.wait_ge(pv_mm.sem, pv_mm.at(u, i - 2) if i >= 2 else pv_mm.at(u - 1, UH - 2 + i))
            for a, b, c in pieces:
                ins = dve.tensor_copy(PT[i % 2][0:a, b:c], ptb[i % 2][0:a, b:c])
            ins.then_inc(pt_even.sem, 1)

        def normalise(u, par):
            dve.wait_ge(probs.sem, probs.at(u))
            dve.wait_ge(normed.sem, normed.at(u - 1))
            dve.reciprocal(rec[:, :], sums[1 - par][:, :]).then_inc(recd.sem, 1)
            dve.wait_ge(pv_mm.sem, pv_mm.at(u))
            dve.wait_ge(recd.sem, recd.at(u))
            if runs(W_O, u):
                dve.wait_ge(aux_mm["T"].sem, aux_mm["T"].at(u))
            heads8 = lambda ap: ap.rearrange("p (h d) -> p h d", h=UH)
            dve.tensor_tensor(heads8(On[:, :]), heads8(ob[0:T, 0:UH * L.d]), rec[:, :, None].to_broadcast([T, UH, L.d]),
                              ALU.mult).then_inc(normed.sem, 1)

        pieces = [(CT, 0, NCT * T)] if n != 1 else [(T, 0, T), (32, T, 2 * T)]
        dve.memset(PT[0][:, :], 0.0)
        for p in range(2):
            dve.memset(S[p][:, :, :], 0.0)
            dve.memset(V[p][:, :, :, :], 0.0)
        if n == 0:
            dve.memset(clo[:, :, :].bitcast(F32), 0.0)
            dve.memset(chi[:, :, :].bitcast(F32), 0.0)
            dve.memset(craw[:, :, :], 0.0)
        if n >= 2:
            dve.memset(cK[:, :, :], 0.0)
            dve.memset(cV[:, :, :], 0.0)
            for p in range(2):
                dve.memset(Kst[p][:, :, :].bitcast(F32), 0.0)
        if n == 1:
            for p in range(2):
                dve.tensor_copy(Kn[p][:, :, T + 16:T + 32], W["perk"][:, 4 * p:4 * p + 4, :])
        dve.drain().then_inc(setup, 1)

        def evacuate_part(u, j, par, i, part):
            for m in uses[i, part] + (uses[i, 0] if part else []):
                k = order[m][0]
                late = n == 0 and k == "K"
                if runs(AUX_WINDOW[k], u) and late == (m not in uses[i, part]):
                    evacuate(u, j, par, m)

        def step(u, j, par):
            for i in range(UH):
                if runs(W_A, u):
                    score(u, j, par, i)
                evacuate_part(u, j, par, i, 0)
                if runs(W_W, u):
                    if i % 2 == 0:
                        move_even(u, i)
                evacuate_part(u, j, par, i, 1)
                if n in (1, 2) and runs(W_N, u):
                    for k in "QK":
                        if L.at[f"{k}_sum"] == i:
                            rope_sum(u, j, par, k)
                    if L.at.get("Q_lo") == i:
                        queries_low(u, par)
                    if L.at.get("K_lo") == i:
                        keys_low(u, par)
            if runs(W_A, u):
                exp_bias(u, par)
            if runs(W_W, u):
                normalise(u, par)

        loop(dve, step)

    @block.scalar
    def _(act):
        def softmax(u, par, i):
            wpar = 1 - par
            if i == 0:
                act.wait_ge(biased.sem, biased.at(u - 1))
                act.wait_ge(recd.sem, recd.at(u - 2))
            s = S[wpar][:, i, 0:L.keys]
            act.activation(s, s, ACT.Exp, bias=nb[wpar][:, i:i + 1], scale=1.0,
                           accum_out=sums[wpar][:, i:i + 1]).then_inc(probs.sem, 1)

        def evacuate(u, j, par, m):
            k, i, bank = order[m]
            src = aux[bank]
            npar = 1 - par
            if k == "K" and n == 0:
                act.wait_ge(aux_mm["K"].sem, aux_mm["K"].at(u, i))
                if i == 0:
                    act.wait_ge(ac_mm.sem, ac_mm.at(u - 1))
                act.copy(Kst[npar][0:64, 2 * i, :], src[0:64, 0:CE])
                act.copy(Kst[npar][64:128, 2 * i + 1, :], src[64:128, 0:CE]).then_inc(khi_done.sem, 1)
            if k == "K" and n == 3:
                act.wait_ge(aux_mm["K"].sem, aux_mm["K"].at(u, i))
                act.wait_ge(done["K"].sem, done["K"].at(u - 1, i))
                if i == 0:
                    act.wait_ge(ac_mm.sem, ac_mm.at(u - 1))
                act.copy(khi[:, i, :], src[:, 0:C]).then_inc(khi3.sem, 1)
            if k == "Q" and n == 3:
                act.wait_ge(aux_mm["Q"].sem, aux_mm["Q"].at(u))
                act.wait_ge(ac_mm.sem, ac_mm.at(u - 1))
                act.activation(Qh[npar][:, :, :], src[:, 0:2 * T].rearrange("p (t q) -> p t q", t=2), ACT.Copy, scale=0.25)\
                   .then_inc(qhi3.sem, 1)
            if k in "QK" and n in (1, 2):
                act.wait_ge(cosd[k].sem, cosd[k].at(u))
                act.wait_ge(roped[k].sem, roped[k].at(u - 1))
                for r in range(4):
                    o = 32 * (r ^ 1)
                    if n == 1 or k == "Q":
                        dst = (qsw if k == "Q" else ksw)[32 * r:32 * r + 32, :, :]
                        sv = src[o:o + 32, 0:4 * T].rearrange("p (t q) -> p t q", t=4)
                    else:
                        dst, sv = ksw[32 * r:32 * r + 32, :], src[o:o + 32, 0:C]
                    ins = act.copy(dst, sv)
                ins.then_inc(swp[k].sem, 1)
            if k == "V":
                act.wait_ge(aux_mm["V"].sem, aux_mm["V"].at(u, i))
                if i == 0:
                    act.wait_ge(pv_mm.sem, pv_mm.at(u - 1))
                if n == 0:
                    dst = V[par][:, i, :, :]
                    sv = src[0:CT, :].rearrange("p (h d) -> p h d", h=UH)
                elif n == 1:
                    dst = V[par][0:T, 0, :, :]
                    sv = src[0:T, :].rearrange("p (h d) -> p h d", h=UH)
                if n < 2:
                    act.copy(dst, sv).then_inc(done["V"].sem, 1)
                elif n == 2:
                    for kv in range(2):
                        sv = src[0:CT, 0:NCT * P].rearrange("p (t h d) -> p t h d", t=NCT, h=2)[:, :, kv, :]
                        ins = act.copy(V[par][:, :, kv, 0:L.d], sv)
                    ins.then_inc(done["V"].sem, 1)
                else:
                    for t in range(NCT):
                        sv = src[0:CT, t * P:(t + 1) * P].rearrange("p (h d) -> p h d", h=UH)
                        ins = act.copy(V[par][:, t, :, 0:L.d], sv)
                    ins.then_inc(done["V"].sem, 1)
            if k == "T":
                act.wait_ge(aux_mm["T"].sem, aux_mm["T"].at(u))
                act.wait_ge(aux_mm["W"].sem, aux_mm["W"].at(u - 1))
                act.copy(OTs[:, :], src[:, 0:L.ot * T]).then_inc(done["T"].sem, 1)

        def queries_own(u):
            for s, (full, own) in enumerate(((qpf, qpo), (qcf, qco))):
                act.wait_ge(qf_done.sem, qf_done.at(u, s))
                act.wait_ge(qlo.sem, qlo.at(u - 1, s))
                act.copy(own[:, :, :], full[:, :, :]).then_inc(qown.sem, 1)

        def queries_twice(u, par, s):
            full, hi = ((qpf, Qp), (qcf, Qc[1 - par]))[s]
            act.wait_ge(qf_done.sem, qf_done.at(u, s))
            if s == 0:
                act.wait_ge(aux_mm["G"].sem, aux_mm["G"].at(u - 1))
            else:
                act.wait_ge(ac_mm.sem, ac_mm.at(u - 1))
            for r in range(2):
                for d in range(2):
                    ins = act.copy(hi[64 * d:64 * d + 64, r:UH:2, :], full[64 * r:64 * r + 64, :, :])
            ins.then_inc(qhi.sem, 1)

        def queries_high(u, par):
            act.wait_ge(roped["Q"].sem, roped["Q"].at(u))
            act.wait_ge(ac_mm.sem, ac_mm.at(u - 1))
            for r in range(2):
                for d in range(2):
                    ins = act.copy(Qh[1 - par][64 * d:64 * d + 64, r:UH:2, :], qf[64 * r:64 * r + 64, :, :])
            ins.then_inc(qhi2.sem, 1)

        def keys_high(u, par):
            act.wait_ge(roped["K"].sem, roped["K"].at(u))
            act.wait_ge(ac_mm.sem, ac_mm.at(u - 1))
            act.copy(Kst[1 - par][0:64, 0, 0:C], kf[0:64, 0:C])
            act.copy(Kst[1 - par][64:128, 1, 0:C], kf[64:128, 0:C]).then_inc(khi2.sem, 1)

        def split(j):
            act.wait_ge(batch_sem["ctxK_in"], 16 * (j + 1) + 16)
            act.copy(chi[:, :, 0:CE], craw[:, :, 0:CE]).then_inc(split_hi, 1)

        def move_odd(u, i):
            act.wait_ge(pt_mm.sem, pt_mm.at(u, i))
            act.wait_ge(pv_mm.sem, pv_mm.at(u, i - 2) if i >= 2 else pv_mm.at(u - 1, UH - 2 + i))
            for a, b, c in ([(CT, 0, NCT * T)] if n != 1 else [(T, 0, T), (32, T, 2 * T)]):
                ins = act.copy(PT[i % 2][0:a, b:c], ptb[i % 2][0:a, b:c])
            ins.then_inc(pt_odd.sem, 1)

        def evacuate_part(u, j, par, i, part):
            for m in uses[i, part]:
                if runs(AUX_WINDOW[order[m][0]], u):
                    evacuate(u, j, par, m)

        def step(u, j, par):
            if starts(u):
                act.wait_ge(setup, 1)
                if n == 0:
                    split(-1)
            if runs(W_W, u):
                softmax(u, par, 0)
            for i in range(UH):
                if runs(W_W, u) and i + 1 < UH:
                    softmax(u, par, i + 1)
                if n == 0 and i == 3 and par == 1 and runs((0, UNITS - 3), u):
                    act.wait_ge(aux_mm["V"].sem, aux_mm["V"].at(u))
                    split(j)
                evacuate_part(u, j, par, i, 0)
                if runs(W_W, u) and i % 2 == 1:
                    move_odd(u, i)
                evacuate_part(u, j, par, i, 1)
                if runs(W_N, u):
                    if L.at.get("Q_own") == i:
                        queries_own(u)
                    for s, stage in enumerate(("Q_position", "Q_content")):
                        if L.at.get(stage) == i:
                            queries_twice(u, par, s)
                    if L.at.get("Q_hi") == i:
                        queries_high(u, par)
                    if L.at.get("K_hi") == i:
                        keys_high(u, par)

        loop(act, step)

    @block.gpsimd
    def _(pool):
        def add_mask(u, par, g):
            pool.wait_ge(b_in[g].sem, b_in[g].at(u))
            s = S[1 - par][:, 4 * g:4 * g + 4, 0:C]
            pool.tensor_tensor(s, s, W["cmask"][:, None, :].to_broadcast([T, 4, C]), ALU.add).then_inc(b_add[g].sem, 1)

        def step(u, j, par):
            if n == 0:
                if starts(u):
                    pool.wait_ge(setup, 1)
                if runs(W_N, u):
                    for s, (full, own, lo) in enumerate(((qpf, qpo, Lp), (qcf, qco, Lc[1 - par]))):
                        pool.wait_ge(qown.sem, qown.at(u, s))
                        if s == 0:
                            pool.wait_ge(aux_mm["G"].sem, aux_mm["G"].at(u - 1))
                        else:
                            pool.wait_ge(ac_mm.sem, ac_mm.at(u - 1))
                        pool.tensor_tensor(lo[:, :, :], full[:, :, :], own[:, :, :].bitcast(F32), ALU.subtract).then_inc(qlo.sem, 1)
                if runs((0, UNITS - 1), u):
                    add_mask(u - 1, 1 - par, 1)
                if starts(u) or (par == 1 and runs((0, UNITS - 3), u)):
                    pool.wait_ge(split_hi, j + 2)
                    pool.tensor_tensor(clo[:, :, 0:CE], craw[:, :, 0:CE], chi[:, :, 0:CE].bitcast(F32), ALU.subtract)\
                        .then_inc(split_lo, 1)
                if runs(W_N, u):
                    add_mask(u, par, 0)
            if n in (1, 2) and runs(W_N, u):
                if starts(u):
                    pool.wait_ge(setup, 1)
                for k in "QK":
                    pool.wait_ge(swp[k].sem, swp[k].at(u))
                    sin = W["sinq" if k == "Q" else "sink"]
                    if n == 1 or k == "Q":
                        t = (qsw if k == "Q" else ksw)[:, :, :]
                        sv = sin[:, None, 0:T].to_broadcast([P, 4, T])
                    else:
                        t, sv = ksw[:, :], sin[:, 0:C]
                    pool.tensor_tensor(t, t, sv, ALU.mult).then_inc(sind[k].sem, 1)

        if n != 3:
            loop(pool, step)

    @block.sync
    def _(sp):
        def load_ctx(dst, src, s):
            sp.dma_start(dst[:, :, 0:io["ctx_cols"]], src).then_inc(s, 16)

        ctx_src = lambda b: row(io["ctxT"], b).rearrange("(k p) c -> p k c", k=KT)
        xT_src = lambda b: row(io["xT"], b).rearrange("(k p) q -> p k q", k=KT)

        def step(u, j, par):
            npar = 1 - par
            if starts(u):
                sp.dma_start(xT[:, :, :], xT_src(0)).then_inc(batch_sem["xT_in"], 16)
                sp.wait_ge(setup, 1)
                if n == 1:
                    for p in range(2):
                        sp.dma_start(Vx[p][16:32, :, 0:L.d], io["perv"][:, UH * p:UH * p + UH, :]).then_inc(extras, 16)
                    sp.dma_start(xTv[:, :, :], xT_src(0)).then_inc(batch_sem["ctxV_in"], 16)
                if n == 0:
                    load_ctx(craw, ctx_src(0), batch_sem["ctxK_in"])
                if n >= 2:
                    load_ctx(cK, ctx_src(0), batch_sem["ctxK_in"])
                    load_ctx(cV, ctx_src(0), batch_sem["ctxV_in"])
            if n == 2 and runs(W_N, u):
                src = row(io["mask"], batch_of(j, par, 1))
                sp.wait_ge(scored.sem, scored.at(u - 1))
                sp.dma_start(mask[npar][:, :], src).then_inc(m_in[npar], 16)
            if n == 1 and runs(W_A, u):
                src = row(io["memv"], j)[par * 512:par * 512 + 512].rearrange("(o h d) -> o h d", o=1, h=UH).to_broadcast([16, UH, L.d])
                sp.wait_ge(pv_mm.sem, pv_mm.at(u - 1))
                sp.dma_start(Vx[par][0:16, :, 0:L.d], src).then_inc(vx_in[par], 16)
            if par == 1 and runs((0, UNITS - 1), u):
                src = row(io["res"], j)
                sp.wait_ge(done["W"].sem, done["W"].at(u - 1))
                sp.dma_start(xres[:, :], src).then_inc(batch_sem["res_in"], 16)
            if par == 0 and runs((0, UNITS - 4), u):
                ctx_next, xT_next = ctx_src(j + 1) if n != 1 else None, xT_src(j + 1)
                last = aux_mm["K"] if n == 1 else aux_mm["Q"]
                sp.wait_ge(last.sem, last.at(u))
                sp.dma_start(xT[:, :, :], xT_next).then_inc(batch_sem["xT_in"], 16)
                if n == 0:
                    sp.wait_ge(split_lo, j + 1)
                    load_ctx(craw, ctx_next, batch_sem["ctxK_in"])
                if n >= 2:
                    sp.wait_ge(aux_mm["K"].sem, aux_mm["K"].at(u))
                    load_ctx(cK, ctx_next, batch_sem["ctxK_in"])
            if par == 1 and n >= 1 and runs((0, UNITS - 3), u):
                src = xT_src(j + 1) if n == 1 else ctx_src(j + 1)
                sp.wait_ge(aux_mm["V"].sem, aux_mm["V"].at(u))
                if n == 1:
                    sp.dma_start(xTv[:, :, :], src).then_inc(batch_sem["ctxV_in"], 16)
                else:
                    load_ctx(cV, src, batch_sem["ctxV_in"])
            if par == 1 and runs(W_O, u):
                dst = row(io["y"], j - 1)
                sp.wait_ge(done["W"].sem, done["W"].at(u))
                sp.dma_start(dst, Yout[:, :]).then_inc(batch_sem["y_out"], 16)
            if n == 0 and runs(W_N, u):
                for g in range(2):
                    sp.wait_ge(b_in[g].sem, b_in[g].at(u - 1))
                    sp.sem_inc(sp_gate, 1)
                    sp.wait_ge(done["G"].sem, done["G"].at(u, 4 * g + 3))
                    sp.dma_start(io["gscr"][g], Gs[g][:, :, :]).then_inc(g_out[g].sem, 16)
                    sp.wait_ge(g_out[g].sem, g_out[g].at(u))
                    if runs(W_W, u):
                        sp.sem_inc(sp_gate, 1)
                        sp.wait_ge(pt_mm.sem, pt_mm.at(u, 4 * g + 3))
                    skew = bass.AP(tensor=io["gscr"][g].tensor, offset=io["gscr"][g].offset + T - 1,
                                   ap=[[4 * NR - 1, T], [NR, 4], [1, C]])
                    sp.dma_start(S[npar][:, 4 * g:4 * g + 4, 0:C], skew).then_inc(b_in[g].sem, 16)

        loop(sp, step)
        sp.wait_ge(batch_sem["y_out"], 16 * B)



def context_pass(nc, ctx, ident, io):
    def sb(name, shape, dt=F32):
        return ctx.enter_context(nc.sbuf_tensor(f"c_{name}", shape, dt))

    EVERY = (0, B - 1)
    FULL = 2

    def sig(name, per, by=1):
        return Signal(nc, f"c_{name}", EVERY, per, FULL, by)

    X = [sb(f"ctx{p}", [CT, NCT, H]) for p in range(2)]
    bn = sb("bn", [CT, NCT, 6])
    mv = sb("mv", [CT, NCT, 2])
    ms, ms2, sd, rs = (sb(k, [CT, NCT]) for k in ("ms", "ms2", "sd", "rs"))
    XT = [sb(f"ctxT{p}", [P, KT, CP]) for p in range(2)]
    means = sb("means", [P, KT, B])
    eps, ones = sb("eps", [P, 1]), sb("ones", [CT, 2])
    ps = [ctx.enter_context(nc.psum_tensor(f"c_ps{k}", [P, 512], F32)) for k in range(6)]
    setup = nc.alloc_semaphore("c_setup")
    loaded = [nc.alloc_semaphore(f"c_in{p}") for p in range(2)]
    stored = [nc.alloc_semaphore(f"c_out{p}") for p in range(2)]
    gate = nc.alloc_semaphore("c_gate")
    m_out = nc.alloc_semaphore("c_means_out")
    summed, stats, mean2, meansq = sig("summed", 1), sig("stats", 1), sig("mean2", 1), sig("meansq", 1)
    aggr, rooted, inv = sig("aggr", 1), sig("rooted", 1), sig("inv", 1)
    scaled, turned, moved, mcopied = sig("scaled", 1), sig("turned", KT), sig("moved", KT), sig("mcopied", 1)
    block = ctx.enter_context(nc.Block())

    def loop(e, step):
        for b in range(FULL):
            step(b, b // 2, b % 2)
        with e.Fori(FULL // 2, B // 2) as j:
            step(2 * j, j, 0)
            step(2 * j + 1, j, 1)

    @block.sync
    def _(sp):
        sp.wait_ge(setup, 1)

        def load(b, j, p):
            src = row(io["ctx"], b)
            sp.wait_ge(turned.sem, turned.at(b - 2))
            sp.dma_start(X[p][:, 0:2, :], src[0:2 * CT, :].rearrange("(t p) h -> p t h", t=2)).then_inc(loaded[p], 16)
            sp.dma_start(X[p][0:C - 2 * CT, 2, :], src[2 * CT:C, :]).then_inc(loaded[p], 16)

        for b in range(FULL):
            load(b, b // 2, b % 2)
        with sp.Fori(FULL // 2, B // 2) as j:
            load(2 * j, j, 0)
            load(2 * j + 1, j, 1)
        sp.wait_ge(mcopied.sem, B)
        sp.dma_start(io["means"].rearrange("k p b -> p k b"), means[:, :, :]).then_inc(m_out, 16)
        for s in stored:
            sp.wait_ge(s, 16 * (B // 2))
        sp.wait_ge(m_out, 16)

    @block.vector
    def _(dve):
        for p in range(2):
            dve.memset(X[p][:, :, :], 0.0)
        dve.memset(eps[:, :], 1e-6)
        dve.memset(ones[:, :], 1.0 / C)
        dve.drain().then_inc(setup, 1)

        def step(b, j, p):
            dve.wait_ge(loaded[p], 32 * j + 32)
            for t in range(NCT):
                ins = dve.bn_stats(bn[:, t, :], X[p][:, t, :])
            ins.then_inc(stats.sem, 1)
            dve.wait_ge(stats.sem, stats.at(b))
            dve.sem_inc(gate, 1)
            for t in range(NCT):
                ins = dve.bn_aggr(mv[:, t, :], bn[:, t, :])
            ins.then_inc(aggr.sem, 1)
            dve.wait_ge(aggr.sem, aggr.at(b))
            dve.tensor_tensor(ms2[:, :], mv[:, :, 0], mv[:, :, 0], ALU.mult).then_inc(mean2.sem, 1)
            dve.wait_ge(mean2.sem, mean2.at(b))
            dve.wait_ge(rooted.sem, rooted.at(b - 1))
            dve.tensor_tensor(ms[:, :], ms2[:, :], mv[:, :, 1], ALU.add).then_inc(meansq.sem, 1)
            dve.wait_ge(rooted.sem, rooted.at(b))
            dve.reciprocal(rs[:, :], sd[:, :]).then_inc(inv.sem, 1)
            dve.wait_ge(inv.sem, inv.at(b))
            dve.wait_ge(summed.sem, summed.at(b))
            for t in range(NCT):
                ins = dve.tensor_scalar(X[p][:, t, :], X[p][:, t, :], rs[:, t:t + 1], None, ALU.mult)
            ins.then_inc(scaled.sem, 1)
            dve.wait_ge(turned.sem, turned.at(b, 0))
            if not isinstance(b, int) or b >= 2:
                dve.wait_ge(stored[p], 16 * j)
            dve.tensor_copy(XT[p][:, 0, :], ps[2 * p][:, 0:CP]).then_inc(moved.sem, 1)
            at = slice(b, b + 1) if isinstance(b, int) else bass.ds(b, 1)
            dve.tensor_copy(means[:, :, at].rearrange("p k a -> p (k a)"), ps[4][:, 0:2 * KT:2]).then_inc(mcopied.sem, 1)

        loop(dve, step)

    @block.scalar
    def _(act):
        act.wait_ge(setup, 1)

        def step(b, j, p):
            dst = row(io["ctxnT"], b).rearrange("(k p) c -> p k c", k=KT)
            act.wait_ge(meansq.sem, meansq.at(b))
            act.wait_ge(inv.sem, inv.at(b - 1))
            act.activation(sd[:, :], ms[:, :], ACT.Sqrt, bias=eps[0:CT, 0:1]).then_inc(rooted.sem, 1)
            act.wait_ge(moved.sem, moved.at(b, 0))
            act.wait_ge(turned.sem, turned.at(b, 1))
            if not isinstance(b, int) or b >= 2:
                act.wait_ge(stored[p], 16 * j)
            act.copy(XT[p][:, 1, :], ps[2 * p + 1][:, 0:CP]).then_inc(moved.sem, 1)
            act.wait_ge(moved.sem, moved.at(b))
            act.dma_start(dst, XT[p][:, :, :]).then_inc(stored[p], 16)

        loop(act, step)

    @block.tensor
    def _(pe):
        pe.wait_ge(setup, 1)

        def step(b, j, p):
            pe.wait_ge(loaded[p], 32 * j + 32)
            pe.wait_ge(mcopied.sem, mcopied.at(b - 1))
            for k in range(KT):
                for t in range(NCT):
                    mm = pe.matmul(ps[4][:, 2 * k:2 * k + 2], X[p][:, t, k * P:(k + 1) * P], ones[:, :], start=(t == 0), stop=(t == NCT - 1))
            mm.then_inc(summed.sem, 1)
            pe.wait_ge(scaled.sem, scaled.at(b))
            pe.wait_ge(moved.sem, moved.at(b - 2))
            for k in range(KT):
                for t in range(NCT):
                    mm = pe.transpose(ps[2 * p + k][:, t * CT:(t + 1) * CT], X[p][:, t, k * P:(k + 1) * P], ident[0:CT, 0:CT])
                mm.then_inc(turned.sem, 1)

        loop(pe, step)


GB = 4
NG = B // GB
GT = GB * T
F_PRE, F_MID, F_POST = (-1, NG - 2), (0, NG - 1), (1, NG)
F_FULL = 2


NORM_AT = {0: {"post": 1, "pre": 4, "next": 7}, 1: {"next": 4, "pre": 5}, 2: {"next": 5, "pre": 7}}


def feed_forward(nc, ctx, n, ident, W, io, eps_pre, eps_post, eps_next, ftiles):
    gated = n != 0
    NF = len(ftiles)

    def sb(name, shape, dt=F32):
        return ctx.enter_context(nc.sbuf_tensor(f"f{n}_{name}", shape, dt))

    def sig(name, window, per, by=1):
        return Signal(nc, f"f{n}_{name}", window, per, F_FULL, by)

    Yin = [sb(f"y{p}", [T, GB, H]) for p in range(2)]
    Xn = sb("norm", [T, GB, H])
    Xs = sb("affine", [T, GB, H])
    XT = [sb(f"xT_{k}", [P, KT, GT], F32R) for k in ("hi", "lo")]
    R = [sb(f"resid{p}", [T, GB, H]) for p in range(2)]
    Z = [sb(f"z{p}", [T, GB, H]) for p in range(2)]
    Zn, Zs = sb("znorm", [T, GB, H]), sb("zaffine", [T, GB, H])
    Zx = sb("znext", [T, GB, H])
    Zg = sb("zgain", [T, GB, H])
    ZT = sb("zT", [P, KT, GT])
    hf = [sb(f"hidden{p}", [P, GT]) for p in range(2)]
    sg = [sb(f"silu{p}", [P, GT]) for p in range(2)]
    Hh, Hl = sb("h_hi", [P, NF, GT], F32R), sb("h_lo", [P, NF, GT], F32R)
    st = {k: {"bn": sb(f"{k}_bn", [T, GB, 6]), "mv": sb(f"{k}_mv", [T, GB, 2]), "m2": sb(f"{k}_m2", [T, GB]),
              "v": sb(f"{k}_v", [T, GB]), "sd": sb(f"{k}_sd", [T, GB]), "rs": sb(f"{k}_rs", [T, GB])} for k in ("pre", "post", "next")}
    epst = sb("eps", [P, 3])
    ps = [ctx.enter_context(nc.psum_tensor(f"f{n}_ps{k}", [P, 512], F32)) for k in range(8)]
    hb, fb, tb = ps[0:4], ps[4:6], ps[6:8]
    norm_at = NORM_AT[n]

    setup = nc.alloc_semaphore(f"f{n}_setup")
    gate, pool_gate, sp_gate = (nc.alloc_semaphore(f"f{n}_{k}") for k in ("gate", "pool_gate", "sp_gate"))
    y_in = [nc.alloc_semaphore(f"f{n}_y_in{p}") for p in range(2)]
    z_out = [sig("z_out", F_POST, 1, 16)]
    zt_out = [sig(f"zt_out{k}", F_POST, 1, 16) for k in range(KT)]
    norms = {"pre": F_PRE, "next": F_POST}
    if n == 0:
        norms["post"] = F_POST
    N = {k: {s: sig(f"{k}_{s}", w, 1) for s in ("bn", "mv", "m2", "v", "sd", "rs", "out", "g", "b")} for k, w in norms.items()}
    p_mm, p_hi, p_lo = sig("p_mm", F_PRE, KT), sig("p_hi", F_PRE, KT), sig("p_lo", F_PRE, KT)
    q_mm, q_done = sig("q_mm", F_POST, KT), sig("q_done", F_POST, KT)
    h_mm, h_act, h_val = sig("h_mm", F_MID, NF), sig("h_act", F_MID, NF), sig("h_val", F_MID, NF)
    h_hi, h_lo = sig("h_hi", F_MID, NF), sig("h_lo", F_MID, NF)
    o_mm, o_done = sig("o_mm", F_MID, GB), sig("o_done", F_MID, GB)
    resid, base, gbase = sig("resid", F_PRE, 1), sig("base", F_PRE, 1), sig("zg", F_POST, 1)
    zg2 = sig("zg2", F_POST, 1)
    block = ctx.enter_context(nc.Block())

    def loop(e, step):
        for s in range(-1, F_FULL):
            step(s, s // 2, s % 2)
        with e.Fori(F_FULL // 2, NG // 2 - 1) as j:
            step(2 * j, j, 0)
            step(2 * j + 1, j, 1)
        for s in range(NG - 2, NG + 1):
            step(s, s // 2, s % 2)

    def norms_here(f, s, root=False):
        return [k for k, at in norm_at.items() if f == (min(at + 1, NF) if root else at) and runs(norms[k], s)]

    wide = lambda ap: ap[:, None, :].to_broadcast([T, GB, H])
    pre_in = Xs if n == 0 else Xn

    @block.tensor
    def _(pe):
        def output(s, t):
            pe.wait_ge(o_done.sem, o_done.at(s, t - 2) if t >= 2 else o_done.at(s - 1, GB - 2 + t))
            for f, (f0, fn) in enumerate(ftiles):
                if t == 0:
                    pe.wait_ge(h_lo.sem, h_lo.at(s, f))
                for a, (hh, wi) in enumerate(((Hh, 0), (Hh, 1), (Hl, 0))):
                    mm = pe.matmul(fb[t % 2][0:T, 0:H], hh[0:fn, f, t * T:(t + 1) * T], W["w2"][wi][0:fn, f, :],
                                   start=(f == 0 and a == 0), stop=(f == NF - 1 and a == 2))
            mm.then_inc(o_mm.sem, 1)

        def step(s, j, p):
            if isinstance(s, int) and s == -1:
                pe.wait_ge(setup, 1)
            if runs(F_MID, s):
                for f, (f0, fn) in enumerate(ftiles):
                    if f == 0:
                        pe.wait_ge(p_lo.sem, p_lo.at(s - 1))
                        pe.wait_ge(q_done.sem, q_done.at(s - 1))
                    banks = [hb[(2 * f) % 4], hb[(2 * f + 1) % 4]] if gated else [hb[f % 4]]
                    back = 2 if gated else 4
                    pe.wait_ge(h_val.sem, h_val.at(s, f - back) if f >= back else h_val.at(s - 1, NF - back + f))
                    for g, bank in enumerate(banks):
                        c0 = g * W["f"] + f0
                        for k in range(KT):
                            for a, (wi, xi) in enumerate(((0, 0), (0, 1), (1, 0))):
                                mm = pe.matmul(bank[0:fn, 0:GT], W["w1"][wi][:, k, c0:c0 + fn], XT[xi][:, k, :],
                                               start=(k == 0 and a == 0), stop=(k == KT - 1 and a == 2))
                    mm.then_inc(h_mm.sem, 1)
                output(s, 0)
                output(s, 1)
            if runs(F_POST, s):
                pe.wait_ge(N["next"]["out"].sem, N["next"]["out"].at(s))
                pe.wait_ge(h_val.sem, h_val.at(s))
                for k in range(KT):
                    for t in range(GB):
                        mm = pe.transpose(hb[k][:, t * T:(t + 1) * T], Zx[:, t, k * P:(k + 1) * P], ident[0:T, 0:T])
                    mm.then_inc(q_mm.sem, 1)
            if runs(F_PRE, s):
                last = N["pre"]["b"] if n == 0 else N["pre"]["out"]
                pe.wait_ge(last.sem, last.at(s))
                pe.wait_ge(p_lo.sem, p_lo.at(s - 1))
                for k in range(KT):
                    for t in range(GB):
                        mm = pe.transpose(tb[k][:, t * T:(t + 1) * T], pre_in[:, t, k * P:(k + 1) * P], ident[0:T, 0:T])
                    mm.then_inc(p_mm.sem, 1)
            if runs(F_MID, s):
                output(s, 2)
                output(s, 3)

        loop(pe, step)

    @block.vector
    def _(dve):
        for c, e in enumerate((eps_pre, eps_post, eps_next)):
            dve.memset(epst[:, c:c + 1], e)
        dve.drain().then_inc(setup, 1)

        def norm(s, k, src, dst, centred):
            a, g = st[k], N[k]
            for t in range(GB):
                ins = dve.bn_stats(a["bn"][:, t, :], src[:, t, :])
            ins.then_inc(g["bn"].sem, 1)
            dve.wait_ge(g["bn"].sem, g["bn"].at(s))
            dve.sem_inc(gate, 1)
            for t in range(GB):
                ins = dve.bn_aggr(a["mv"][:, t, :], a["bn"][:, t, :])
            ins.then_inc(g["mv"].sem, 1)
            dve.wait_ge(g["mv"].sem, g["mv"].at(s))
            dve.tensor_tensor(a["m2"][:, :], a["mv"][:, :, 0], a["mv"][:, :, 0], ALU.mult).then_inc(g["m2"].sem, 1)
            dve.wait_ge(g["m2"].sem, g["m2"].at(s))
            if centred:
                dve.tensor_copy(a["v"][:, :], a["mv"][:, :, 1]).then_inc(g["v"].sem, 1)
            else:
                dve.tensor_tensor(a["v"][:, :], a["m2"][:, :], a["mv"][:, :, 1], ALU.add).then_inc(g["v"].sem, 1)
            dve.wait_ge(g["sd"].sem, g["sd"].at(s))
            dve.reciprocal(a["rs"][:, :], a["sd"][:, :]).then_inc(g["rs"].sem, 1)
            dve.wait_ge(g["rs"].sem, g["rs"].at(s))
            for t in range(GB):
                if centred:
                    ins = dve.tensor_scalar(dst[:, t, :], src[:, t, :], a["mv"][:, t, 0:1], a["rs"][:, t:t + 1], ALU.subtract, ALU.mult)
                else:
                    ins = dve.tensor_scalar(dst[:, t, :], src[:, t, :], a["rs"][:, t:t + 1], None, ALU.mult)
            ins.then_inc(g["out"].sem, 1)

        def hidden(s, f):
            f0, fn = ftiles[f]
            dve.wait_ge(h_act.sem, h_act.at(s, f))
            if gated:
                dve.wait_ge(h_mm.sem, h_mm.at(s, f))
                dve.wait_ge(h_hi.sem, h_hi.at(s, f - 2) if f >= 2 else h_hi.at(s - 1, NF - 2 + f))
                dve.wait_ge(h_lo.sem, h_lo.at(s, f - 2) if f >= 2 else h_lo.at(s - 1, NF - 2 + f))
                dve.scalar_tensor_tensor(hf[f % 2][0:fn, :], hb[(2 * f) % 4][0:fn, 0:GT], W["b1"][0:fn, f:f + 1],
                                         sg[f % 2][0:fn, :], ALU.add, ALU.mult).then_inc(h_val.sem, 1)
                dve.wait_ge(h_val.sem, h_val.at(s, f))
            if f == 0:
                dve.wait_ge(o_mm.sem, o_mm.at(s - 1))
            dve.tensor_copy(Hh[0:fn, f, :], hf[f % 2][0:fn, :]).then_inc(h_hi.sem, 1)
            dve.wait_ge(h_hi.sem, h_hi.at(s, f))
            dve.tensor_tensor(Hl[0:fn, f, :], hf[f % 2][0:fn, :], Hh[0:fn, f, :].bitcast(F32), ALU.subtract).then_inc(h_lo.sem, 1)

        def one_norm(s, j, p, k):
            if k == "pre":
                dve.wait_ge(y_in[1 - p], 16 * (j + 1 + p))
                if n == 0:
                    dve.wait_ge(N["pre"]["g"].sem, N["pre"]["g"].at(s - 1))
                else:
                    dve.wait_ge(p_mm.sem, p_mm.at(s - 1))
                norm(s, "pre", Yin[1 - p], Xn, n == 0)
                return
            dve.wait_ge(o_done.sem, o_done.at(s - 1))
            if k == "post":
                dve.wait_ge(N["post"]["g"].sem, N["post"]["g"].at(s - 1))
                norm(s, "post", Z[1 - p], Zn, True)
                return
            if n == 0:
                dve.wait_ge(N["post"]["b"].sem, N["post"]["b"].at(s))
            dve.wait_ge(q_mm.sem, q_mm.at(s - 1))
            if n == 2:
                dve.wait_ge(gbase.sem, gbase.at(s - 1))
            norm(s, "next", Zs if n == 0 else Z[1 - p], Zx, False)

        def norm_after(s, j, p, f):
            for k in norms_here(f, s):
                one_norm(s, j, p, k)

        def output(s, p, t):
            dve.wait_ge(o_mm.sem, o_mm.at(s, t))
            if t == 0:
                dve.wait_ge(resid.sem, resid.at(s - 1))
                last = N["post" if n == 0 else "next"]["out"]
                dve.wait_ge(last.sem, last.at(s - 1))
                if n == 1:
                    dve.wait_ge(z_out[0].sem, z_out[0].at(s - 1))
            dve.tensor_tensor(Z[p][:, t, :], fb[t % 2][0:T, 0:H], R[p][:, t, :], ALU.add).then_inc(o_done.sem, 1)

        def step(s, j, p):
            for f in range(NF):
                if runs(F_MID, s):
                    hidden(s, f)
                norm_after(s, j, p, f)
            if runs(F_MID, s):
                output(s, p, 0)
            norm_after(s, j, p, NF)
            if runs(F_MID, s):
                output(s, p, 1)
            if runs(F_PRE, s):
                for k in range(KT):
                    dve.wait_ge(p_hi.sem, p_hi.at(s, k))
                    dve.tensor_tensor(XT[1][:, k, :], tb[k][:, 0:GT], XT[0][:, k, :].bitcast(F32), ALU.subtract).then_inc(p_lo.sem, 1)
            if runs(F_MID, s):
                output(s, p, 2)
                output(s, p, 3)

        loop(dve, step)

    @block.scalar
    def _(act):
        act.wait_ge(setup, 1)

        def root(s, k):
            c = ("pre", "post", "next").index(k)
            act.wait_ge(N[k]["v"].sem, N[k]["v"].at(s))
            act.wait_ge(N[k]["rs"].sem, N[k]["rs"].at(s - 1))
            act.activation(st[k]["sd"][:, :], st[k]["v"][:, :], ACT.Sqrt, bias=epst[0:T, c:c + 1]).then_inc(N[k]["sd"].sem, 1)

        def hidden(s, f):
            f0, fn = ftiles[f]
            act.wait_ge(h_mm.sem, h_mm.at(s, f))
            if gated:
                act.wait_ge(h_val.sem, h_val.at(s, f - 2) if f >= 2 else h_val.at(s - 1, NF - 2 + f))
                act.activation(sg[f % 2][0:fn, :], hb[(2 * f + 1) % 4][0:fn, 0:GT], ACT.Silu, bias=W["bg"][0:fn, f:f + 1])\
                   .then_inc(h_act.sem, 1)
            else:
                act.wait_ge(h_lo.sem, h_lo.at(s, f - 2) if f >= 2 else h_lo.at(s - 1, NF - 2 + f))
                act.activation(hf[f % 2][0:fn, :], hb[f % 4][0:fn, 0:GT], ACT.Relu, bias=W["b1"][0:fn, f:f + 1])\
                   .then_inc(h_act.sem, 1)
                act.wait_ge(h_act.sem, h_act.at(s, f))
                act.sem_inc(h_val.sem, 1)

        def step(s, j, p):
            for f in range(NF):
                if runs(F_MID, s):
                    hidden(s, f)
                for k in norms_here(f, s, True):
                    root(s, k)
            for k in norms_here(NF, s, True):
                root(s, k)
            if runs(F_POST, s):
                for k in range(KT):
                    act.wait_ge(q_mm.sem, q_mm.at(s, k))
                    act.wait_ge(zt_out[k].sem, zt_out[k].at(s - 1))
                    act.copy(ZT[:, k, :], hb[k][:, 0:GT]).then_inc(q_done.sem, 1)
            if runs(F_PRE, s):
                for k in range(KT):
                    act.wait_ge(p_mm.sem, p_mm.at(s, k))
                    if k == 0:
                        act.wait_ge(h_mm.sem, h_mm.at(s))
                    act.copy(XT[0][:, k, :], tb[k][:, 0:GT]).then_inc(p_hi.sem, 1)

        loop(act, step)

    @block.gpsimd
    def _(pool):
        def step(s, j, p):
            if runs(F_POST, s) and n == 0:
                g = N["post"]
                pool.wait_ge(g["out"].sem, g["out"].at(s))
                pool.tensor_tensor(Zn[:, :, :], Zn[:, :, :], wide(W["gamma2"]), ALU.mult).then_inc(gbase.sem, 1)
                pool.wait_ge(gbase.sem, gbase.at(s))
                pool.wait_ge(z_out[0].sem, z_out[0].at(s - 1))
                pool.wait_ge(N["next"]["out"].sem, N["next"]["out"].at(s - 1))
                pool.tensor_tensor(Zs[:, :, :], Zn[:, :, :], wide(W["beta2"]), ALU.add).then_inc(g["b"].sem, 1)
                pool.wait_ge(g["b"].sem, g["b"].at(s))
                pool.sem_inc(g["g"].sem, 1)
            if runs(F_PRE, s) and n == 0:
                g = N["pre"]
                pool.wait_ge(g["out"].sem, g["out"].at(s))
                pool.tensor_tensor(Xn[:, :, :], Xn[:, :, :], wide(W["gamma1"]), ALU.mult).then_inc(base.sem, 1)
                pool.wait_ge(base.sem, base.at(s))
                pool.wait_ge(p_mm.sem, p_mm.at(s - 1))
                pool.wait_ge(resid.sem, resid.at(s - 1))
                pool.tensor_tensor(Xs[:, :, :], Xn[:, :, :], wide(W["beta1"]), ALU.add).then_inc(g["b"].sem, 1)
                pool.wait_ge(g["b"].sem, g["b"].at(s))
                pool.sem_inc(g["g"].sem, 1)
            if runs(F_POST, s) and n == 2:
                pool.wait_ge(N["next"]["out"].sem, N["next"]["out"].at(s))
                pool.wait_ge(z_out[0].sem, z_out[0].at(s - 1))
                pool.tensor_tensor(Zg[:, :, :], Zx[:, :, :], wide(W["gq"]), ALU.mult).then_inc(gbase.sem, 1)
                pool.wait_ge(gbase.sem, gbase.at(s))
                pool.tensor_tensor(Zg[:, :, :], Zg[:, :, :], wide(W["bo"]), ALU.add).then_inc(zg2.sem, 1)
            if runs(F_PRE, s):
                src = Xs if n == 0 else Yin[1 - p]
                if n != 0:
                    pool.wait_ge(y_in[1 - p], 16 * (j + 1 + p))
                pool.wait_ge(o_done.sem, o_done.at(s - 1))
                pool.sem_inc(pool_gate, 1)
                if n == 2:
                    pool.tensor_copy(R[1 - p][:, :, :], src[:, :, :]).then_inc(resid.sem, 1)
                else:
                    pool.tensor_tensor(R[1 - p][:, :, :], src[:, :, :], wide(W["b2"]), ALU.add).then_inc(resid.sem, 1)

        loop(pool, step)

    @block.sync
    def _(sp):
        def group(ap, s):
            return row(ap.rearrange("(g t) p h -> g p t h", t=GB), s)

        def step(s, j, p):
            if isinstance(s, int) and s == -1:
                for g in range(2):
                    sp.dma_start(Yin[g][:, :, :], group(io["y"], g)).then_inc(y_in[g], 16)
            if runs((0, NG - 3), s):
                src = group(io["y"], s + 2)
                last = N["pre"]["out"]
                sp.wait_ge(last.sem, last.at(s - 1))
                if n != 0:
                    sp.sem_inc(sp_gate, 1)
                    sp.wait_ge(resid.sem, resid.at(s - 1))
                sp.dma_start(Yin[p][:, :, :], src).then_inc(y_in[p], 16)
            if runs(F_POST, s):
                dst = group(io["x_next"], s - 1)
                dstT = row(io["xT_next"].rearrange("(g t) (k p) q -> g p k t q", t=GB, k=KT), s - 1)
                if n == 1:
                    sp.wait_ge(z_out[0].sem, z_out[0].at(s - 1))
                    sp.sem_inc(sp_gate, 1)
                    sp.wait_ge(o_done.sem, o_done.at(s - 1))
                    sp.dma_start(dst, Z[1 - p][:, :, :]).then_inc(z_out[0].sem, 16)
                else:
                    ready = N["post"]["b"] if n == 0 else zg2
                    sp.wait_ge(ready.sem, ready.at(s))
                    sp.dma_start(dst, (Zs if n == 0 else Zg)[:, :, :]).then_inc(z_out[0].sem, 16)
                sp.wait_ge(q_done.sem, q_done.at(s))
                for k in range(KT):
                    sp.dma_start(dstT[:, k], ZT[:, k, :].rearrange("p (t q) -> p t q", t=GB)).then_inc(zt_out[k].sem, 16)

        loop(sp, step)
        for z in z_out:
            sp.wait_ge(z.sem, z.at(NG))
        for k in range(KT):
            sp.wait_ge(zt_out[k].sem, zt_out[k].at(NG))


def prepare(nc, name, loads, scales=(), splits=()):
    loaded = nc.alloc_semaphore(f"{name}_loaded")
    scaled = nc.alloc_semaphore(f"{name}_scaled")
    high = nc.alloc_semaphore(f"{name}_high")

    with nc.Block() as block:
        @block.sync
        def _(sp):
            for dst, src in loads:
                sp.dma_start(dst, src).then_inc(loaded, 16)
            sp.wait_ge(loaded, 16 * len(loads))

        @block.vector
        def _(dve):
            dve.wait_ge(loaded, 16 * len(loads))
            for src, dst, gain in scales:
                for k in range(src.shape[1]):
                    ins = dve.tensor_scalar(dst[:, k, :], src[:, k, :], gain[:, k:k + 1], None, ALU.mult)
                ins.then_inc(scaled, 1)
            if scales and splits:
                dve.wait_ge(scaled, len(scales))
            for q, (full, hi, lo) in enumerate(splits):
                dve.wait_ge(high, q + 1)
                dve.tensor_tensor(lo, full, hi.bitcast(F32), ALU.subtract)

        @block.scalar
        def _(act):
            act.wait_ge(loaded, 16 * len(loads))
            if scales and splits:
                act.wait_ge(scaled, len(scales))
            for full, hi, lo in splits:
                act.copy(hi, full).then_inc(high, 1)


def rows(ap):
    return ap.rearrange("(k p) c -> p k c", p=P)


def spread(ap, n):
    return ap.rearrange("(o h) -> o h", o=1).to_broadcast([n, ap.shape[0]])


def tiles(nc, ctx, name, shapes):
    made = {}
    for k, shape in shapes.items():
        if shape[0] == "pair":
            made[k] = [ctx.enter_context(nc.sbuf_tensor(f"{name}_{k}_{h}", list(shape[1:]), F32R)) for h in ("hi", "lo")]
        else:
            made[k] = ctx.enter_context(nc.sbuf_tensor(f"{name}_{k}", list(shape), F32))
    return made


def setup_layer0(nc, ctx, io):
    W = tiles(nc, ctx, "w0", {
        "wq": (P, KT, 1024), "wk": ("pair", P, KT, 1024), "wv": ("pair", P, KT, 1024), "wo": (P, 8, H),
        "we": (P, KT, 2, 2 * UH), "ce": (1, 2, 2 * UH), "ones": (1, P), "pb": (P, 8), "cb": (P, 8),
        "segm": (T, NR), "cmask": (T, C), "ident": (P, P)})
    W["rst"] = ctx.enter_context(nc.sbuf_tensor("w0_relpos", [P, 16, NR], F32R))
    with ExitStack() as tmp:
        raw = tiles(nc, tmp, "s0", {"wk": (P, KT, 1024), "wv": (P, KT, 1024)})
        prepare(nc, "s0a", [
            (W["wq"][:, :, :], rows(io["L0_Wq"])), (raw["wk"][:, :, :], rows(io["L0_Wk"])), (raw["wv"][:, :, :], rows(io["L0_Wv"])),
            (W["wo"][:, :, :], rows(io["L0_WoT"])), (W["ident"][:, :], io["ident"])],
            splits=[(raw[k][:, kk, :], W[k][0][:, kk, :], W[k][1][:, kk, :]) for k in ("wk", "wv") for kk in range(KT)])
    with ExitStack() as tmp:
        t = tiles(nc, tmp, "t0", {"wr": (P, KT, 1024), "pos": (P, KT, NR), "wqT": (P, 8, H), "E": (P, 8, 4), "sb": (P, 8),
                                  "rawp": (P, 8), "rawc": (P, 8), "seg": (T, C), "zero": (T, NR), "mask": (T, C)})
        seg8 = tmp.enter_context(nc.sbuf_tensor("t0_seg8", [T, C], U8))
        ps = [tmp.enter_context(nc.psum_tensor(f"t0_ps{k}", [P, 512], F32)) for k in range(4)]
        loaded, zeroed, sflt = (nc.alloc_semaphore(f"t0_{k}") for k in ("loaded", "zeroed", "seg_float"))
        dz, dsk, dld = (nc.alloc_semaphore(f"t0_{k}") for k in ("seg_cleared", "seg_skewed", "seg_back"))
        r_mm, r_hi, r_lo = (nc.alloc_semaphore(f"t0_{k}") for k in ("r_mm", "r_hi", "r_lo"))
        e_mm = nc.alloc_semaphore("t0_e_mm")
        loads = [(t["wr"][:, :, :], rows(io["L0_Wr"])), (t["pos"][:, :, :], rows(io["L0_posT"])),
                 (t["wqT"][:, :, :], rows(io["L0_WqT"])), (t["E"][:, :, :], io["L0_segE"]), (t["sb"][:, :], io["L0_segb"]),
                 (t["rawp"][:, :], io["L0_posb"]), (t["rawc"][:, :], io["L0_contb"]), (seg8[:, :], io["seg"]),
                 (t["mask"][:, :], io["cmask"])]
        with nc.Block() as block:
            @block.sync
            def _(sp):
                for dst, src in loads:
                    sp.dma_start(dst, src).then_inc(loaded, 16)
                sp.wait_ge(zeroed, 1)
                sp.dma_start(io["segscr"], t["zero"][:, :]).then_inc(dz, 16)
                sp.wait_ge(dz, 16)
                sp.wait_ge(sflt, 1)
                skew = bass.AP(tensor=io["segscr"].tensor, offset=io["segscr"].offset + T - 1, ap=[[NR - 1, T], [1, C]])
                sp.dma_start(skew, t["seg"][:, :]).then_inc(dsk, 16)
                sp.wait_ge(dsk, 16)
                sp.dma_start(W["segm"][:, :], io["segscr"]).then_inc(dld, 16)
                sp.wait_ge(dld, 16)

            @block.vector
            def _(dve):
                dve.memset(t["zero"][:, :], 0.0).then_inc(zeroed, 1)
                dve.memset(W["ones"][:, :], 1.0)
                dve.wait_ge(loaded, 16 * len(loads))
                dve.tensor_copy(t["seg"][:, :], seg8[:, :]).then_inc(sflt, 1)
                dve.tensor_scalar(W["cmask"][:, :], t["mask"][:, :], NEG, None, ALU.mult)
                dve.tensor_scalar(W["pb"][:, :], t["rawp"][:, :], 0.125, None, ALU.mult)
                dve.tensor_scalar(W["cb"][:, :], t["rawc"][:, :], 0.125, None, ALU.mult)
                for q in range(8):
                    src, even, odd = ps[q % 2], 2 * q, 2 * q + 1
                    dve.wait_ge(r_hi, q + 1)
                    dve.tensor_tensor(W["rst"][64:128, even, :], src[0:64, 0:NR], W["rst"][0:64, even, :].bitcast(F32), ALU.subtract)
                    dve.tensor_tensor(W["rst"][0:64, odd, :], src[64:128, 0:NR], W["rst"][64:128, odd, :].bitcast(F32),
                                      ALU.subtract).then_inc(r_lo, 1)

            @block.scalar
            def _(act):
                for q in range(8):
                    act.wait_ge(r_mm, q + 1)
                    act.copy(W["rst"][0:64, 2 * q, :], ps[q % 2][0:64, 0:NR])
                    act.copy(W["rst"][64:128, 2 * q + 1, :], ps[q % 2][64:128, 0:NR]).then_inc(r_hi, 1)
                act.wait_ge(e_mm, 1)
                for s in range(2):
                    for k in range(KT):
                        src = ps[2][:, k * 32:k * 32 + 32].rearrange("p (n q s r) -> p n q s r", n=2, q=4, s=2)[:, :, :, s, :]
                        dst = W["we"][:, k, :, s * UH:(s + 1) * UH].rearrange("p n (q r) -> p n q r", q=4)
                        act.activation(dst, src, ACT.Copy, scale=0.125)
                    src = ps[3][0:1, 0:32].rearrange("p (n q s r) -> p n q s r", n=2, q=4, s=2)[:, :, :, s, :]
                    dst = W["ce"][0:1, :, s * UH:(s + 1) * UH].rearrange("p n (q r) -> p n q r", q=4)
                    act.activation(dst, src, ACT.Copy, scale=0.125)

            @block.tensor
            def _(pe):
                pe.wait_ge(loaded, 16 * len(loads))
                for q in range(8):
                    if q >= 2:
                        pe.wait_ge(r_lo, q - 1)
                    for k in range(KT):
                        mm = pe.matmul(ps[q % 2][:, 0:NR], t["wr"][:, k, q * P:(q + 1) * P], t["pos"][:, k, :], start=(k == 0), stop=(k == KT - 1))
                    mm.then_inc(r_mm, 1)
                for q in range(8):
                    for k in range(KT):
                        pe.matmul(ps[2][:, k * 32 + q * 4:k * 32 + q * 4 + 4], t["wqT"][:, q, k * P:(k + 1) * P], t["E"][:, q, :],
                                  start=True, stop=True)
                    mm = pe.matmul(ps[3][0:1, q * 4:q * 4 + 4], t["sb"][:, q:q + 1], t["E"][:, q, :], start=True, stop=True)
                mm.then_inc(e_mm, 1)
    return W


def setup_layer1(nc, ctx, io):
    W = tiles(nc, ctx, "w1", {
        "wq": (P, KT, 1024), "wk": (P, KT, 1024), "wv": (P, KT, 1024), "wo": (P, 8, H), "ident": (P, P), "gain": (P, KT),
        "cosq": (P, T), "sinq": (P, T), "cosk": (P, T), "sink": (P, T), "mask": (T, T + 32),
        "memk": (P, B, 8), "perk": (P, 8, 16)})
    with ExitStack() as tmp:
        t = tiles(nc, tmp, "t1", {"wk": (P, KT, 1024), "wv": (P, KT, 1024), "wm": (P, KT, H), "means": (P, KT, B), "pw": (P, KT),
                                  "sq": (P, KT, B), "avg": (P, P), "sd": (P, B), "rs": (P, B), "pool": (P, KT, B),
                                  "tok": (P, KT, B), "memv": (B, 1024), "eps": (P, 1)})
        ps = [tmp.enter_context(nc.psum_tensor(f"t1_ps{k}", [P, 512], F32)) for k in range(5)]
        names = ("loaded", "ready", "squared", "ms_mm", "rooted", "inv", "pooled", "gained", "tok_mm", "tok_sb", "kv_mm", "v_sb", "v_out")
        s = {k: nc.alloc_semaphore(f"t1_{k}") for k in names}
        loads = [(W["wq"][:, :, :], rows(io["L1_Wq"])), (t["wk"][:, :, :], rows(io["L1_Wk"])), (t["wv"][:, :, :], rows(io["L1_Wv"])),
                 (W["wo"][:, :, :], rows(io["L1_Wo"])), (W["ident"][:, :], io["ident"]), (W["gain"][:, :], io["L1_gain"]),
                 (W["cosq"][:, :], io["cos8"][:, 0:T]), (W["sinq"][:, :], io["sin8"][:, 0:T]),
                 (W["cosk"][:, :], io["cos"][:, 0:T]), (W["sink"][:, :], io["sin"][:, 0:T]), (W["mask"][:, :], io["causal"]),
                 (W["perk"][:, :, :], io["L1_perk"]), (t["wm"][:, :, :], rows(io["L1_Wm"])),
                 (t["means"][:, :, :], io["means"].rearrange("k p b -> p k b")), (t["pw"][:, :], io["L1_poolw"])]
        with nc.Block() as block:
            @block.sync
            def _(sp):
                for dst, src in loads:
                    sp.dma_start(dst, src).then_inc(s["loaded"], 16)
                sp.wait_ge(s["v_sb"], 2)
                sp.dma_start(io["memv"], t["memv"][:, :]).then_inc(s["v_out"], 16)
                sp.wait_ge(s["v_out"], 16)

            @block.vector
            def _(dve):
                dve.memset(t["avg"][:, :], 1.0 / H)
                dve.memset(t["eps"][:, :], 1.1920929e-07)
                dve.drain().then_inc(s["ready"], 1)
                dve.wait_ge(s["loaded"], 16 * len(loads))
                dve.tensor_tensor(t["sq"][:, :, :], t["means"][:, :, :], t["means"][:, :, :], ALU.mult).then_inc(s["squared"], 1)
                dve.wait_ge(s["rooted"], 1)
                dve.reciprocal(t["rs"][:, :], t["sd"][:, :]).then_inc(s["inv"], 1)
                dve.wait_ge(s["inv"], 1)
                dve.tensor_tensor(t["pool"][:, :, :], t["means"][:, :, :], t["rs"][:, None, :].to_broadcast([P, KT, B]), ALU.mult)\
                   .then_inc(s["pooled"], 1)
                dve.wait_ge(s["pooled"], 1)
                for k in range(KT):
                    ins = dve.tensor_scalar(t["pool"][:, k, :], t["pool"][:, k, :], t["pw"][:, k:k + 1], None, ALU.mult)
                ins.then_inc(s["gained"], 1)
                for src, dst in ((W["wq"], W["wq"]), (t["wk"], W["wk"]), (t["wv"], W["wv"])):
                    for k in range(KT):
                        dve.tensor_scalar(dst[:, k, :], src[:, k, :], W["gain"][:, k:k + 1], None, ALU.mult)

            @block.scalar
            def _(act):
                act.wait_ge(s["ready"], 1)
                act.wait_ge(s["ms_mm"], 1)
                act.activation(t["sd"][:, :], ps[0][:, 0:B], ACT.Sqrt, bias=t["eps"][:, 0:1]).then_inc(s["rooted"], 1)
                act.wait_ge(s["tok_mm"], KT)
                for k in range(KT):
                    act.copy(t["tok"][:, k, :], ps[1][:, k * B:(k + 1) * B]).then_inc(s["tok_sb"], 1)
                act.wait_ge(s["kv_mm"], 1)
                act.copy(W["memk"][:, :, :].rearrange("p b t -> p t b"), ps[2][:, 0:8 * B].rearrange("p (t b) -> p t b", t=8))
                for g in range(2):
                    act.wait_ge(s["kv_mm"], 2 + g)
                    act.copy(t["memv"][:, g * 512:(g + 1) * 512], ps[3 + g][0:B, :]).then_inc(s["v_sb"], 1)

            @block.tensor
            def _(pe):
                pe.wait_ge(s["ready"], 1)
                pe.wait_ge(s["squared"], 1)
                for k in range(KT):
                    mm = pe.matmul(ps[0][:, 0:B], t["avg"][:, :], t["sq"][:, k, :], start=(k == 0), stop=(k == KT - 1))
                mm.then_inc(s["ms_mm"], 1)
                pe.wait_ge(s["gained"], 1)
                for o in range(KT):
                    for k in range(KT):
                        mm = pe.matmul(ps[1][:, o * B:(o + 1) * B], t["wm"][:, k, o * P:(o + 1) * P], t["pool"][:, k, :],
                                       start=(k == 0), stop=(k == KT - 1))
                    mm.then_inc(s["tok_mm"], 1)
                pe.wait_ge(s["tok_sb"], KT)
                for o in range(8):
                    for k in range(KT):
                        mm = pe.matmul(ps[2][:, o * B:(o + 1) * B], t["wk"][:, k, o * P:(o + 1) * P], t["tok"][:, k, :],
                                       start=(k == 0), stop=(k == KT - 1))
                mm.then_inc(s["kv_mm"], 1)
                for g in range(2):
                    for k in range(KT):
                        mm = pe.matmul(ps[3 + g][0:B, :], t["tok"][:, k, :], t["wv"][:, k, g * 512:(g + 1) * 512],
                                       start=(k == 0), stop=(k == KT - 1))
                    mm.then_inc(s["kv_mm"], 1)
    return W


def setup_layer2(nc, ctx, io):
    W = tiles(nc, ctx, "w2", {
        "wq": (P, KT, 1024), "wk": (P, KT, H), "wv": (P, KT, H), "wo": (P, 8, H), "ident": (P, P), "gain": (P, KT),
        "cosq": (P, T), "sinq": (P, T), "cosk": (P, C), "sink": (P, C)})
    prepare(nc, "s2", [
        (W["wq"][:, :, :], rows(io["L2_Wq"])), (W["wk"][:, :, :], rows(io["L2_Wk"])), (W["wv"][:, :, :], rows(io["L2_Wv"])),
        (W["wo"][:, :, :], rows(io["L2_Wo"])), (W["ident"][:, :], io["ident"]), (W["gain"][:, :], io["L2_gain"]),
        (W["cosq"][:, :], io["cos8"][:, 0:T]), (W["sinq"][:, :], io["sin8"][:, 0:T]),
        (W["cosk"][:, :], io["cos"]), (W["sink"][:, :], io["sin"])],
        scales=[(W[k], W[k], W["gain"]) for k in ("wq", "wk", "wv")])
    return W


def setup_layer3(nc, ctx, io):
    W = tiles(nc, ctx, "w3", {
        "wq": (P, KT, 512), "wk": (P, KT, 512), "wv": (P, KT, H), "wo": (P, KT, H), "ident": (P, P), "gq": (P, KT), "gkv": (P, KT),
        "neg": (P, 1)})
    prepare(nc, "s3", [
        (W["wq"][:, :, :], rows(io["L3_Wq"])), (W["wk"][:, :, :], rows(io["L3_Wk"])), (W["wv"][:, :, :], rows(io["L3_Wv"])),
        (W["wo"][:, :, :], rows(io["L3_Wo"])), (W["ident"][:, :], io["ident"]), (W["gq"][:, :], io["L3_gq"]),
        (W["gkv"][:, :], io["L3_gkv"]), (W["neg"][:, :], io["neg"])],
        scales=[(W["wq"], W["wq"], W["gq"]), (W["wk"], W["wk"], W["gkv"]), (W["wv"], W["wv"], W["gkv"])])
    return W


F_TILES = {0: [(k * P, P) for k in range(8)], 1: [(k * P, P) for k in range(5)] + [(640, 42)], 2: [(k * P, P) for k in range(8)]}


def setup_feed_forward(nc, ctx, n, io):
    ftiles = F_TILES[n]
    NF, width = len(ftiles), ftiles[-1][0] + ftiles[-1][1]
    cols = width if n == 0 else 2 * width
    shapes = {"w1": ("pair", P, KT, cols), "w2": ("pair", P, NF, H), "ident": (P, P), "b1": (P, NF), "bg": (P, NF)}
    shapes.update({0: {k: (T, H) for k in ("gamma1", "beta1", "gamma2", "beta2", "b2")},
                   1: {"b2": (T, H), "gain": (P, KT)}, 2: {"gq": (T, H), "bo": (T, H), "gain": (P, KT)}}[n])
    W = tiles(nc, ctx, f"wf{n}", shapes)
    with ExitStack() as tmp:
        raw = tiles(nc, tmp, f"sf{n}", {"w1": (P, KT, cols), "w2": (P, NF, H)})
        loads = [(W["ident"][:, :], io["ident"])]
        if n == 2:
            loads += [(raw["w1"][:, :, 0:width], rows(io["L2_Wup"])), (raw["w1"][:, :, width:cols], rows(io["L2_Wgate"]))]
        else:
            loads.append((raw["w1"][:, :, :], rows(io[f"F{n}_W1"])))
        whole = [f for f, (f0, fn) in enumerate(ftiles) if fn == P]
        nw = len(whole)
        loads.append((raw["w2"][:, 0:nw, :], rows(io[f"F{n}_W2"][0:nw * P, :])))
        for f, (f0, fn) in enumerate(ftiles):
            if fn < P:
                loads.append((raw["w2"][0:fn, f, :], io[f"F{n}_W2"][f0:f0 + fn, :]))
        if n < 2:
            for k in ["b1"] if n == 0 else ["b1", "bg"]:
                loads.append((W[k][:, :], io[f"F{n}_{k}"]))
            loads.append((W["b2"][:, :], spread(io[f"F{n}_b2"], T)))
        if n == 0:
            for k in ("gamma1", "beta1", "gamma2", "beta2"):
                loads.append((W[k][:, :], spread(io[f"F0_{k}"], T)))
        if n > 0:
            loads.append((W["gain"][:, :], io[f"F{n}_gain"]))
        if n == 2:
            loads += [(W[k][:, :], io["zeros"]) for k in ("b1", "bg")]
            loads += [(W["gq"][:, :], spread(io["L3_gq_row"], T)), (W["bo"][:, :], spread(io["L3_bo"], T))]
        splits = [(raw["w1"][:, kk, :], W["w1"][0][:, kk, :], W["w1"][1][:, kk, :]) for kk in range(KT)]
        splits.append(tuple(w[:, 0:nw, :] for w in (raw["w2"], *W["w2"])))
        for f, (f0, fn) in enumerate(ftiles):
            if fn < P:
                splits.append(tuple(w[0:fn, f, :] for w in (raw["w2"], *W["w2"])))
        prepare(nc, f"sf{n}", loads, scales=[(raw["w1"], raw["w1"], W["gain"])] if n else (), splits=splits)
    W["f"] = width
    return W, ftiles


def program(nc, io):
    dram = lambda name, shape: nc.dram_tensor(name, shape, F32).ap()
    ctxnT = dram("ctx_normT", (B, H, CP))
    means, memv = dram("ctx_means", (KT, P, B)), dram("mem_values", (B, 1024))
    segscr = dram("seg_skew", (T, NR))
    relpos = [dram(f"relpos_skew{g}", (T, 4, NR)) for g in range(2)]
    y = dram("attn_out", (B, T, H))
    x = [dram(f"x_{n}", (B, T, H)) for n in range(3)]
    xT = [dram(f"x_normT_{n}", (B, H, T)) for n in range(3)]
    io = dict(io, means=means, memv=memv, segscr=segscr)

    with nc.cleanup_on_exit(), ExitStack() as ctx:
        ident = ctx.enter_context(nc.sbuf_tensor("c_ident", [P, P], F32))
        prepare(nc, "sc", [(ident[:, :], io["ident"])])
        context_pass(nc, ctx, ident, dict(ctx=io["ctx"], ctxnT=ctxnT, means=means))

    setups = [setup_layer0, setup_layer1, setup_layer2, setup_layer3]
    streams = [dict(ctxT=io["ctxT"], ctx_cols=C, xT=io["xT"], res=io["x"], y=y, gscr=relpos),
               dict(xT=xT[0], res=x[0], y=y, memv=memv, perv=io["L1_perv"]),
               dict(ctxT=ctxnT, ctx_cols=CP, xT=xT[1], res=x[1], y=y, mask=io["mask"]),
               dict(ctxT=ctxnT, ctx_cols=CP, xT=xT[2], res=x[2], y=io["out"])]
    guards = [(1e-12, 1e-12, 1.1920929e-07), (1.1920929e-07, 1e-6, 1e-6), (1e-6, 1e-6, 1e-6)]
    for n, L in enumerate(LAYERS):
        with nc.cleanup_on_exit(), ExitStack() as ctx:
            W = setups[n](nc, ctx, io)
            attention(nc, ctx, L, W, streams[n])
        if n < 3:
            with nc.cleanup_on_exit(), ExitStack() as ctx:
                W, ftiles = setup_feed_forward(nc, ctx, n, io)
                feed_forward(nc, ctx, n, W["ident"], W, dict(y=y, x_next=x[n], xT_next=xT[n]), *guards[n], ftiles)


def kernel(**inputs):
    import numpy as _np
    import concourse.bacc as _bacc
    from concourse import mybir as _mybir
    from concourse.bass_utils import run_bass_kernel_spmd as _run

    a = {k.replace("_xattn", ""): _np.asarray(v) for k, v in inputs.items()}
    f32 = _np.float32
    pairs = _np.concatenate([h * 64 + _np.r_[0:64:2, 1:64:2] for h in range(16)])
    qkv = a["L1_to_qkv_w"]
    per_row = lambda v: v.reshape(KT, P).T
    per_unit = lambda v: _np.pad(v, (0, -len(v) % P)).reshape(-1, P).T
    E = _np.zeros((P, 8, 4), a["L0_segment_encoding"].dtype)
    for s in range(2):
        for r in range(2):
            E[64 * r:64 * r + 64, :, 2 * s + r] = a["L0_segment_encoding"][s].reshape(8, 2, 64)[:, r, :].T
    doubled = lambda w: _np.repeat(w.T.reshape(H, 16, 1, 16), 2, axis=2).reshape(H, 512)
    freq = (f32(1.0) / f32(10000.0) ** (_np.arange(0, 64, 2, dtype=f32) / f32(64)))[_np.arange(P) % 32]
    angle = _np.arange(C, dtype=f32)[None, :] * freq[:, None]
    side = _np.where(_np.arange(P) // 32 % 2 == 0, f32(-1), f32(1))[:, None]
    cos, sin = _np.cos(angle).astype(f32), (_np.sin(angle) * side).astype(f32)
    causal = _np.concatenate([_np.where(_np.arange(T)[:, None] >= _np.arange(T)[None, :], f32(0), f32(NEG)), _np.zeros((T, 32), f32)], 1)
    arrays = {
        "ident": _np.eye(P, dtype=f32), "zeros": _np.zeros((P, 8), f32),
        "neg": _np.where(_np.arange(P) % 32 >= 16, f32(-1), f32(0))[:, None],
        "cos": cos, "sin": sin, "cos8": (cos / 8).astype(f32), "sin8": (sin / 8).astype(f32), "causal": causal.astype(f32),
        "x": a["x"], "xT": a["x"].transpose(0, 2, 1), "ctx": a["ctx_1024"], "ctxT": a["ctx_1024"].transpose(0, 2, 1),
        "cmask": a["mask_1x1xSxS2_ff0"][0, 0], "seg": a["mask_1xSxS2_bk1"][0], "mask": a["mask_Bx1xSxS2_ff0"][:, 0],
        "L0_Wq": a["L0_Wq"].reshape(H, 1024), "L0_WqT": a["L0_Wq"].reshape(H, 1024).T, "L0_Wk": a["L0_Wk"].reshape(H, 1024),
        "L0_Wv": a["L0_Wv"].reshape(H, 1024), "L0_Wr": a["L0_Wr"].reshape(H, 1024), "L0_WoT": a["L0_Wo"].reshape(H, 1024).T,
        "L0_posT": a["L0_position_encoding"][0].T[:, 1:1 + NR], "L0_segE": E, "L0_segb": a["L0_segment_bias"].reshape(8, P).T,
        "L0_posb": a["L0_position_bias"].reshape(8, P).T, "L0_contb": a["L0_content_bias"].reshape(8, P).T,
        "F0_W1": a["L0_W1"], "F0_b1": per_unit(a["L0_b1"]), "F0_W2": a["L0_W2"], "F0_b2": a["L0_b2"],
        "F0_gamma1": a["L0_ln1_gamma"], "F0_beta1": a["L0_ln1_beta"], "F0_gamma2": a["L0_ln2_gamma"], "F0_beta2": a["L0_ln2_beta"],
        "L1_Wq": qkv[:, 0:1024][:, pairs], "L1_Wk": qkv[:, 1024:2048][:, pairs], "L1_Wv": qkv[:, 2048:3072],
        "L1_Wo": a["L1_to_out_w"], "L1_gain": per_row(a["L1_attn_norm_w"]), "L1_Wm": a["L1_to_mem_tokens_w"],
        "L1_poolw": per_row(a["L1_mem_pool_norm_w"]),
        "L1_perk": a["L1_persist_mem"].transpose(0, 2, 1).reshape(1024, 16)[pairs].reshape(8, P, 16).transpose(1, 0, 2),
        "L1_perv": a["L1_persist_mem"].transpose(1, 0, 2),
        "F1_W1": a["L1_ff_w1"], "F1_b1": per_unit(a["L1_ff_b1"][:682]), "F1_bg": per_unit(a["L1_ff_b1"][682:]), "F1_W2": a["L1_ff_w2"], "F1_b2": a["L1_ff_b2"], "F1_gain": per_row(a["L1_ff_norm_w"]),
        "L2_Wq": a["L2_Wq"], "L2_Wk": a["L2_Wk"], "L2_Wv": a["L2_Wv"], "L2_Wo": a["L2_Wo"], "L2_gain": per_row(a["L2_ln1_w"]),
        "L2_Wup": a["L2_Wup"], "L2_Wgate": a["L2_Wgate"], "F2_W2": a["L2_Wdown"], "F2_gain": per_row(a["L2_ln2_w"]),
        "L3_Wq": doubled(a["L3_wq"]), "L3_Wk": doubled(a["L3_wk"]), "L3_Wv": a["L3_wv"].T, "L3_Wo": a["L3_wo"].T,
        "L3_gq": per_row(a["L3_gq"]), "L3_gkv": per_row(a["L3_gkv"]), "L3_gq_row": a["L3_gq"], "L3_bo": a["L3_bo"],
    }
    arrays = {f"in_{k}": _np.ascontiguousarray(v) for k, v in arrays.items()}
    nc = _bacc.Bacc("TRN2", target_bir_lowering=False, num_devices=1)
    io = {k[3:]: nc.dram_tensor(k, v.shape, _mybir.dt.from_np(v.dtype), kind="ExternalInput").ap() for k, v in arrays.items()}
    io["out"] = nc.dram_tensor("out", (B, T, H), F32, kind="ExternalOutput").ap()
    program(nc, io)
    return _run(nc, [arrays], core_ids=[0]).results[0]["out"]
```

```python
from contextlib import ExitStack, contextmanager
from functools import partial

import numpy as np

import concourse.bass as bass
from concourse import mybir

F32 = mybir.dt.float32
F32R = mybir.dt.float32r
U8 = mybir.dt.uint8
ALU = mybir.AluOpType
ACT = mybir.ActivationFunctionType
AX = mybir.AxisListType

B, T, C, H = 32, 100, 361, 256
P = 128
KT = H // P
CT = 121
NCT = 3
CP = CT * NCT
CE = 362
NR = C + T - 1
UH = 8
UNITS = 2 * B
NEG = -1e30


class Signal:

    def __init__(self, nc, name, window, per, full, by=1):
        self.sem = nc.alloc_semaphore(name)
        self.window, self.per, self.full, self.by = window, per, full, by

    def at(self, u, i=None):
        i = self.per - 1 if i is None else i
        first, last = self.window
        if isinstance(u, int):
            before = self.per * max(0, min(u - 1, last) - first + 1)
            return self.by * (before + (i + 1 if first <= u <= last else 0))
        before = self.per * (self.full - first)
        return u * (self.per * self.by) + self.by * (before - self.full * self.per + i + 1)


def runs(window, u):
    return not isinstance(u, int) or window[0] <= u <= window[1]


def starts(u):
    return isinstance(u, int) and u == -1


def row(ap, i):
    if isinstance(i, int):
        return ap[i]
    names = " ".join(f"d{k}" for k in range(1, len(ap.shape)))
    rest = tuple(slice(None) for _ in ap.shape[1:])
    first = names.split()[0]
    return ap[(bass.ds(i, 1),) + rest].rearrange(f"a {names} -> (a {first}) " + " ".join(names.split()[1:]))


W_N, W_A, W_W, W_O = (-1, UNITS - 2), (0, UNITS - 1), (1, UNITS), (2, UNITS + 1)
A_FULL = 4


class Layer:

    def __init__(self, n, d, keys, key_tiles, aux, banks, at=None):
        self.n, self.d = n, d
        self.keys = keys
        self.key_tiles = key_tiles
        self.sw = key_tiles[-1][0] + key_tiles[-1][1]
        self.ncols = keys + keys % 2
        self.aux = aux
        self.banks = banks
        self.at = at or {}
        self.ot = UH * d // P


LATE = [True, False, False, True]
WIDE = [(0, CT), (CT, CT), (2 * CT, CT)]
LAYERS = [
    Layer(0, 64, C, WIDE,
          {(0, 0): "Q", (0, 1): "V", (1, 1): "TV", (2, 0): "WV", (2, 1): "G", (3, 0): "G", (4, 0): "GK", (4, 1): "G",
           (5, 0): "GK", (5, 1): "G", (6, 0): "K", (6, 1): "G", (7, 0): "KG"},
          {"K": [0, 2], "V": [0, 2], "Q": [1], "T": [1], "W": [1], "G": [1]}, {"Q_own": 0, "Q_position": 1, "Q_content": 6, "split": 3}),
    Layer(1, 64, T + 32, [(0, T), (T, 32)],
          {(0, 0): "Q", (1, 0): "K", (1, 1): "V", (3, 0): "T", (5, 0): "W"},
          {"Q": [0], "V": [0], "W": [1], "K": [1], "T": [1]}, {"Q_sum": 3, "K_sum": 4, "split": 6}),
    Layer(2, 64, C, WIDE,
          {(0, 0): "Q", (2, 0): "K", (4, 0): "T", (5, 0): "V", (6, 0): "W"},
          {"Q": [2], "V": [2], "W": [1], "K": [1], "T": [1]},
          {"Q_sum": 3, "K_sum": 4, "Q_hi": 4, "K_hi": 6, "Q_lo": 5, "K_lo": 6, "split": 7}),
    Layer(3, 16, C, WIDE,
          {(0, 0): "QK", (1, 1): "K", (2, 0): "V", (4, 1): "T", (5, 1): "W"},
          {"Q": [0], "K": [1, 2], "V": [0, 2], "T": [2], "W": [2]}, {"split": 4}),
]
AUX_WINDOW = {"Q": W_N, "K": W_N, "G": W_N, "V": W_A, "T": W_O, "W": W_O}


def attention(nc, ctx, L, W, io):
    n = L.n

    def sb(name, shape, dt=F32):
        return ctx.enter_context(nc.sbuf_tensor(f"a{n}_{name}", shape, dt))

    def sig(name, window, per, by=1):
        return Signal(nc, f"a{n}_{name}", window, per, A_FULL, by)

    S = [sb(f"scores{p}", [T, UH, L.sw]) for p in range(2)]
    V = [sb(f"values{p}", [CT, len(L.key_tiles), UH, L.d]) for p in range(2)]
    PT = [sb(f"probsT{p}", [P, len(L.key_tiles) * T]) for p in range(2)]
    mx = [sb(f"rowmax{p}", [T, UH]) for p in range(2)]
    nb = [sb(f"expbias{p}", [T, UH]) for p in range(2)]
    sums = [sb(f"sums{p}", [T, UH]) for p in range(2)]
    rec = sb("recip", [T, UH])
    On = sb("attn", [T, UH * L.d])
    if n in (1, 2):
        OTs = [sb(f"attnT_{h}", [P, L.ot * T], F32R) for h in ("hi", "lo")]
    else:
        OTs = sb("attnT", [P, L.ot * T])
    SC = T if n == 1 else CE
    craw, chi, clo = sb("src", [P, KT, SC + SC % 4]), sb("src_hi", [P, KT, SC + SC % 4], F32R), sb("src_lo", [P, KT, SC + SC % 4], F32R)
    xres = sb("residual", [T, H])
    Yacc, Yout = sb("yacc", [T, H]), sb("yout", [T, H])
    xT = sb("queriesT", [P, KT, T])
    if n == 0:
        Kst = [sb(f"kstack{p}", [P, UH, CE], F32R) for p in range(2)]
        Qc = [sb(f"qc_hi{p}", [P, UH, T], F32R) for p in range(2)]
        Lc = [sb(f"qc_lo{p}", [P, UH // 2, T], F32R) for p in range(2)]
        Qp, Lp = sb("qp_hi", [P, UH, T], F32R), sb("qp_lo", [P, UH // 2, T], F32R)
        qcf, qpf = sb("qc", [P, 4, T]), sb("qp", [P, 4, T])
        qco, qpo = sb("qc_own", [P, 4, T], F32R), sb("qp_own", [P, 4, T], F32R)
        e0 = [sb(f"seg0_{p}", [T, UH]) for p in range(2)]
        de = [sb(f"segd_{p}", [T, UH]) for p in range(2)]
        mtot = sb("maxtotal", [T, UH])
        rowsum, ctxsum = sb("rowsum", [P, KT]), sb("ctxsum", [P, KT, B])
        summed, sum_kept = nc.alloc_semaphore("a0_summed"), nc.alloc_semaphore("a0_sum_kept")
        Gs = [sb(f"relpos{g}", [T, 4, NR]) for g in range(2)]
    if n == 1:
        Kn = [sb(f"keys{p}", [P, 4, L.keys]) for p in range(2)]
        qf = [sb(f"queries{p}", [P, 4, T]) for p in range(2)]
        qsw, qcos = sb("rope_swapped", [P, 4, T]), sb("rope_cos", [P, 4, T])
        ksw, kcos = sb("rope_kswapped", [P, 4, T]), sb("rope_kcos", [P, 4, T])
        Vx = [sb(f"extra_values{p}", [32, UH, L.d]) for p in range(2)]
    if n == 2:
        Kst = [sb(f"kstack{p}", [P, 2, CE], F32R) for p in range(2)]
        Qh = [sb(f"q_hi{p}", [P, UH, T], F32R) for p in range(2)]
        Ql = [sb(f"q_lo{p}", [P, UH, T], F32R) for p in range(2)]
        qf, kf = sb("queries", [P, 4, T]), sb("keys", [P, CE])
        qsw, qcos = sb("rope_swapped", [P, 4, T]), sb("rope_cos", [P, 4, T])
        ksw, kcos = sb("rope_kswapped", [P, C]), sb("rope_kcos", [P, C])
        rsb, cosr, sinr = sb("rs", [P, C]), sb("cos_rs", [P, C]), sb("sin_rs", [P, C])
    if n == 3:
        Kst = [sb(f"kstack{p}", [P, 2, CE], F32R) for p in range(2)]
        khi = sb("k_hi", [P, 2, C], F32R)
        Qh = [sb(f"q_hi{p}", [P, 2, T], F32R) for p in range(2)]
        Ql = [sb(f"q_lo{p}", [P, 2, T], F32R) for p in range(2)]
    if n >= 2:
        mask = [sb(f"mask{p}", [T, C]) for p in range(2)]
        rsv = sb("rs_values", [CT, NCT])
        cV = sb("ctx_v", [P, KT, CE + 2])

    ps = [ctx.enter_context(nc.psum_tensor(f"a{n}_ps{k}", [P, 512], F32)) for k in range(8)]
    ac, aux, ptb, ob = ps[0:2], ps[2:5], ps[5:7], ps[7]

    setup = nc.alloc_semaphore(f"a{n}_setup")
    extras = nc.alloc_semaphore(f"a{n}_extras")
    sp_gate = nc.alloc_semaphore(f"a{n}_sp_gate")
    gate = nc.alloc_semaphore(f"a{n}_gate")
    ac_mm = sig("ac_mm", W_A, UH)
    scored = sig("scored", W_A, UH)
    biased = sig("biased", W_A, 1)
    maxed = sig("maxed", W_A, 1)
    probs = sig("probs", W_W, UH)
    pt_mm = sig("pt_mm", W_W, UH)
    pt_even = sig("pt_even", W_W, UH // 2)
    pt_odd = sig("pt_odd", W_W, UH // 2)
    pv_mm = sig("pv_mm", W_W, UH)
    recd = sig("recd", W_W, 1)
    normed = sig("normed", W_W, 1)
    count = {k: sum(s.count(k) for s in L.aux.values()) for k in AUX_WINDOW}
    aux_mm = {k: sig(f"{k}_mm", AUX_WINDOW[k], c) for k, c in count.items() if c}
    done = {k: sig(f"{k}_done", AUX_WINDOW[k], c) for k, c in count.items() if c}
    batch_sem = {k: nc.alloc_semaphore(f"a{n}_{k}") for k in ("xT_in", "res_in", "y_out", "ctxK_in", "ctxV_in")}
    if n == 0:
        qf_done = sig("qf_done", W_N, 2)
        qhi = sig("qhi", W_N, 2)
        qown = sig("qown", W_N, 2)
        qlo = sig("qlo", W_N, 2)
        segd = sig("segd", W_N, 1)
        khi_done = sig("khi", W_N, 4)
        g_out = [sig(f"g_out{g}", W_N, 1, 16) for g in range(2)]
        b_in = [sig(f"b_in{g}", W_N, 1, 16) for g in range(2)]
        b_add = [sig(f"b_add{g}", W_N, 1) for g in range(2)]
    split_hi, split_lo = (nc.alloc_semaphore(f"a{n}_{k}") for k in ("split_hi", "split_lo"))
    if n in (1, 2):
        ot_hi = sig("ot_hi", W_O, 1)
        swp = {k: sig(f"{k}_swapped", W_N, 1) for k in "QK"}
        cosd = {k: sig(f"{k}_cos", W_N, 1) for k in "QK"}
        sind = {k: sig(f"{k}_sin", W_N, 1) for k in "QK"}
        roped = {k: sig(f"{k}_roped", W_N, 1) for k in "QK"}
    if n == 1:
        vx_in = [nc.alloc_semaphore(f"a1_vx{p}") for p in range(2)]
        kx_done = sig("kx_done", W_N, 1)
    if n == 2:
        rsb_in, tables = nc.alloc_semaphore("a2_rs_in"), nc.alloc_semaphore("a2_tables")
        qhi2 = sig("qhi", W_N, 1)
        khi2 = sig("khi", W_N, 1)
        qlo2 = sig("qlo", W_N, 1)
    if n >= 2:
        m_in = [nc.alloc_semaphore(f"a{n}_mask{p}") for p in range(2)]
        rsv_in = nc.alloc_semaphore(f"a{n}_rs_values_in")
    if n == 3:
        khi3 = sig("khi", W_N, 2)
        qhi3 = sig("qhi", W_N, 1)

    parts = [(i, part) for i in range(UH) for part in range(2)]
    flat = [(at, k) for at in parts for k in L.aux.get(at, "")]
    order = []
    for m, (_, k) in enumerate(flat):
        number = sum(k == other for _, other in flat[:m])
        order.append((k, number, L.banks[k][number % len(L.banks[k])]))
    uses = {at: [m for m, (other, _) in enumerate(flat) if other == at] for at in parts}
    free = dict(done, **(swp if n in (1, 2) else {}))

    def bank_free(pe, u, m):
        v, q = u, m
        while True:
            q -= 1
            if q < 0:
                v, q = v - 1, len(order) - 1
            if isinstance(v, int) and v < -1:
                return
            k, i, bank = order[q]
            if bank == order[m][2] and runs(AUX_WINDOW[k], v):
                pe.wait_ge(free[k].sem, free[k].at(v, i))
                return

    def batch_of(j, par, ahead):
        return j + (par + ahead) // 2

    def loop(e, step):
        step(-1, -1, 1)
        for u in range(0, A_FULL):
            step(u, u // 2, u % 2)
        with e.Fori(A_FULL // 2, UNITS // 2 - 1) as j:
            step(2 * j, j, 0)
            step(2 * j + 1, j, 1)
        for u in range(UNITS - 2, UNITS + 2):
            step(u, u // 2, u % 2)

    heads = lambda i: slice(64 * (i % 2), 64 * (i % 2) + 64)
    block = ctx.enter_context(nc.Block())

    @block.tensor
    def _(pe):
        def mm3(out, w, x, first, last):
            pe.matmul(out, w[0], x[0], start=first, stop=False)
            pe.matmul(out, w[0], x[1], start=False, stop=False)
            return pe.matmul(out, w[1], x[0], start=False, stop=last)

        def project(u, j, par, m):
            k, i, bank = order[m]
            out = aux[bank]
            npar, nbatch = 1 - par, batch_of(j, par, 1)
            bank_free(pe, u, m)
            if k == "Q":
                pe.wait_ge(batch_sem["xT_in"], 16 * nbatch + 16)
                if n == 3:
                    for t in range(2):
                        for kk in range(KT):
                            mm = pe.matmul(out[:, t * T:(t + 1) * T], W["wq"][:, kk, (2 * npar + t) * P:(2 * npar + t + 1) * P],
                                           xT[:, kk, :], start=(kk == 0), stop=(kk == KT - 1))
                else:
                    for t in range(4):
                        for kk in range(KT):
                            mm = pe.matmul(out[:, t * T:(t + 1) * T], W["wq"][:, kk, (4 * npar + t) * P:(4 * npar + t + 1) * P],
                                           xT[:, kk, :], start=(kk == 0), stop=(kk == KT - 1))
                if n == 0:
                    seg = out[0:T, 4 * T:4 * T + 2 * UH]
                    for kk in range(KT):
                        pe.matmul(seg, xT[:, kk, :], W["we"][:, kk, npar, :], start=(kk == 0), stop=False)
                    mm = pe.matmul(seg, W["ones"][0:1, 0:T], W["ce"][0:1, npar, :], start=False, stop=True)
            if k == "K":
                if n == 0:
                    if i == 0 and par == 1:
                        pe.wait_ge(split_hi, nbatch + 1)
                        pe.wait_ge(split_lo, nbatch + 1)
                    c0 = (4 * npar + i) * P
                    for kk in range(KT):
                        mm = mm3(out[:, 0:CE], [w[:, kk, c0:c0 + P] for w in W["wk"]],
                                 [chi[:, kk, 0:CE], clo[:, kk, 0:CE]], kk == 0, kk == KT - 1)
                if n == 1:
                    for t in range(4):
                        for kk in range(KT):
                            mm = pe.matmul(out[:, t * T:(t + 1) * T], W["wk"][:, kk, (4 * npar + t) * P:(4 * npar + t + 1) * P],
                                           xT[:, kk, :], start=(kk == 0), stop=(kk == KT - 1))
                if n >= 2:
                    if i == 0 and par == 1:
                        pe.wait_ge(split_hi, nbatch + 1)
                        pe.wait_ge(split_lo, nbatch + 1)
                    c0 = (npar if n == 2 else 2 * npar + i) * P
                    for kk in range(KT):
                        mm = mm3(out[:, 0:CE], [w[:, kk, c0:c0 + P] for w in W["wk"]],
                                 [chi[:, kk, 0:CE], clo[:, kk, 0:CE]], kk == 0, kk == KT - 1)
            if k == "G":
                if i == 0:
                    pe.wait_ge(qhi.sem, qhi.at(u, 0))
                    pe.wait_ge(qlo.sem, qlo.at(u, 0))
                h = UH * npar + i
                pe.matmul(out[0:T, 0:NR], Qp[:, i, :], W["rst"][:, h, 0:NR], start=True, stop=False)
                mm = pe.matmul(out[0:T, 0:NR], Lp[heads(i), i // 2, :], W["rst"][heads(i), h, 0:NR], start=False, stop=True)
            if k == "V":
                if n == 0:
                    c0 = 512 * par
                    for kk in range(KT):
                        mm = mm3(out[0:CT, :], [x[:, kk, CT * i:CT * i + CT] for x in (chi, clo)],
                                 [w[:, kk, c0:c0 + 512] for w in W["wv"]], kk == 0, kk == KT - 1)
                if n == 1:
                    if par == 0:
                        pe.wait_ge(split_hi, j + 1)
                        pe.wait_ge(split_lo, j + 1)
                    for kk in range(KT):
                        mm = mm3(out[0:T, :], [x[:, kk, 0:T] for x in (chi, clo)],
                                 [w[:, kk, 512 * par:512 * par + 512] for w in W["wv"]], kk == 0, kk == KT - 1)
                if n >= 2:
                    pe.wait_ge(batch_sem["ctxV_in"], 16 * j + 16)
                    for t in range(NCT):
                        for kk in range(KT):
                            mm = pe.matmul(out[0:CT, t * P:(t + 1) * P], cV[:, kk, CT * t:CT * t + CT],
                                           W["wv"][:, kk, P * par:P * par + P], start=(kk == 0), stop=(kk == KT - 1))
            if k == "T":
                pe.wait_ge(normed.sem, normed.at(u - 1))
                for q in range(L.ot):
                    mm = pe.transpose(out[:, q * T:(q + 1) * T], On[:, q * P:(q + 1) * P], W["ident"][0:T, 0:T])
            if k == "W":
                pe.wait_ge(done["T"].sem, done["T"].at(u))
                for q in range(L.ot):
                    if n in (1, 2):
                        mm = mm3(out[0:T, 0:H], [x[:, q * T:(q + 1) * T] for x in OTs],
                                 [w[:, L.ot * par + q, :] for w in W["wo"]], q == 0, q == L.ot - 1)
                        continue
                    mm = pe.matmul(out[0:T, 0:H], OTs[:, q * T:(q + 1) * T], W["wo"][:, L.ot * par + q, :],
                                   start=(q == 0), stop=(q == L.ot - 1))
            mm.then_inc(aux_mm[k].sem, 1)

        def scores(u, par, i):
            if i >= 2:
                pe.wait_ge(scored.sem, scored.at(u, i - 2))
            else:
                pe.wait_ge(scored.sem, scored.at(u - 1, UH - 2 + i))
            out = ac[i % 2][0:T, 0:L.ncols]
            if n == 0:
                if i == 0:
                    pe.wait_ge(qhi.sem, qhi.at(u - 1, 1))
                    pe.wait_ge(qlo.sem, qlo.at(u - 1, 1))
                if i % 2 == 0:
                    pe.wait_ge(done["K"].sem, done["K"].at(u - 1, i // 2))
                pe.matmul(out, Qc[par][:, i, :], Kst[par][:, i, :], start=True, stop=False)
                mm = pe.matmul(out, Lc[par][heads(i), i // 2, :], Kst[par][heads(i), i, :], start=False, stop=True)
            if n == 1:
                if i == 0:
                    pe.wait_ge(roped["Q"].sem, roped["Q"].at(u - 1))
                    pe.wait_ge(roped["K"].sem, roped["K"].at(u - 1))
                    pe.wait_ge(kx_done.sem, kx_done.at(u - 1))
                mm = pe.matmul(out, qf[par][heads(i), i // 2, :], Kn[par][heads(i), i // 2, :], start=True, stop=True)
            if n == 2:
                if i == 0:
                    pe.wait_ge(qhi2.sem, qhi2.at(u - 1))
                    pe.wait_ge(qlo2.sem, qlo2.at(u - 1))
                    pe.wait_ge(done["K"].sem, done["K"].at(u - 1))
                kv = i // 4
                pe.matmul(out, Qh[par][:, i, :], Kst[par][:, kv, :], start=True, stop=False)
                mm = pe.matmul(out, Ql[par][heads(kv), i, :], Kst[par][heads(kv), kv, :], start=False, stop=True)
            if n == 3:
                if i == 0:
                    pe.wait_ge(done["Q"].sem, done["Q"].at(u - 1))
                if i % 4 == 0:
                    pe.wait_ge(done["K"].sem, done["K"].at(u - 1, i // 4))
                r = slice(32 * (i % 4), 32 * (i % 4) + 32)
                pe.matmul(out, Qh[par][r, i // 4, :], Kst[par][r, i // 4, :], start=True, stop=False)
                mm = pe.matmul(out, Ql[par][r, i // 4, :], Kst[par][r, i // 4, :], start=False, stop=True)
            mm.then_inc(ac_mm.sem, 1)

        def moved(u, i):
            s = pt_odd if i % 2 else pt_even
            pe.wait_ge(s.sem, s.at(u, i // 2))

        def transposes(u, par, i):
            wpar = 1 - par
            pe.wait_ge(probs.sem, probs.at(u, i))
            if i >= 2:
                moved(u, i - 2)
            else:
                moved(u - 1, UH - 2 + i)
            for t, (c0, cn) in enumerate(L.key_tiles):
                mm = pe.transpose(ptb[i % 2][0:cn, t * T:(t + 1) * T], S[wpar][:, i, c0:c0 + cn], W["ident"][0:T, 0:T])
            mm.then_inc(pt_mm.sem, 1)

        def weigh(u, j, par, i):
            wpar = 1 - par
            moved(u, i)
            if i == 0:
                pe.wait_ge(done["V"].sem, done["V"].at(u - 1))
                if n == 1:
                    pe.wait_ge(vx_in[wpar], 16 * batch_of(j, par, -1) + 16)
                pe.wait_ge(normed.sem, normed.at(u - 1))
            out = ob[0:T, i * L.d:(i + 1) * L.d]
            last = len(L.key_tiles) - 1
            for t, (c0, cn) in enumerate(L.key_tiles):
                v = Vx[wpar][:, i, :] if n == 1 and t == 1 else V[wpar][0:cn, t, i // 4 if n == 2 else i, :]
                mm = pe.matmul(out, PT[i % 2][0:cn, t * T:(t + 1) * T], v, start=(t == 0), stop=(t == last))
            mm.then_inc(pv_mm.sem, 1)

        def products(u, j, par, i, part):
            for m in uses[i, part]:
                if runs(AUX_WINDOW[order[m][0]], u):
                    project(u, j, par, m)

        def step(u, j, par):
            if starts(u):
                pe.wait_ge(setup, 1)
                if n == 1:
                    pe.wait_ge(extras, 32)
            for i in range(UH):
                if runs(W_A, u):
                    scores(u, par, i)
                products(u, j, par, i, 0)
                if runs(W_W, u):
                    transposes(u, par, i)
                    if i > 0 and not LATE[n]:
                        weigh(u, j, par, i - 1)
                products(u, j, par, i, 1)
                if runs(W_W, u) and i > 0 and LATE[n]:
                    weigh(u, j, par, i - 1)
            if runs(W_W, u):
                weigh(u, j, par, UH - 1)

        loop(pe, step)

    @block.vector
    def _(dve):
        def rope(u, j, par, k, m):
            _, _, bank = order[m]
            npar = 1 - par
            tile, swapped, cosb = (qf, qsw, qcos) if k == "Q" else ((Kn if n == 1 else kf), ksw, kcos)
            wide = n == 1 or k == "Q"
            src = aux[bank][:, 0:4 * T].rearrange("p (t q) -> p t q", t=4) if wide else aux[bank][:, 0:C]
            cos = W["cosq"] if k == "Q" else (W["cosk"] if n == 1 else cosr)
            if n == 2 and k == "K" and par == 1:
                dve.wait_ge(tables, 2 * (batch_of(j, par, 1) + 1))
            cos = cos[:, None, 0:T].to_broadcast([P, 4, T]) if wide else cos[:, 0:C]
            cosv = cosb[:, :, :] if wide else cosb[:, :]
            dve.wait_ge(roped[k].sem, roped[k].at(u - 1))
            dve.tensor_tensor(cosv, src, cos, ALU.mult).then_inc(cosd[k].sem, 1)

        def rope_sum(u, j, par, k):
            npar = 1 - par
            if k == "Q":
                dst = qf[npar][:, :, :] if n == 1 else qf[:, :, :]
                a, b = qcos[:, :, :], qsw[:, :, :]
            elif n == 1:
                dst, a, b = Kn[npar][:, :, 0:T], kcos[:, :, :], ksw[:, :, :]
            else:
                dst, a, b = kf[:, 0:C], kcos[:, :], ksw[:, :]
            dve.wait_ge(cosd[k].sem, cosd[k].at(u))
            dve.wait_ge(sind[k].sem, sind[k].at(u))
            if n == 1:
                dve.wait_ge(ac_mm.sem, ac_mm.at(u - 1))
            elif k == "Q":
                dve.wait_ge(qlo2.sem, qlo2.at(u - 1))
                dve.wait_ge(qhi2.sem, qhi2.at(u - 1))
            else:
                dve.wait_ge(khi2.sem, khi2.at(u - 1))
                dve.wait_ge(done["K"].sem, done["K"].at(u - 1))
            dve.tensor_tensor(dst, a, b, ALU.add).then_inc(roped[k].sem, 1)
            if n == 1 and k == "K":
                nbatch = batch_of(j, par, 1)
                at = slice(nbatch, nbatch + 1) if isinstance(nbatch, int) else bass.ds(nbatch, 1)
                mem = W["memk"][:, at, 4 * npar:4 * npar + 4].rearrange("p a t -> p t a")
                dve.tensor_copy(Kn[npar][:, :, T:T + 16], mem.to_broadcast([P, 4, 16])).then_inc(kx_done.sem, 1)

        def queries_low(u, par):
            npar = 1 - par
            dve.wait_ge(roped["Q"].sem, roped["Q"].at(u))
            dve.wait_ge(ac_mm.sem, ac_mm.at(u - 1))
            dve.wait_ge(qhi2.sem, qhi2.at(u))
            for g in range(2):
                for r in range(2):
                    rr, dd = slice(64 * r, 64 * r + 64), slice(64 * g, 64 * g + 64)
                    ins = dve.tensor_tensor(Ql[npar][dd, 4 * g + r:4 * g + 4:2, :], qf[rr, 2 * g:2 * g + 2, :],
                                            Qh[npar][rr, 4 * g + r:4 * g + 4:2, :].bitcast(F32), ALU.subtract)
            ins.then_inc(qlo2.sem, 1)

        def keys_low(u, par):
            npar = 1 - par
            dve.wait_ge(roped["K"].sem, roped["K"].at(u))
            dve.wait_ge(khi2.sem, khi2.at(u))
            dve.tensor_tensor(Kst[npar][64:128, 0, 0:C], kf[0:64, 0:C], Kst[npar][0:64, 0, 0:C].bitcast(F32), ALU.subtract)
            dve.tensor_tensor(Kst[npar][0:64, 1, 0:C], kf[64:128, 0:C], Kst[npar][64:128, 1, 0:C].bitcast(F32),
                              ALU.subtract).then_inc(done["K"].sem, 1)

        def evacuate(u, j, par, m):
            k, i, bank = order[m]
            src = aux[bank]
            npar = 1 - par
            if k == "Q" and n == 0:
                dve.wait_ge(aux_mm["Q"].sem, aux_mm["Q"].at(u))
                q4 = src[:, 0:4 * T].rearrange("p (t q) -> p t q", t=4)
                for s, (dst, bias) in enumerate(((qpf, W["pb"]), (qcf, W["cb"]))):
                    dve.wait_ge(qhi.sem, qhi.at(u - 1, s))
                    dve.wait_ge(qlo.sem, qlo.at(u - 1, s))
                    bb = bias[:, 4 * npar:4 * npar + 4, None].to_broadcast([P, 4, T])
                    dve.scalar_tensor_tensor(dst[:, :, :], q4, 0.125, bb, ALU.mult, ALU.add).then_inc(qf_done.sem, 1)
                dve.tensor_copy(e0[npar][:, :], src[0:T, 4 * T:4 * T + UH]).then_inc(segd.sem, 1)
                dve.wait_ge(segd.sem, segd.at(u))
                dve.tensor_tensor(de[npar][:, :], src[0:T, 4 * T + UH:4 * T + 2 * UH], e0[npar][:, :], ALU.subtract)\
                   .then_inc(done["Q"].sem, 1)
            if k == "G":
                dve.wait_ge(aux_mm["G"].sem, aux_mm["G"].at(u, i))
                if i % 4 == 0:
                    dve.wait_ge(g_out[i // 4].sem, g_out[i // 4].at(u - 1))
                if i == 0:
                    dve.wait_ge(done["Q"].sem, done["Q"].at(u))
                dve.scalar_tensor_tensor(Gs[i // 4][:, i % 4, :], W["segm"][:, :], de[npar][:, i:i + 1], src[0:T, 0:NR],
                                         ALU.mult, ALU.add).then_inc(done["G"].sem, 1)
            if k == "K" and n == 0:
                dve.wait_ge(khi_done.sem, khi_done.at(u, i))
                dve.tensor_tensor(Kst[npar][64:128, 2 * i, :], src[0:64, 0:CE], Kst[npar][0:64, 2 * i, :].bitcast(F32), ALU.subtract)
                dve.tensor_tensor(Kst[npar][0:64, 2 * i + 1, :], src[64:128, 0:CE],
                                  Kst[npar][64:128, 2 * i + 1, :].bitcast(F32), ALU.subtract).then_inc(done["K"].sem, 1)
            if k == "K" and n == 3:
                dve.wait_ge(khi3.sem, khi3.at(u, i))
                dve.scalar_tensor_tensor(Kst[npar][:, i, 0:C], khi[:, i, :].bitcast(F32), W["neg"][:, 0:1], src[:, 0:C],
                                         ALU.mult, ALU.add).then_inc(done["K"].sem, 1)
            if k == "Q" and n == 3:
                dve.wait_ge(qhi3.sem, qhi3.at(u))
                dve.scalar_tensor_tensor(Ql[npar][:, :, :], src[:, 0:2 * T].rearrange("p (t q) -> p t q", t=2), 0.25,
                                         Qh[npar][:, :, :].bitcast(F32), ALU.mult, ALU.subtract).then_inc(done["Q"].sem, 1)
            if k in "QK" and n in (1, 2):
                dve.wait_ge(aux_mm[k].sem, aux_mm[k].at(u))
                rope(u, j, par, k, m)
            if k == "T" and n in (1, 2):
                dve.wait_ge(ot_hi.sem, ot_hi.at(u))
                dve.tensor_tensor(OTs[1][:, :], src[:, 0:L.ot * T], OTs[0][:, :].bitcast(F32), ALU.subtract).then_inc(done["T"].sem, 1)
            if k == "W":
                dve.wait_ge(aux_mm["W"].sem, aux_mm["W"].at(u))
                if par == 0:
                    dve.wait_ge(batch_sem["res_in"], 16 * (j - 1) + 16)
                    dve.tensor_tensor(Yacc[:, :], src[0:T, 0:H], xres[:, :], ALU.add).then_inc(done["W"].sem, 1)
                else:
                    dve.wait_ge(done["W"].sem, done["W"].at(u - 1))
                    dve.wait_ge(batch_sem["y_out"], 16 * (j - 1))
                    dve.tensor_tensor(Yout[:, :], src[0:T, 0:H], Yacc[:, :], ALU.add).then_inc(done["W"].sem, 1)

        def score(u, j, par, i):
            dve.wait_ge(ac_mm.sem, ac_mm.at(u, i))
            if i == 0:
                dve.wait_ge(biased.sem, biased.at(u - 1))
                if n != 0:
                    dve.wait_ge(pt_mm.sem, pt_mm.at(u - 1))
                if n >= 2:
                    dve.wait_ge(m_in[par], 16 * j + 16)
            if n == 0 and i % 4 == 0:
                dve.wait_ge(b_add[i // 4].sem, b_add[i // 4].at(u - 1))
            dst, m = S[par][:, i, 0:L.keys], mx[par][:, i:i + 1]
            src = ac[i % 2][0:T, 0:L.keys]
            other = {0: lambda: dst, 1: lambda: W["mask"][:, :], 2: lambda: mask[par][:, :], 3: lambda: mask[par][:, :]}[n]()
            dve.sem_inc(gate, 1)
            dve.tensor_tensor_reduce(out=dst, in0=src, in1=other, scale=1.0, scalar=-3.0e38,
                                     op0=ALU.mult if n == 3 else ALU.add, op1=ALU.max,
                                     accum_out=m).then_inc(scored.sem, 1)

        def exp_bias(u, par):
            dve.wait_ge(scored.sem, scored.at(u))
            dve.wait_ge(probs.sem, probs.at(u - 1))
            if n == 0:
                dve.tensor_tensor(mtot[:, :], mx[par][:, :], e0[par][:, :], ALU.add).then_inc(maxed.sem, 1)
                dve.wait_ge(maxed.sem, maxed.at(u))
                dve.tensor_tensor(nb[par][:, :], e0[par][:, :], mtot[:, :], ALU.subtract).then_inc(biased.sem, 1)
            else:
                dve.tensor_scalar(nb[par][:, :], mx[par][:, :], -1.0, None, ALU.mult).then_inc(biased.sem, 1)

        def move_even(u, i):
            dve.wait_ge(pt_mm.sem, pt_mm.at(u, i))
            dve.wait_ge(pv_mm.sem, pv_mm.at(u, i - 2) if i >= 2 else pv_mm.at(u - 1, UH - 2 + i))
            for a, b, c in pieces:
                ins = dve.tensor_copy(PT[i % 2][0:a, b:c], ptb[i % 2][0:a, b:c])
            ins.then_inc(pt_even.sem, 1)

        def normalise(u, par):
            dve.wait_ge(probs.sem, probs.at(u))
            dve.wait_ge(normed.sem, normed.at(u - 1))
            dve.reciprocal(rec[:, :], sums[1 - par][:, :]).then_inc(recd.sem, 1)
            dve.wait_ge(pv_mm.sem, pv_mm.at(u))
            dve.wait_ge(recd.sem, recd.at(u))
            if runs(W_O, u):
                dve.wait_ge(aux_mm["T"].sem, aux_mm["T"].at(u))
            heads8 = lambda ap: ap.rearrange("p (h d) -> p h d", h=UH)
            dve.tensor_tensor(heads8(On[:, :]), heads8(ob[0:T, 0:UH * L.d]), rec[:, :, None].to_broadcast([T, UH, L.d]),
                              ALU.mult).then_inc(normed.sem, 1)

        pieces = [(CT, 0, NCT * T)] if n != 1 else [(T, 0, T), (32, T, 2 * T)]
        if n != 1:
            for p in range(2):
                dve.memset(S[p][:, :, C:L.sw], 0.0)
            dve.memset(craw[:, :, C:CE], 0.0)
        if n == 0:
            dve.memset(clo[:, :, CE:CE + 2].bitcast(F32), 0.0)
            dve.memset(chi[:, :, CE:CE + 2].bitcast(F32), 0.0)
        if n >= 2:
            dve.memset(cV[:, :, C:CE + 2], 0.0)
            for p in range(2):
                dve.memset(Kst[p][:, :, C:CE].bitcast(F32), 0.0)
        if n == 1:
            for p in range(2):
                dve.tensor_copy(Kn[p][:, :, T + 16:T + 32], W["perk"][:, 4 * p:4 * p + 4, :])
        dve.drain().then_inc(setup, 1)

        def evacuate_part(u, j, par, i, part):
            for m in uses[i, part] + (uses[i, 0] if part else []):
                k = order[m][0]
                late = n == 0 and k == "K"
                if runs(AUX_WINDOW[k], u) and late == (m not in uses[i, part]):
                    evacuate(u, j, par, m)

        def sum_context(j):
            b = j + 1
            dve.wait_ge(batch_sem["ctxK_in"], 16 * b + 16)
            dve.tensor_reduce(rowsum[:, :], craw[:, :, 0:C], AX.X, ALU.add).then_inc(summed, 1)
            dve.wait_ge(summed, b + 1)
            at = slice(b, b + 1) if isinstance(b, int) else bass.ds(b, 1)
            dve.tensor_copy(ctxsum[:, :, at].rearrange("p k a -> p (k a)"), rowsum[:, :]).then_inc(sum_kept, 1)

        def step(u, j, par):
            if n == 0 and starts(u):
                sum_context(j)
            for i in range(UH):
                if n == 0 and i == L.at["split"] and par == 1 and runs((0, UNITS - 3), u):
                    sum_context(j)
                if runs(W_A, u):
                    score(u, j, par, i)
                evacuate_part(u, j, par, i, 0)
                if runs(W_W, u):
                    if i % 2 == 0:
                        move_even(u, i)
                evacuate_part(u, j, par, i, 1)
                if n in (1, 2) and runs(W_N, u):
                    for k in "QK":
                        if L.at[f"{k}_sum"] == i:
                            rope_sum(u, j, par, k)
                    if L.at.get("Q_lo") == i:
                        queries_low(u, par)
                    if L.at.get("K_lo") == i:
                        keys_low(u, par)
            if runs(W_A, u):
                exp_bias(u, par)
            if runs(W_W, u):
                normalise(u, par)

        loop(dve, step)

    @block.scalar
    def _(act):
        def softmax(u, par, i):
            wpar = 1 - par
            if i == 0:
                act.wait_ge(biased.sem, biased.at(u - 1))
                act.wait_ge(recd.sem, recd.at(u - 2))
            s = S[wpar][:, i, 0:L.keys]
            act.activation(s, s, ACT.Exp, bias=nb[wpar][:, i:i + 1], scale=1.0,
                           accum_out=sums[wpar][:, i:i + 1]).then_inc(probs.sem, 1)

        def evacuate(u, j, par, m):
            k, i, bank = order[m]
            src = aux[bank]
            npar = 1 - par
            if k == "K" and n == 0:
                act.wait_ge(aux_mm["K"].sem, aux_mm["K"].at(u, i))
                if i == 0:
                    act.wait_ge(ac_mm.sem, ac_mm.at(u - 1))
                act.copy(Kst[npar][0:64, 2 * i, :], src[0:64, 0:CE])
                act.copy(Kst[npar][64:128, 2 * i + 1, :], src[64:128, 0:CE]).then_inc(khi_done.sem, 1)
            if k == "K" and n == 3:
                act.wait_ge(aux_mm["K"].sem, aux_mm["K"].at(u, i))
                act.wait_ge(done["K"].sem, done["K"].at(u - 1, i))
                if i == 0:
                    act.wait_ge(ac_mm.sem, ac_mm.at(u - 1))
                act.copy(khi[:, i, :], src[:, 0:C]).then_inc(khi3.sem, 1)
            if k == "Q" and n == 3:
                act.wait_ge(aux_mm["Q"].sem, aux_mm["Q"].at(u))
                act.wait_ge(ac_mm.sem, ac_mm.at(u - 1))
                act.activation(Qh[npar][:, :, :], src[:, 0:2 * T].rearrange("p (t q) -> p t q", t=2), ACT.Copy, scale=0.25)\
                   .then_inc(qhi3.sem, 1)
            if k in "QK" and n in (1, 2):
                act.wait_ge(cosd[k].sem, cosd[k].at(u))
                act.wait_ge(roped[k].sem, roped[k].at(u - 1))
                for r in range(4):
                    o = 32 * (r ^ 1)
                    if n == 1 or k == "Q":
                        dst = (qsw if k == "Q" else ksw)[32 * r:32 * r + 32, :, :]
                        sv = src[o:o + 32, 0:4 * T].rearrange("p (t q) -> p t q", t=4)
                    else:
                        dst, sv = ksw[32 * r:32 * r + 32, :], src[o:o + 32, 0:C]
                    ins = act.copy(dst, sv)
                ins.then_inc(swp[k].sem, 1)
            if k == "V":
                act.wait_ge(aux_mm["V"].sem, aux_mm["V"].at(u, i))
                if i == 0:
                    act.wait_ge(pv_mm.sem, pv_mm.at(u - 1))
                if n == 0:
                    dst = V[par][:, i, :, :]
                    sv = src[0:CT, :].rearrange("p (h d) -> p h d", h=UH)
                elif n == 1:
                    dst = V[par][0:T, 0, :, :]
                    sv = src[0:T, :].rearrange("p (h d) -> p h d", h=UH)
                if n < 2:
                    act.copy(dst, sv).then_inc(done["V"].sem, 1)
                else:
                    nv = 2 if n == 2 else UH
                    act.wait_ge(rsv_in, 16 * j + 16)
                    for t in range(NCT):
                        sv = src[0:CT, t * P:(t + 1) * P].rearrange("p (h d) -> p h d", h=nv)
                        ins = act.activation(V[par][:, t, 0:nv, :], sv, ACT.Copy, scale=rsv[:, t:t + 1])
                    ins.then_inc(done["V"].sem, 1)
            if k == "T":
                act.wait_ge(aux_mm["T"].sem, aux_mm["T"].at(u))
                act.wait_ge(aux_mm["W"].sem, aux_mm["W"].at(u - 1))
                if n in (1, 2):
                    act.copy(OTs[0][:, :], src[:, 0:L.ot * T]).then_inc(ot_hi.sem, 1)
                else:
                    act.copy(OTs[:, :], src[:, 0:L.ot * T]).then_inc(done["T"].sem, 1)

        def queries_own(u):
            for s, (full, own) in enumerate(((qpf, qpo), (qcf, qco))):
                act.wait_ge(qf_done.sem, qf_done.at(u, s))
                act.wait_ge(qlo.sem, qlo.at(u - 1, s))
                act.copy(own[:, :, :], full[:, :, :]).then_inc(qown.sem, 1)

        def queries_twice(u, par, s):
            full, hi = ((qpf, Qp), (qcf, Qc[1 - par]))[s]
            act.wait_ge(qf_done.sem, qf_done.at(u, s))
            if s == 0:
                act.wait_ge(aux_mm["G"].sem, aux_mm["G"].at(u - 1))
            else:
                act.wait_ge(ac_mm.sem, ac_mm.at(u - 1))
            for r in range(2):
                for d in range(2):
                    ins = act.copy(hi[64 * d:64 * d + 64, r:UH:2, :], full[64 * r:64 * r + 64, :, :])
            ins.then_inc(qhi.sem, 1)

        def queries_high(u, par):
            act.wait_ge(roped["Q"].sem, roped["Q"].at(u))
            act.wait_ge(ac_mm.sem, ac_mm.at(u - 1))
            for r in range(2):
                for d in range(2):
                    ins = act.copy(Qh[1 - par][64 * d:64 * d + 64, r:UH:2, :], qf[64 * r:64 * r + 64, :, :])
            ins.then_inc(qhi2.sem, 1)

        def keys_high(u, par):
            act.wait_ge(roped["K"].sem, roped["K"].at(u))
            act.wait_ge(ac_mm.sem, ac_mm.at(u - 1))
            act.copy(Kst[1 - par][0:64, 0, 0:C], kf[0:64, 0:C])
            act.copy(Kst[1 - par][64:128, 1, 0:C], kf[64:128, 0:C]).then_inc(khi2.sem, 1)

        def split(j):
            act.wait_ge(batch_sem["ctxK_in"], 16 * (j + 1) + 16)
            act.copy(chi[:, :, 0:SC], craw[:, :, 0:SC]).then_inc(split_hi, 1)

        def move_odd(u, i):
            act.wait_ge(pt_mm.sem, pt_mm.at(u, i))
            act.wait_ge(pv_mm.sem, pv_mm.at(u, i - 2) if i >= 2 else pv_mm.at(u - 1, UH - 2 + i))
            for a, b, c in ([(CT, 0, NCT * T)] if n != 1 else [(T, 0, T), (32, T, 2 * T)]):
                ins = act.copy(PT[i % 2][0:a, b:c], ptb[i % 2][0:a, b:c])
            ins.then_inc(pt_odd.sem, 1)

        def evacuate_part(u, j, par, i, part):
            for m in uses[i, part]:
                if runs(AUX_WINDOW[order[m][0]], u):
                    evacuate(u, j, par, m)

        def step(u, j, par):
            if starts(u):
                act.wait_ge(setup, 1)
                split(-1)
            if runs(W_W, u):
                softmax(u, par, 0)
            for i in range(UH):
                if runs(W_W, u) and i + 1 < UH:
                    softmax(u, par, i + 1)
                if n < 2 and i == L.at["split"] and par == 1 and runs((0, UNITS - 3), u):
                    act.wait_ge(aux_mm["V"].sem, aux_mm["V"].at(u))
                    split(j)
                if n >= 2 and i == L.at["split"] and par == 0 and runs((0, UNITS - 4), u):
                    act.wait_ge(aux_mm["K"].sem, aux_mm["K"].at(u))
                    split(j)
                evacuate_part(u, j, par, i, 0)
                if runs(W_W, u) and i % 2 == 1:
                    move_odd(u, i)
                evacuate_part(u, j, par, i, 1)
                if runs(W_N, u):
                    if L.at.get("Q_own") == i:
                        queries_own(u)
                    for s, stage in enumerate(("Q_position", "Q_content")):
                        if L.at.get(stage) == i:
                            queries_twice(u, par, s)
                    if L.at.get("Q_hi") == i:
                        queries_high(u, par)
                    if L.at.get("K_hi") == i:
                        keys_high(u, par)

        loop(act, step)

    @block.gpsimd
    def _(pool):
        def add_mask(u, par, g):
            pool.wait_ge(b_in[g].sem, b_in[g].at(u))
            s = S[1 - par][:, 4 * g:4 * g + 4, 0:C]
            pool.tensor_tensor(s, s, W["cmask"][:, None, :].to_broadcast([T, 4, C]), ALU.add).then_inc(b_add[g].sem, 1)

        def rotation_tables(u, j):
            if not starts(u):
                pool.wait_ge(cosd["K"].sem, cosd["K"].at(u))
                pool.wait_ge(sind["K"].sem, sind["K"].at(u))
            pool.wait_ge(rsb_in, 16 * (j + 1) + 16)
            pool.tensor_tensor(cosr[:, :], W["cosk"][:, :], rsb[:, :], ALU.mult).then_inc(tables, 1)
            pool.tensor_tensor(sinr[:, :], W["sink"][:, :], rsb[:, :], ALU.mult).then_inc(tables, 1)

        def split_low(j):
            pool.wait_ge(split_hi, j + 2)
            pool.tensor_tensor(clo[:, :, 0:SC], craw[:, :, 0:SC], chi[:, :, 0:SC].bitcast(F32), ALU.subtract).then_inc(split_lo, 1)

        def step(u, j, par):
            if n == 0:
                if starts(u):
                    pool.wait_ge(setup, 1)
                if runs(W_N, u):
                    for s, (full, own, lo) in enumerate(((qpf, qpo, Lp), (qcf, qco, Lc[1 - par]))):
                        pool.wait_ge(qown.sem, qown.at(u, s))
                        if s == 0:
                            pool.wait_ge(aux_mm["G"].sem, aux_mm["G"].at(u - 1))
                        else:
                            pool.wait_ge(ac_mm.sem, ac_mm.at(u - 1))
                        pool.tensor_tensor(lo[:, :, :], full[:, :, :], own[:, :, :].bitcast(F32), ALU.subtract).then_inc(qlo.sem, 1)
                if runs((0, UNITS - 1), u):
                    add_mask(u - 1, 1 - par, 1)
                if starts(u) or (par == 1 and runs((0, UNITS - 3), u)):
                    split_low(j)
                if runs(W_N, u):
                    add_mask(u, par, 0)
            if n != 0 and starts(u):
                pool.wait_ge(setup, 1)
                split_low(-1)
                if n == 2:
                    rotation_tables(u, j)
            if n in (1, 2) and runs(W_N, u):
                for k in "QK":
                    pool.wait_ge(swp[k].sem, swp[k].at(u))
                    sin = W["sinq" if k == "Q" else "sink"]
                    if n == 1 or k == "Q":
                        t = (qsw if k == "Q" else ksw)[:, :, :]
                        sv = sin[:, None, 0:T].to_broadcast([P, 4, T])
                    else:
                        t, sv = ksw[:, :], sinr[:, :]
                        if par == 1:
                            pool.wait_ge(tables, 2 * (batch_of(j, par, 1) + 1))
                    pool.tensor_tensor(t, t, sv, ALU.mult).then_inc(sind[k].sem, 1)
            if (n == 1 and par == 1 and runs((0, UNITS - 3), u)) or (n >= 2 and par == 0 and runs((0, UNITS - 4), u)):
                split_low(j)
                if n == 2:
                    rotation_tables(u, j)

        loop(pool, step)

    @block.sync
    def _(sp):
        def load_ctx(dst, src, s):
            sp.dma_start(dst[:, :, 0:C], src).then_inc(s, 16)

        ctx_src = lambda b: row(io["ctxT"], b).rearrange("(k p) c -> p k c", k=KT)
        rs_src = lambda b, parts: row(io["rs"], b)[0:C].rearrange("(o c) -> o c", o=1).to_broadcast([parts, C])
        rsv_src = lambda b: row(io["rs_rows"].rearrange("p b t -> b p t"), b)
        xT_src = lambda b: row(io["xT"], b).rearrange("(k p) q -> p k q", k=KT)

        def step(u, j, par):
            npar = 1 - par
            if starts(u):
                sp.dma_start(xT[:, :, :], xT_src(0)).then_inc(batch_sem["xT_in"], 16)
                sp.wait_ge(setup, 1)
                if n == 1:
                    for p in range(2):
                        sp.dma_start(Vx[p][16:32, :, 0:L.d], io["perv"][:, UH * p:UH * p + UH, :]).then_inc(extras, 16)
                    sp.dma_start(craw[:, :, 0:T], xT_src(0)).then_inc(batch_sem["ctxK_in"], 16)
                if n != 1:
                    load_ctx(craw, ctx_src(0), batch_sem["ctxK_in"])
                if n >= 2:
                    load_ctx(cV, ctx_src(0), batch_sem["ctxV_in"])
                    sp.dma_start(rsv[:, :], rsv_src(0)).then_inc(rsv_in, 16)
                if n == 2:
                    sp.dma_start(rsb[:, :], rs_src(0, P)).then_inc(rsb_in, 16)
            if isinstance(u, int) and u == 1 and io["ahead"]:
                io["ahead"].issue(sp)
            if n >= 2 and runs(W_N, u):
                nbatch = batch_of(j, par, 1)
                src = row(io["mask"], nbatch) if n == 2 else rs_src(nbatch, T)
                sp.wait_ge(scored.sem, scored.at(u - 1))
                sp.dma_start(mask[npar][:, :], src).then_inc(m_in[npar], 16)
            if n == 1 and runs(W_A, u):
                src = row(io["memv"], j)[par * 512:par * 512 + 512].rearrange("(o h d) -> o h d", o=1, h=UH).to_broadcast([16, UH, L.d])
                sp.wait_ge(pv_mm.sem, pv_mm.at(u - 1))
                sp.dma_start(Vx[par][0:16, :, 0:L.d], src).then_inc(vx_in[par], 16)
            if par == 1 and runs((0, UNITS - 1), u):
                src = row(io["res"], j)
                sp.wait_ge(done["W"].sem, done["W"].at(u - 1))
                sp.dma_start(xres[:, :], src).then_inc(batch_sem["res_in"], 16)
            if par == 0 and runs((0, UNITS - 4), u):
                rs_next = rs_src(j + 1, P) if n == 2 else None
                ctx_next, xT_next = ctx_src(j + 1) if n != 1 else xT_src(j + 1), xT_src(j + 1)
                last = aux_mm["K"] if n == 1 else aux_mm["Q"]
                sp.wait_ge(last.sem, last.at(u))
                sp.dma_start(xT[:, :, :], xT_next).then_inc(batch_sem["xT_in"], 16)
                sp.wait_ge(split_lo, j + 1)
                if n == 1:
                    sp.dma_start(craw[:, :, 0:T], ctx_next).then_inc(batch_sem["ctxK_in"], 16)
                else:
                    if n == 0:
                        sp.wait_ge(sum_kept, j + 1)
                    load_ctx(craw, ctx_next, batch_sem["ctxK_in"])
                if n == 2:
                    sp.wait_ge(tables, 2 * j + 2)
                    sp.dma_start(rsb[:, :], rs_next).then_inc(rsb_in, 16)
            if par == 1 and n >= 2 and runs((0, UNITS - 3), u):
                src, src_rs = ctx_src(j + 1), rsv_src(j + 1)
                sp.wait_ge(done["V"].sem, done["V"].at(u))
                load_ctx(cV, src, batch_sem["ctxV_in"])
                sp.dma_start(rsv[:, :], src_rs).then_inc(rsv_in, 16)
            if par == 1 and runs(W_O, u):
                dst = row(io["y"], j - 1)
                sp.wait_ge(done["W"].sem, done["W"].at(u))
                sp.dma_start(dst, Yout[:, :]).then_inc(batch_sem["y_out"], 16)
            if n == 0 and runs(W_N, u):
                for g in range(2):
                    sp.wait_ge(b_in[g].sem, b_in[g].at(u - 1))
                    sp.sem_inc(sp_gate, 1)
                    sp.wait_ge(done["G"].sem, done["G"].at(u, 4 * g + 3))
                    sp.dma_start(io["gscr"][g], Gs[g][:, :, :]).then_inc(g_out[g].sem, 16)
                    sp.wait_ge(g_out[g].sem, g_out[g].at(u))
                    if runs(W_W, u):
                        sp.sem_inc(sp_gate, 1)
                        sp.wait_ge(pt_mm.sem, pt_mm.at(u, 4 * g + 3))
                    skew = bass.AP(tensor=io["gscr"][g].tensor, offset=io["gscr"][g].offset + T - 1,
                                   ap=[[4 * NR - 1, T], [NR, 4], [1, C]])
                    sp.dma_start(S[npar][:, 4 * g:4 * g + 4, 0:C], skew).then_inc(b_in[g].sem, 16)

        loop(sp, step)
        if n == 0:
            sp.wait_ge(sum_kept, B)
            sp.dma_start(io["sums"].rearrange("k p b -> p k b"), ctxsum[:, :, :]).then_inc(batch_sem["ctxV_in"], 16)
            sp.wait_ge(batch_sem["ctxV_in"], 16)
        sp.wait_ge(batch_sem["y_out"], 16 * B)



def context_pass(nc, ctx, ident, io):
    def sb(name, shape, dt=F32):
        return ctx.enter_context(nc.sbuf_tensor(f"c_{name}", shape, dt))

    DEEP = 4

    def sig(name, per, by=1):
        return Signal(nc, f"c_{name}", (0, B - 1), per, DEEP, by)

    X = [sb(f"ctx{q}", [CT, NCT, H]) for q in range(DEEP)]
    sq = [sb(f"squares{q}", [CT, NCT, H]) for q in range(DEEP)]
    ssq = [sb(f"sumsq{q}", [CT, NCT]) for q in range(DEEP)]
    ss, sd, rs = (sb(k, [CT, B, NCT]) for k in ("ss", "sd", "rs"))
    rsT = sb("rsT", [B * NCT, CT])
    eps = sb("eps", [P, 1])
    bank = ctx.enter_context(nc.psum_tensor("c_ps", [P, 512], F32))
    setup = nc.alloc_semaphore("c_setup")
    loaded = [nc.alloc_semaphore(f"c_in{q}") for q in range(DEEP)]
    gate = nc.alloc_semaphore("c_gate")
    rooted, inv, turned, moved, out = (nc.alloc_semaphore(f"c_{k}") for k in ("rooted", "inv", "turned", "moved", "out"))
    squared, last_squared, kept = sig("squared", 1), sig("last_squared", 1), sig("kept", 1)
    block = ctx.enter_context(nc.Block())

    def loop(e, step):
        for b in range(DEEP):
            step(b, b // DEEP, b % DEEP)
        with e.Fori(1, B // DEEP) as j:
            for q in range(DEEP):
                step(DEEP * j + q, j, q)

    def at(b):
        return slice(b, b + 1) if isinstance(b, int) else bass.ds(b, 1)

    @block.sync
    def _(sp):
        io["ident"].issue(sp)
        sp.wait_ge(setup, 1)

        def step(b, j, q):
            src = row(io["ctx"], b)
            sp.wait_ge(kept.sem, kept.at(b - DEEP))
            sp.dma_start(X[q][:, 0:2, :], src[0:2 * CT, :].rearrange("(t p) h -> p t h", t=2)).then_inc(loaded[q], 16)
            sp.dma_start(X[q][0:C - 2 * CT, 2, :], src[2 * CT:C, :]).then_inc(loaded[q], 16)
            if isinstance(b, int) and b == DEEP - 1 and io["ahead"]:
                io["ahead"].issue(sp)

        loop(sp, step)
        sp.wait_ge(inv, 1)
        sp.dma_start(io["rs_rows"], rs[:, :, :]).then_inc(out, 16)
        sp.wait_ge(moved, 1)
        sp.dma_start(io["rs"].rearrange("b (t p) -> (b t) p", t=NCT), rsT[:, :]).then_inc(out, 16)
        sp.wait_ge(out, 32)

    @block.vector
    def _(dve):
        for q in range(DEEP):
            dve.memset(X[q][:, :, :], 0.0)
        dve.memset(eps[:, :], 1e-6)
        dve.drain().then_inc(setup, 1)

        def step(b, j, q):
            dve.wait_ge(loaded[q], 32 * j + 32)
            dve.wait_ge(kept.sem, kept.at(b - DEEP))
            dve.sem_inc(gate, 1)
            x = X[q][:, NCT - 1, :]
            dve.tensor_tensor_reduce(out=sq[q][:, NCT - 1, :], in0=x, in1=x, scale=1.0, scalar=0.0, op0=ALU.mult, op1=ALU.add,
                                     accum_out=ssq[q][:, NCT - 1:NCT]).then_inc(last_squared.sem, 1)
            dve.wait_ge(squared.sem, squared.at(b))
            dve.wait_ge(last_squared.sem, last_squared.at(b))
            dve.tensor_copy(ss[:, at(b), :].rearrange("p a t -> p (a t)"), ssq[q][:, :]).then_inc(kept.sem, 1)

        loop(dve, step)
        dve.wait_ge(rooted, 1)
        dve.reciprocal(rs[:, :, :], sd[:, :, :]).then_inc(inv, 1)
        dve.wait_ge(turned, 1)
        dve.tensor_copy(rsT[:, :], bank[0:B * NCT, 0:CT]).then_inc(moved, 1)

    @block.scalar
    def _(act):
        act.wait_ge(setup, 1)

        def step(b, j, q):
            act.wait_ge(loaded[q], 32 * j + 32)
            act.wait_ge(kept.sem, kept.at(b - DEEP))
            for t in range(NCT - 1):
                ins = act.activation(sq[q][:, t, :], X[q][:, t, :], ACT.Square, accum_out=ssq[q][:, t:t + 1])
            ins.then_inc(squared.sem, 1)

        loop(act, step)
        act.wait_ge(kept.sem, B)
        act.activation(sd[:, :, :], ss[:, :, :], ACT.Sqrt, bias=eps[0:CT, 0:1], scale=1.0 / H).then_inc(rooted, 1)

    @block.tensor
    def _(pe):
        io["ident"].wait(pe)
        pe.wait_ge(inv, 1)
        pe.transpose(bank[0:B * NCT, 0:CT], rs[:, :, :].rearrange("p b t -> p (b t)"), ident[0:CT, 0:CT]).then_inc(turned, 1)


GB = 4
NG = B // GB
GT = GB * T
F_PRE, F_MID, F_POST = (-1, NG - 2), (0, NG - 1), (1, NG)
F_FULL = 2


NORM_AT = {0: {"post": 1, "pre": 4, "next": 7}, 1: {"next": 4, "pre": 5}, 2: {"next": 5, "pre": 7}}


def feed_forward(nc, ctx, n, ident, W, io, eps_pre, eps_post, eps_next, ftiles):
    gated = n != 0
    NF = len(ftiles)

    def sb(name, shape, dt=F32):
        return ctx.enter_context(nc.sbuf_tensor(f"f{n}_{name}", shape, dt))

    def sig(name, window, per, by=1):
        return Signal(nc, f"f{n}_{name}", window, per, F_FULL, by)

    Yin = [sb(f"y{p}", [T, GB, H]) for p in range(2)]
    Xn = sb("norm", [T, GB, H])
    Xs = sb("affine", [T, GB, H]) if n == 0 else None
    XT = [sb(f"xT_{k}", [P, KT, GT], F32R) for k in ("hi", "lo")]
    R = [sb(f"resid{p}", [T, GB, H]) for p in range(2)]
    Z = [sb(f"z{p}", [T, GB, H]) for p in range(2)]
    if n == 0:
        Zn, Zs = sb("znorm", [T, GB, H]), sb("zaffine", [T, GB, H])
    Zx = sb("znext", [T, GB, H])
    if n == 2:
        Zg = sb("zgain", [T, GB, H])
    ZT = sb("zT", [P, KT, GT])
    hf = [sb(f"hidden{p}", [P, GT]) for p in range(2)]
    sg = [] if n == 0 else [sb(f"silu{p}", [P, GT]) for p in range(2)]
    Hh, Hl = sb("h_hi", [P, NF, GT], F32R), sb("h_lo", [P, NF, GT], F32R)
    st = {k: {"bn": sb(f"{k}_bn", [T, GB, 6]), "mv": sb(f"{k}_mv", [T, GB, 2]), "m2": sb(f"{k}_m2", [T, GB]),
              "v": sb(f"{k}_v", [T, GB]), "sd": sb(f"{k}_sd", [T, GB]), "rs": sb(f"{k}_rs", [T, GB])} for k in ("pre", "post", "next")}
    epst = sb("eps", [P, 3])
    ps = [ctx.enter_context(nc.psum_tensor(f"f{n}_ps{k}", [P, 512], F32)) for k in range(8)]
    hb, fb, tb = ps[0:4], ps[4:6], ps[6:8]
    norm_at = NORM_AT[n]

    setup = nc.alloc_semaphore(f"f{n}_setup")
    gate, pool_gate, sp_gate = (nc.alloc_semaphore(f"f{n}_{k}") for k in ("gate", "pool_gate", "sp_gate"))
    y_in = [nc.alloc_semaphore(f"f{n}_y_in{p}") for p in range(2)]
    z_out = [sig("z_out", F_POST, 1, 16)]
    zt_out = [sig(f"zt_out{k}", F_POST, 1, 16) for k in range(KT)]
    norms = {"pre": F_PRE, "next": F_POST}
    if n == 0:
        norms["post"] = F_POST
    N = {k: {s: sig(f"{k}_{s}", w, 1) for s in ("bn", "mv", "m2", "v", "sd", "rs", "out", "g", "b")} for k, w in norms.items()}
    p_mm, p_hi, p_lo = sig("p_mm", F_PRE, KT), sig("p_hi", F_PRE, KT), sig("p_lo", F_PRE, KT)
    q_mm, q_done = sig("q_mm", F_POST, KT), sig("q_done", F_POST, KT)
    h_mm, h_act, h_val = sig("h_mm", F_MID, NF), sig("h_act", F_MID, NF), sig("h_val", F_MID, NF)
    h_hi, h_lo = sig("h_hi", F_MID, NF), sig("h_lo", F_MID, NF)
    o_mm, o_done = sig("o_mm", F_MID, GB), sig("o_done", F_MID, GB)
    resid, base, gbase = sig("resid", F_PRE, 1), sig("base", F_PRE, 1), sig("zg", F_POST, 1)
    zg2 = sig("zg2", F_POST, 1)
    block = ctx.enter_context(nc.Block())

    def loop(e, step):
        for s in range(-1, F_FULL):
            step(s, s // 2, s % 2)
        with e.Fori(F_FULL // 2, NG // 2 - 1) as j:
            step(2 * j, j, 0)
            step(2 * j + 1, j, 1)
        for s in range(NG - 2, NG + 1):
            step(s, s // 2, s % 2)

    def norms_here(f, s, root=False):
        return [k for k, at in norm_at.items() if f == (min(at + 1, NF) if root else at) and runs(norms[k], s)]

    wide = lambda ap: ap[:, None, :].to_broadcast([T, GB, H])
    pre_in = Xs if n == 0 else Xn

    @block.tensor
    def _(pe):
        def output(s, t):
            pe.wait_ge(o_done.sem, o_done.at(s, t - 2) if t >= 2 else o_done.at(s - 1, GB - 2 + t))
            for f, (f0, fn) in enumerate(ftiles):
                if t == 0:
                    pe.wait_ge(h_lo.sem, h_lo.at(s, f))
                for a, (hh, wi) in enumerate(((Hh, 0), (Hh, 1), (Hl, 0))):
                    mm = pe.matmul(fb[t % 2][0:T, 0:H], hh[0:fn, f, t * T:(t + 1) * T], W["w2"][wi][0:fn, f, :],
                                   start=(f == 0 and a == 0), stop=(f == NF - 1 and a == 2))
            mm.then_inc(o_mm.sem, 1)

        def step(s, j, p):
            if isinstance(s, int) and s == -1:
                pe.wait_ge(setup, 1)
            if runs(F_MID, s):
                for f, (f0, fn) in enumerate(ftiles):
                    if f == 0:
                        pe.wait_ge(p_lo.sem, p_lo.at(s - 1))
                        pe.wait_ge(q_done.sem, q_done.at(s - 1))
                    banks = [hb[(2 * f) % 4], hb[(2 * f + 1) % 4]] if gated else [hb[f % 4]]
                    back = 2 if gated else 4
                    pe.wait_ge(h_val.sem, h_val.at(s, f - back) if f >= back else h_val.at(s - 1, NF - back + f))
                    for g, bank in enumerate(banks):
                        c0 = g * W["f"] + f0
                        for k in range(KT):
                            for a, (wi, xi) in enumerate(((0, 0), (0, 1), (1, 0))):
                                mm = pe.matmul(bank[0:fn, 0:GT], W["w1"][wi][:, k, c0:c0 + fn], XT[xi][:, k, :],
                                               start=(k == 0 and a == 0), stop=(k == KT - 1 and a == 2))
                    mm.then_inc(h_mm.sem, 1)
                output(s, 0)
                output(s, 1)
            if runs(F_POST, s):
                pe.wait_ge(N["next"]["out"].sem, N["next"]["out"].at(s))
                pe.wait_ge(h_val.sem, h_val.at(s))
                for k in range(KT):
                    for t in range(GB):
                        mm = pe.transpose(hb[k][:, t * T:(t + 1) * T], Zx[:, t, k * P:(k + 1) * P], ident[0:T, 0:T])
                    mm.then_inc(q_mm.sem, 1)
            if runs(F_PRE, s):
                last = N["pre"]["b"] if n == 0 else N["pre"]["out"]
                pe.wait_ge(last.sem, last.at(s))
                pe.wait_ge(p_lo.sem, p_lo.at(s - 1))
                for k in range(KT):
                    for t in range(GB):
                        mm = pe.transpose(tb[k][:, t * T:(t + 1) * T], pre_in[:, t, k * P:(k + 1) * P], ident[0:T, 0:T])
                    mm.then_inc(p_mm.sem, 1)
            if runs(F_MID, s):
                output(s, 2)
                output(s, 3)

        loop(pe, step)

    @block.vector
    def _(dve):
        for c, e in enumerate((eps_pre, eps_post, eps_next)):
            dve.memset(epst[:, c:c + 1], e)
        dve.drain().then_inc(setup, 1)

        def norm(s, k, src, dst, centred):
            a, g = st[k], N[k]
            for t in range(GB):
                ins = dve.bn_stats(a["bn"][:, t, :], src[:, t, :])
            ins.then_inc(g["bn"].sem, 1)
            dve.wait_ge(g["bn"].sem, g["bn"].at(s))
            dve.sem_inc(gate, 1)
            for t in range(GB):
                ins = dve.bn_aggr(a["mv"][:, t, :], a["bn"][:, t, :])
            ins.then_inc(g["mv"].sem, 1)
            dve.wait_ge(g["mv"].sem, g["mv"].at(s))
            dve.tensor_tensor(a["m2"][:, :], a["mv"][:, :, 0], a["mv"][:, :, 0], ALU.mult).then_inc(g["m2"].sem, 1)
            dve.wait_ge(g["m2"].sem, g["m2"].at(s))
            if centred:
                dve.tensor_copy(a["v"][:, :], a["mv"][:, :, 1]).then_inc(g["v"].sem, 1)
            else:
                dve.tensor_tensor(a["v"][:, :], a["m2"][:, :], a["mv"][:, :, 1], ALU.add).then_inc(g["v"].sem, 1)
            dve.wait_ge(g["sd"].sem, g["sd"].at(s))
            dve.reciprocal(a["rs"][:, :], a["sd"][:, :]).then_inc(g["rs"].sem, 1)
            dve.wait_ge(g["rs"].sem, g["rs"].at(s))
            for t in range(GB):
                if centred:
                    ins = dve.tensor_scalar(dst[:, t, :], src[:, t, :], a["mv"][:, t, 0:1], a["rs"][:, t:t + 1], ALU.subtract, ALU.mult)
                else:
                    ins = dve.tensor_scalar(dst[:, t, :], src[:, t, :], a["rs"][:, t:t + 1], None, ALU.mult)
            ins.then_inc(g["out"].sem, 1)

        def hidden(s, f):
            f0, fn = ftiles[f]
            dve.wait_ge(h_act.sem, h_act.at(s, f))
            if gated:
                dve.wait_ge(h_mm.sem, h_mm.at(s, f))
                dve.wait_ge(h_hi.sem, h_hi.at(s, f - 2) if f >= 2 else h_hi.at(s - 1, NF - 2 + f))
                dve.wait_ge(h_lo.sem, h_lo.at(s, f - 2) if f >= 2 else h_lo.at(s - 1, NF - 2 + f))
                dve.scalar_tensor_tensor(hf[f % 2][0:fn, :], hb[(2 * f) % 4][0:fn, 0:GT], W["b1"][0:fn, f:f + 1],
                                         sg[f % 2][0:fn, :], ALU.add, ALU.mult).then_inc(h_val.sem, 1)
                dve.wait_ge(h_val.sem, h_val.at(s, f))
            if f == 0:
                dve.wait_ge(o_mm.sem, o_mm.at(s - 1))
            dve.tensor_copy(Hh[0:fn, f, :], hf[f % 2][0:fn, :]).then_inc(h_hi.sem, 1)
            dve.wait_ge(h_hi.sem, h_hi.at(s, f))
            dve.tensor_tensor(Hl[0:fn, f, :], hf[f % 2][0:fn, :], Hh[0:fn, f, :].bitcast(F32), ALU.subtract).then_inc(h_lo.sem, 1)

        def one_norm(s, j, p, k):
            if k == "pre":
                dve.wait_ge(y_in[1 - p], 16 * (j + 1 + p))
                if n == 0:
                    dve.wait_ge(N["pre"]["g"].sem, N["pre"]["g"].at(s - 1))
                else:
                    dve.wait_ge(p_mm.sem, p_mm.at(s - 1))
                norm(s, "pre", Yin[1 - p], Xn, n == 0)
                return
            dve.wait_ge(o_done.sem, o_done.at(s - 1))
            if k == "post":
                dve.wait_ge(N["post"]["g"].sem, N["post"]["g"].at(s - 1))
                norm(s, "post", Z[1 - p], Zn, True)
                return
            if n == 0:
                dve.wait_ge(N["post"]["b"].sem, N["post"]["b"].at(s))
            dve.wait_ge(q_mm.sem, q_mm.at(s - 1))
            if n == 2:
                dve.wait_ge(gbase.sem, gbase.at(s - 1))
            norm(s, "next", Zs if n == 0 else Z[1 - p], Zx, False)

        def norm_after(s, j, p, f):
            for k in norms_here(f, s):
                one_norm(s, j, p, k)

        def output(s, p, t):
            dve.wait_ge(o_mm.sem, o_mm.at(s, t))
            if t == 0:
                dve.wait_ge(resid.sem, resid.at(s - 1))
                last = N["post" if n == 0 else "next"]["out"]
                dve.wait_ge(last.sem, last.at(s - 1))
                if n == 1:
                    dve.wait_ge(z_out[0].sem, z_out[0].at(s - 1))
            dve.tensor_tensor(Z[p][:, t, :], fb[t % 2][0:T, 0:H], R[p][:, t, :], ALU.add).then_inc(o_done.sem, 1)

        def step(s, j, p):
            for f in range(NF):
                if runs(F_MID, s):
                    hidden(s, f)
                norm_after(s, j, p, f)
            if runs(F_MID, s):
                output(s, p, 0)
            norm_after(s, j, p, NF)
            if runs(F_MID, s):
                output(s, p, 1)
            if runs(F_PRE, s):
                for k in range(KT):
                    dve.wait_ge(p_hi.sem, p_hi.at(s, k))
                    dve.tensor_tensor(XT[1][:, k, :], tb[k][:, 0:GT], XT[0][:, k, :].bitcast(F32), ALU.subtract).then_inc(p_lo.sem, 1)
            if runs(F_MID, s):
                output(s, p, 2)
                output(s, p, 3)

        loop(dve, step)

    @block.scalar
    def _(act):
        act.wait_ge(setup, 1)

        def root(s, k):
            c = ("pre", "post", "next").index(k)
            act.wait_ge(N[k]["v"].sem, N[k]["v"].at(s))
            act.wait_ge(N[k]["rs"].sem, N[k]["rs"].at(s - 1))
            act.activation(st[k]["sd"][:, :], st[k]["v"][:, :], ACT.Sqrt, bias=epst[0:T, c:c + 1]).then_inc(N[k]["sd"].sem, 1)

        def hidden(s, f):
            f0, fn = ftiles[f]
            act.wait_ge(h_mm.sem, h_mm.at(s, f))
            if gated:
                act.wait_ge(h_val.sem, h_val.at(s, f - 2) if f >= 2 else h_val.at(s - 1, NF - 2 + f))
                act.activation(sg[f % 2][0:fn, :], hb[(2 * f + 1) % 4][0:fn, 0:GT], ACT.Silu, bias=W["bg"][0:fn, f:f + 1])\
                   .then_inc(h_act.sem, 1)
            else:
                act.wait_ge(h_lo.sem, h_lo.at(s, f - 2) if f >= 2 else h_lo.at(s - 1, NF - 2 + f))
                act.activation(hf[f % 2][0:fn, :], hb[f % 4][0:fn, 0:GT], ACT.Relu, bias=W["b1"][0:fn, f:f + 1])\
                   .then_inc(h_act.sem, 1)
                act.wait_ge(h_act.sem, h_act.at(s, f))
                act.sem_inc(h_val.sem, 1)

        def step(s, j, p):
            for f in range(NF):
                if runs(F_MID, s):
                    hidden(s, f)
                for k in norms_here(f, s, True):
                    root(s, k)
            for k in norms_here(NF, s, True):
                root(s, k)
            if runs(F_POST, s):
                for k in range(KT):
                    act.wait_ge(q_mm.sem, q_mm.at(s, k))
                    act.wait_ge(zt_out[k].sem, zt_out[k].at(s - 1))
                    act.copy(ZT[:, k, :], hb[k][:, 0:GT]).then_inc(q_done.sem, 1)
            if runs(F_PRE, s):
                for k in range(KT):
                    act.wait_ge(p_mm.sem, p_mm.at(s, k))
                    if k == 0:
                        act.wait_ge(h_mm.sem, h_mm.at(s))
                    act.copy(XT[0][:, k, :], tb[k][:, 0:GT]).then_inc(p_hi.sem, 1)

        loop(act, step)

    @block.gpsimd
    def _(pool):
        def step(s, j, p):
            if runs(F_POST, s) and n == 0:
                g = N["post"]
                pool.wait_ge(g["out"].sem, g["out"].at(s))
                pool.tensor_tensor(Zn[:, :, :], Zn[:, :, :], wide(W["gamma2"]), ALU.mult).then_inc(gbase.sem, 1)
                pool.wait_ge(gbase.sem, gbase.at(s))
                pool.wait_ge(z_out[0].sem, z_out[0].at(s - 1))
                pool.wait_ge(N["next"]["out"].sem, N["next"]["out"].at(s - 1))
                pool.tensor_tensor(Zs[:, :, :], Zn[:, :, :], wide(W["beta2"]), ALU.add).then_inc(g["b"].sem, 1)
                pool.wait_ge(g["b"].sem, g["b"].at(s))
                pool.sem_inc(g["g"].sem, 1)
            if runs(F_PRE, s) and n == 0:
                g = N["pre"]
                pool.wait_ge(g["out"].sem, g["out"].at(s))
                pool.tensor_tensor(Xn[:, :, :], Xn[:, :, :], wide(W["gamma1"]), ALU.mult).then_inc(base.sem, 1)
                pool.wait_ge(base.sem, base.at(s))
                pool.wait_ge(p_mm.sem, p_mm.at(s - 1))
                pool.wait_ge(resid.sem, resid.at(s - 1))
                pool.tensor_tensor(Xs[:, :, :], Xn[:, :, :], wide(W["beta1"]), ALU.add).then_inc(g["b"].sem, 1)
                pool.wait_ge(g["b"].sem, g["b"].at(s))
                pool.sem_inc(g["g"].sem, 1)
            if runs(F_POST, s) and n == 2:
                pool.wait_ge(N["next"]["out"].sem, N["next"]["out"].at(s))
                pool.wait_ge(z_out[0].sem, z_out[0].at(s - 1))
                pool.tensor_tensor(Zg[:, :, :], Zx[:, :, :], wide(W["gq"]), ALU.mult).then_inc(gbase.sem, 1)
                pool.wait_ge(gbase.sem, gbase.at(s))
                pool.tensor_tensor(Zg[:, :, :], Zg[:, :, :], wide(W["bo"]), ALU.add).then_inc(zg2.sem, 1)
            if runs(F_PRE, s):
                src = Xs if n == 0 else Yin[1 - p]
                if n != 0:
                    pool.wait_ge(y_in[1 - p], 16 * (j + 1 + p))
                pool.wait_ge(o_done.sem, o_done.at(s - 1))
                pool.sem_inc(pool_gate, 1)
                if n == 2:
                    pool.tensor_copy(R[1 - p][:, :, :], src[:, :, :]).then_inc(resid.sem, 1)
                else:
                    pool.tensor_tensor(R[1 - p][:, :, :], src[:, :, :], wide(W["b2"]), ALU.add).then_inc(resid.sem, 1)

        loop(pool, step)

    @block.sync
    def _(sp):
        def group(ap, s):
            return row(ap.rearrange("(g t) p h -> g p t h", t=GB), s)

        def step(s, j, p):
            if isinstance(s, int) and s == -1:
                for g in range(2):
                    sp.dma_start(Yin[g][:, :, :], group(io["y"], g)).then_inc(y_in[g], 16)
                if io["ahead"]:
                    io["ahead"].issue(sp)
            if runs((0, NG - 3), s):
                src = group(io["y"], s + 2)
                last = N["pre"]["out"]
                sp.wait_ge(last.sem, last.at(s - 1))
                if n != 0:
                    sp.sem_inc(sp_gate, 1)
                    sp.wait_ge(resid.sem, resid.at(s - 1))
                sp.dma_start(Yin[p][:, :, :], src).then_inc(y_in[p], 16)
            if runs(F_POST, s):
                dst = group(io["x_next"], s - 1)
                dstT = row(io["xT_next"].rearrange("(g t) (k p) q -> g p k t q", t=GB, k=KT), s - 1)
                if n == 1:
                    sp.wait_ge(z_out[0].sem, z_out[0].at(s - 1))
                    sp.sem_inc(sp_gate, 1)
                    sp.wait_ge(o_done.sem, o_done.at(s - 1))
                    sp.dma_start(dst, Z[1 - p][:, :, :]).then_inc(z_out[0].sem, 16)
                else:
                    ready = N["post"]["b"] if n == 0 else zg2
                    sp.wait_ge(ready.sem, ready.at(s))
                    sp.dma_start(dst, (Zs if n == 0 else Zg)[:, :, :]).then_inc(z_out[0].sem, 16)
                sp.wait_ge(q_done.sem, q_done.at(s))
                for k in range(KT):
                    sp.dma_start(dstT[:, k], ZT[:, k, :].rearrange("p (t q) -> p t q", t=GB)).then_inc(zt_out[k].sem, 16)

        loop(sp, step)
        for z in z_out:
            sp.wait_ge(z.sem, z.at(NG))
        for k in range(KT):
            sp.wait_ge(zt_out[k].sem, zt_out[k].at(NG))


class Fetch:

    def __init__(self, nc, name):
        self.nc, self.name, self.loads, self.issued = nc, name, [], False
        self.arrived = nc.alloc_semaphore(f"{name}_arrived")

    def issue(self, sp):
        for dst, src in self.loads:
            sp.dma_start(dst, src).then_inc(self.arrived, 16)
        self.issued = True

    def wait(self, e):
        e.wait_ge(self.arrived, 16 * len(self.loads))


def prepare(nc, name, fetch, scales=(), splits=()):
    scaled = nc.alloc_semaphore(f"{name}_scaled")
    high = nc.alloc_semaphore(f"{name}_high")

    with nc.Block() as block:
        @block.sync
        def _(sp):
            if not fetch.issued:
                fetch.issue(sp)
            fetch.wait(sp)

        @block.vector
        def _(dve):
            fetch.wait(dve)
            for src, dst, gain in scales:
                for k in range(src.shape[1]):
                    ins = dve.tensor_scalar(dst[:, k, :], src[:, k, :], gain[:, k:k + 1], None, ALU.mult)
                ins.then_inc(scaled, 1)
            if scales and splits:
                dve.wait_ge(scaled, len(scales))
            for q, (full, hi, lo) in enumerate(splits):
                dve.wait_ge(high, q + 1)
                dve.tensor_tensor(lo, full, hi.bitcast(F32), ALU.subtract)

        @block.scalar
        def _(act):
            fetch.wait(act)
            if scales and splits:
                act.wait_ge(scaled, len(scales))
            for full, hi, lo in splits:
                act.copy(hi, full).then_inc(high, 1)


def rows(ap):
    return ap.rearrange("(k p) c -> p k c", p=P)


def spread(ap, n):
    return ap.rearrange("(o h) -> o h", o=1).to_broadcast([n, ap.shape[0]])


def tiles(nc, ctx, name, shapes, side=None):
    made = {}
    for k, shape in shapes.items():
        if shape[0] == "pair":
            made[k] = [ctx.enter_context(nc.sbuf_tensor(f"{name}_{k}_{h}", list(shape[1:]), F32R, side=side)) for h in ("hi", "lo")]
        else:
            made[k] = ctx.enter_context(nc.sbuf_tensor(f"{name}_{k}", list(shape), F32, side=side))
    return made


def setup_layer0(nc, keep, tmp, io, fetch):
    W = tiles(nc, keep, "w0", {
        "wq": (P, KT, 1024), "wk": ("pair", P, KT, 1024), "wv": ("pair", P, KT, 1024), "wo": (P, 8, H),
        "we": (P, KT, 2, 2 * UH), "ce": (1, 2, 2 * UH), "ones": (1, P), "pb": (P, 8), "cb": (P, 8),
        "segm": (T, NR), "cmask": (T, C), "ident": (P, P)})
    W["rst"] = keep.enter_context(nc.sbuf_tensor("w0_relpos", [P, 16, NR], F32R))
    raw = tiles(nc, tmp, "s0", {"wk": (P, KT, 1024), "wv": (P, KT, 1024)})
    t = tiles(nc, tmp, "t0", {"wr": (P, KT, 1024), "pos": (P, KT, NR), "wqT": (P, 8, H), "E": (P, 8, 4), "sb": (P, 8),
                              "rawp": (P, 8), "rawc": (P, 8), "seg": (T, C), "zero": (T, NR), "mask": (T, C)})
    seg8 = tmp.enter_context(nc.sbuf_tensor("t0_seg8", [T, C], U8))
    fetch.loads += [
        (t["wr"][:, :, :], rows(io["L0_Wr"])), (t["pos"][:, :, :], rows(io["L0_posT"])),
        (t["wqT"][:, :, :], rows(io["L0_WqT"])), (t["E"][:, :, :], io["L0_segE"]), (t["sb"][:, :], io["L0_segb"]),
        (t["rawp"][:, :], io["L0_posb"]), (t["rawc"][:, :], io["L0_contb"]), (seg8[:, :], io["seg"]), (t["mask"][:, :], io["cmask"]),
        (W["wq"][:, :, :], rows(io["L0_Wq"])), (raw["wk"][:, :, :], rows(io["L0_Wk"])), (raw["wv"][:, :, :], rows(io["L0_Wv"])),
        (W["wo"][:, :, :], rows(io["L0_WoT"])), (W["ident"][:, :], io["ident"])]

    def finish():
        prepare(nc, "s0", fetch, splits=[(raw[k][:, kk, :], W[k][0][:, kk, :], W[k][1][:, kk, :]) for k in ("wk", "wv") for kk in range(KT)])
        with ExitStack() as banks:
            layer0_tables(nc, banks, io, W, t, seg8)
        return W

    return finish


def layer0_tables(nc, banks, io, W, t, seg8):
    ps = [banks.enter_context(nc.psum_tensor(f"t0_ps{k}", [P, 512], F32)) for k in range(4)]
    zeroed, sflt = (nc.alloc_semaphore(f"t0_{k}") for k in ("zeroed", "seg_float"))
    dz, dsk, dld = (nc.alloc_semaphore(f"t0_{k}") for k in ("seg_cleared", "seg_skewed", "seg_back"))
    r_mm, r_hi, r_lo = (nc.alloc_semaphore(f"t0_{k}") for k in ("r_mm", "r_hi", "r_lo"))
    e_mm = nc.alloc_semaphore("t0_e_mm")
    with nc.Block() as block:
        @block.sync
        def _(sp):
            sp.wait_ge(zeroed, 1)
            sp.dma_start(io["segscr"], t["zero"][:, :]).then_inc(dz, 16)
            sp.wait_ge(dz, 16)
            sp.wait_ge(sflt, 1)
            skew = bass.AP(tensor=io["segscr"].tensor, offset=io["segscr"].offset + T - 1, ap=[[NR - 1, T], [1, C]])
            sp.dma_start(skew, t["seg"][:, :]).then_inc(dsk, 16)
            sp.wait_ge(dsk, 16)
            sp.dma_start(W["segm"][:, :], io["segscr"]).then_inc(dld, 16)
            sp.wait_ge(dld, 16)

        @block.vector
        def _(dve):
            dve.memset(t["zero"][:, :], 0.0).then_inc(zeroed, 1)
            dve.memset(W["ones"][:, :], 1.0)
            dve.tensor_copy(t["seg"][:, :], seg8[:, :]).then_inc(sflt, 1)
            dve.tensor_scalar(W["cmask"][:, :], t["mask"][:, :], NEG, None, ALU.mult)
            dve.tensor_scalar(W["pb"][:, :], t["rawp"][:, :], 0.125, None, ALU.mult)
            dve.tensor_scalar(W["cb"][:, :], t["rawc"][:, :], 0.125, None, ALU.mult)
            for q in range(8):
                src, even, odd = ps[q % 2], 2 * q, 2 * q + 1
                dve.wait_ge(r_hi, q + 1)
                dve.tensor_tensor(W["rst"][64:128, even, :], src[0:64, 0:NR], W["rst"][0:64, even, :].bitcast(F32), ALU.subtract)
                dve.tensor_tensor(W["rst"][0:64, odd, :], src[64:128, 0:NR], W["rst"][64:128, odd, :].bitcast(F32),
                                  ALU.subtract).then_inc(r_lo, 1)

        @block.scalar
        def _(act):
            for q in range(8):
                act.wait_ge(r_mm, q + 1)
                act.copy(W["rst"][0:64, 2 * q, :], ps[q % 2][0:64, 0:NR])
                act.copy(W["rst"][64:128, 2 * q + 1, :], ps[q % 2][64:128, 0:NR]).then_inc(r_hi, 1)
            act.wait_ge(e_mm, 1)
            for s in range(2):
                for k in range(KT):
                    src = ps[2][:, k * 32:k * 32 + 32].rearrange("p (n q s r) -> p n q s r", n=2, q=4, s=2)[:, :, :, s, :]
                    dst = W["we"][:, k, :, s * UH:(s + 1) * UH].rearrange("p n (q r) -> p n q r", q=4)
                    act.activation(dst, src, ACT.Copy, scale=0.125)
                src = ps[3][0:1, 0:32].rearrange("p (n q s r) -> p n q s r", n=2, q=4, s=2)[:, :, :, s, :]
                dst = W["ce"][0:1, :, s * UH:(s + 1) * UH].rearrange("p n (q r) -> p n q r", q=4)
                act.activation(dst, src, ACT.Copy, scale=0.125)

        @block.tensor
        def _(pe):
            for q in range(8):
                if q >= 2:
                    pe.wait_ge(r_lo, q - 1)
                for k in range(KT):
                    mm = pe.matmul(ps[q % 2][:, 0:NR], t["wr"][:, k, q * P:(q + 1) * P], t["pos"][:, k, :], start=(k == 0), stop=(k == KT - 1))
                mm.then_inc(r_mm, 1)
            for q in range(8):
                for k in range(KT):
                    pe.matmul(ps[2][:, k * 32 + q * 4:k * 32 + q * 4 + 4], t["wqT"][:, q, k * P:(k + 1) * P], t["E"][:, q, :],
                              start=True, stop=True)
                mm = pe.matmul(ps[3][0:1, q * 4:q * 4 + 4], t["sb"][:, q:q + 1], t["E"][:, q, :], start=True, stop=True)
            mm.then_inc(e_mm, 1)


def setup_layer1(nc, keep, tmp, io, fetch):
    W = tiles(nc, keep, "w1", {
        "wq": (P, KT, 1024), "wk": (P, KT, 1024), "wv": ("pair", P, KT, 1024), "wo": ("pair", P, 8, H), "ident": (P, P),
        "gain": (P, KT), "cosq": (P, T), "sinq": (P, T), "cosk": (P, T), "sink": (P, T), "mask": (T, T + 32),
        "memk": (P, B, 8), "perk": (P, 8, 16)})
    t = tiles(nc, tmp, "t1", {"wk": (P, KT, 1024), "wv": (P, KT, 1024), "wo": (P, 8, H), "wm": (P, KT, H), "means": (P, KT, B), "pw": (P, KT),
                              "sq": (P, KT, B), "avg": (P, P), "sd": (P, B), "rs": (P, B), "pool": (P, KT, B),
                              "tok": (P, KT, B), "memv": (B, 1024), "eps": (P, 1)})
    fetch.loads += [(W["wq"][:, :, :], rows(io["L1_Wq"])), (t["wk"][:, :, :], rows(io["L1_Wk"])), (t["wv"][:, :, :], rows(io["L1_Wv"])),
             (t["wo"][:, :, :], rows(io["L1_Wo"])), (W["ident"][:, :], io["ident"]), (W["gain"][:, :], io["L1_gain"]),
             (W["cosq"][:, :], io["cos8"][:, 0:T]), (W["sinq"][:, :], io["sin8"][:, 0:T]),
             (W["cosk"][:, :], io["cos"][:, 0:T]), (W["sink"][:, :], io["sin"][:, 0:T]), (W["mask"][:, :], io["causal"]),
             (W["perk"][:, :, :], io["L1_perk"]), (t["wm"][:, :, :], rows(io["L1_Wm"])),
             (t["means"][:, :, :], io["sums"].rearrange("k p b -> p k b")), (t["pw"][:, :], io["L1_poolw"])]

    def finish():
        with ExitStack() as banks:
            layer1_memory(nc, banks, io, W, t, fetch)
        prepare(nc, "s1", fetch, splits=[(t[k][:, q:q + step, :], W[k][0][:, q:q + step, :], W[k][1][:, q:q + step, :])
                                         for k, step in (("wv", 1), ("wo", 4)) for q in range(0, t[k].shape[1], step)])
        return W

    return finish


def layer1_memory(nc, banks, io, W, t, fetch):
    ps = [banks.enter_context(nc.psum_tensor(f"t1_ps{k}", [P, 512], F32)) for k in range(5)]
    names = ("ready", "averaged", "squared", "ms_mm", "rooted", "inv", "pooled", "gained", "tok_mm", "tok_sb", "kv_mm", "v_sb", "v_out")
    s = {k: nc.alloc_semaphore(f"t1_{k}") for k in names}
    with nc.Block() as block:
        @block.sync
        def _(sp):
            if not fetch.issued:
                fetch.issue(sp)
            fetch.wait(sp)
            sp.wait_ge(s["v_sb"], 2)
            sp.dma_start(io["memv"], t["memv"][:, :]).then_inc(s["v_out"], 16)
            sp.wait_ge(s["v_out"], 16)

        @block.vector
        def _(dve):
            dve.memset(t["avg"][:, :], 1.0 / H)
            dve.memset(t["eps"][:, :], 1.1920929e-07)
            dve.drain().then_inc(s["ready"], 1)
            fetch.wait(dve)
            dve.tensor_scalar(t["means"][:, :, :], t["means"][:, :, :], 1.0 / C, None, ALU.mult).then_inc(s["averaged"], 1)
            dve.wait_ge(s["averaged"], 1)
            dve.tensor_tensor(t["sq"][:, :, :], t["means"][:, :, :], t["means"][:, :, :], ALU.mult).then_inc(s["squared"], 1)
            dve.wait_ge(s["rooted"], 1)
            dve.reciprocal(t["rs"][:, :], t["sd"][:, :]).then_inc(s["inv"], 1)
            dve.wait_ge(s["inv"], 1)
            dve.tensor_tensor(t["pool"][:, :, :], t["means"][:, :, :], t["rs"][:, None, :].to_broadcast([P, KT, B]), ALU.mult)\
               .then_inc(s["pooled"], 1)
            dve.wait_ge(s["pooled"], 1)
            for k in range(KT):
                ins = dve.tensor_scalar(t["pool"][:, k, :], t["pool"][:, k, :], t["pw"][:, k:k + 1], None, ALU.mult)
            ins.then_inc(s["gained"], 1)
            for src, dst in ((W["wq"], W["wq"]), (t["wk"], W["wk"]), (t["wv"], t["wv"])):
                if src is t["wv"]:
                    dve.wait_ge(s["kv_mm"], 3)
                for k in range(KT):
                    dve.tensor_scalar(dst[:, k, :], src[:, k, :], W["gain"][:, k:k + 1], None, ALU.mult)

        @block.scalar
        def _(act):
            act.wait_ge(s["ready"], 1)
            act.wait_ge(s["ms_mm"], 1)
            act.activation(t["sd"][:, :], ps[0][:, 0:B], ACT.Sqrt, bias=t["eps"][:, 0:1]).then_inc(s["rooted"], 1)
            act.wait_ge(s["tok_mm"], KT)
            for k in range(KT):
                act.copy(t["tok"][:, k, :], ps[1][:, k * B:(k + 1) * B]).then_inc(s["tok_sb"], 1)
            act.wait_ge(s["kv_mm"], 1)
            act.copy(W["memk"][:, :, :].rearrange("p b t -> p t b"), ps[2][:, 0:8 * B].rearrange("p (t b) -> p t b", t=8))
            for g in range(2):
                act.wait_ge(s["kv_mm"], 2 + g)
                act.copy(t["memv"][:, g * 512:(g + 1) * 512], ps[3 + g][0:B, :]).then_inc(s["v_sb"], 1)

        @block.tensor
        def _(pe):
            pe.wait_ge(s["ready"], 1)
            pe.wait_ge(s["squared"], 1)
            for k in range(KT):
                mm = pe.matmul(ps[0][:, 0:B], t["avg"][:, :], t["sq"][:, k, :], start=(k == 0), stop=(k == KT - 1))
            mm.then_inc(s["ms_mm"], 1)
            pe.wait_ge(s["gained"], 1)
            for o in range(KT):
                for k in range(KT):
                    mm = pe.matmul(ps[1][:, o * B:(o + 1) * B], t["wm"][:, k, o * P:(o + 1) * P], t["pool"][:, k, :],
                                   start=(k == 0), stop=(k == KT - 1))
                mm.then_inc(s["tok_mm"], 1)
            pe.wait_ge(s["tok_sb"], KT)
            for o in range(8):
                for k in range(KT):
                    mm = pe.matmul(ps[2][:, o * B:(o + 1) * B], t["wk"][:, k, o * P:(o + 1) * P], t["tok"][:, k, :],
                                   start=(k == 0), stop=(k == KT - 1))
            mm.then_inc(s["kv_mm"], 1)
            for g in range(2):
                for k in range(KT):
                    mm = pe.matmul(ps[3 + g][0:B, :], t["tok"][:, k, :], t["wv"][:, k, g * 512:(g + 1) * 512],
                                   start=(k == 0), stop=(k == KT - 1))
                mm.then_inc(s["kv_mm"], 1)


def setup_layer2(nc, keep, tmp, io, fetch):
    W = tiles(nc, keep, "w2", {
        "wq": (P, KT, 1024), "wk": ("pair", P, KT, H), "wv": (P, KT, H), "wo": ("pair", P, 8, H), "ident": (P, P), "gain": (P, KT),
        "cosq": (P, T), "sinq": (P, T), "cosk": (P, C), "sink": (P, C)})
    t = tiles(nc, tmp, "t2", {"wk": (P, KT, H), "wo": (P, 8, H)})
    fetch.loads += [
        (W["wq"][:, :, :], rows(io["L2_Wq"])), (t["wk"][:, :, :], rows(io["L2_Wk"])), (W["wv"][:, :, :], rows(io["L2_Wv"])),
        (t["wo"][:, :, :], rows(io["L2_Wo"])), (W["ident"][:, :], io["ident"]), (W["gain"][:, :], io["L2_gain"]),
        (W["cosq"][:, :], io["cos8"][:, 0:T]), (W["sinq"][:, :], io["sin8"][:, 0:T]),
        (W["cosk"][:, :], io["cos"]), (W["sink"][:, :], io["sin"])]

    def finish():
        prepare(nc, "s2", fetch, scales=[(w, w, W["gain"]) for w in (W["wq"], t["wk"], W["wv"])],
                splits=[(t["wk"][:, :, :], W["wk"][0][:, :, :], W["wk"][1][:, :, :]), (t["wo"][:, :, :], W["wo"][0][:, :, :], W["wo"][1][:, :, :])])
        return W

    return finish


def setup_layer3(nc, keep, tmp, io, fetch):
    W = tiles(nc, keep, "w3", {
        "wq": (P, KT, 512), "wk": ("pair", P, KT, 512), "wv": (P, KT, H), "wo": (P, KT, H), "ident": (P, P), "gq": (P, KT), "gkv": (P, KT),
        "neg": (P, 1)})
    t = tiles(nc, tmp, "t3", {"wk": (P, KT, 512)})
    fetch.loads += [
        (W["wq"][:, :, :], rows(io["L3_Wq"])), (t["wk"][:, :, :], rows(io["L3_Wk"])), (W["wv"][:, :, :], rows(io["L3_Wv"])),
        (W["wo"][:, :, :], rows(io["L3_Wo"])), (W["ident"][:, :], io["ident"]), (W["gq"][:, :], io["L3_gq"]),
        (W["gkv"][:, :], io["L3_gkv"]), (W["neg"][:, :], io["neg"])]

    def finish():
        prepare(nc, "s3", fetch, scales=[(W["wq"], W["wq"], W["gq"]), (t["wk"], t["wk"], W["gkv"]), (W["wv"], W["wv"], W["gkv"])],
                splits=[(t["wk"][:, :, :], W["wk"][0][:, :, :], W["wk"][1][:, :, :])])
        return W

    return finish


F_TILES = {0: [(k * P, P) for k in range(8)], 1: [(k * P, P) for k in range(5)] + [(640, 42)], 2: [(k * P, P) for k in range(8)]}


def setup_feed_forward(nc, keep, tmp, io, fetch, n):
    ftiles = F_TILES[n]
    NF, width = len(ftiles), ftiles[-1][0] + ftiles[-1][1]
    cols = width if n == 0 else 2 * width
    shapes = {"w1": ("pair", P, KT, cols), "w2": ("pair", P, NF, H), "ident": (P, P), "b1": (P, NF), "bg": (P, NF)}
    shapes.update({0: {k: (T, H) for k in ("gamma1", "beta1", "gamma2", "beta2", "b2")},
                   1: {"b2": (T, H), "gain": (P, KT)}, 2: {"gq": (T, H), "bo": (T, H), "gain": (P, KT)}}[n])
    W = tiles(nc, keep, f"wf{n}", shapes, side="right")
    raw = tiles(nc, tmp, f"sf{n}", {"w1": (P, KT, cols), "w2": (P, NF, H)}, side="right")
    fetch.loads += [(W["ident"][:, :], io["ident"])]
    if n == 2:
        fetch.loads += [(raw["w1"][:, :, 0:width], rows(io["L2_Wup"])), (raw["w1"][:, :, width:cols], rows(io["L2_Wgate"]))]
    else:
        fetch.loads.append((raw["w1"][:, :, :], rows(io[f"F{n}_W1"])))
    whole = [f for f, (f0, fn) in enumerate(ftiles) if fn == P]
    nw = len(whole)
    fetch.loads.append((raw["w2"][:, 0:nw, :], rows(io[f"F{n}_W2"][0:nw * P, :])))
    for f, (f0, fn) in enumerate(ftiles):
        if fn < P:
            fetch.loads.append((raw["w2"][0:fn, f, :], io[f"F{n}_W2"][f0:f0 + fn, :]))
    if n < 2:
        for k in ["b1"] if n == 0 else ["b1", "bg"]:
            fetch.loads.append((W[k][:, :], io[f"F{n}_{k}"]))
        fetch.loads.append((W["b2"][:, :], spread(io[f"F{n}_b2"], T)))
    if n == 0:
        for k in ("gamma1", "beta1", "gamma2", "beta2"):
            fetch.loads.append((W[k][:, :], spread(io[f"F0_{k}"], T)))
    if n > 0:
        fetch.loads.append((W["gain"][:, :], io[f"F{n}_gain"]))
    if n == 2:
        fetch.loads += [(W[k][:, :], io["zeros"]) for k in ("b1", "bg")]
        fetch.loads += [(W["gq"][:, :], spread(io["L3_gq_row"], T)), (W["bo"][:, :], spread(io["L3_bo"], T))]
    splits = [(raw["w1"][:, kk, :], W["w1"][0][:, kk, :], W["w1"][1][:, kk, :]) for kk in range(KT)]
    splits.append(tuple(w[:, 0:nw, :] for w in (raw["w2"], *W["w2"])))
    for f, (f0, fn) in enumerate(ftiles):
        if fn < P:
            splits.append(tuple(w[0:fn, f, :] for w in (raw["w2"], *W["w2"])))
    W["f"] = width

    def finish():
        prepare(nc, f"sf{n}", fetch, scales=[(raw["w1"], raw["w1"], W["gain"])] if n else (), splits=splits)
        return W

    return finish


@contextmanager
def cleared(nc):
    before = nc.snapshot_sems()
    yield
    nc.clear_and_free_semaphores(nc.allocated_since(before))
    nc.all_engine_barrier()


class Phase:

    def __init__(self, nc, name, setup, io):
        self.nc, self.name, self.setup, self.io = nc, name, setup, io
        self.keep, self.tmp = ExitStack(), ExitStack()

    def allocate(self):
        self.fetch = Fetch(self.nc, self.name)
        self.work_out = self.setup(self.nc, self.keep, self.tmp, self.io, self.fetch)

    def finish(self):
        W = self.work_out()
        self.tmp.close()
        return W


def program(nc, io):
    dram = lambda name, shape: nc.dram_tensor(name, shape, F32).ap()
    rs, rs_rows = dram("ctx_rs", (B, CP)), dram("ctx_rs_rows", (CT, B, NCT))
    sums, memv = dram("ctx_sums", (KT, P, B)), dram("mem_values", (B, 1024))
    segscr = dram("seg_skew", (T, NR))
    relpos = [dram(f"relpos_skew{g}", (T, 4, NR)) for g in range(2)]
    y = dram("attn_out", (B, T, H))
    x = [dram(f"x_{n}", (B, T, H)) for n in range(3)]
    xT = [dram(f"x_normT_{n}", (B, H, T)) for n in range(3)]
    io = dict(io, sums=sums, memv=memv, segscr=segscr)

    streams = [dict(ctxT=io["ctxT"], xT=io["xT"], res=io["x"], y=y, gscr=relpos, sums=sums),
               dict(xT=xT[0], res=x[0], y=y, memv=memv, perv=io["L1_perv"]),
               dict(ctxT=io["ctxT"], rs=rs, rs_rows=rs_rows, xT=xT[1], res=x[1], y=y, mask=io["mask"]),
               dict(ctxT=io["ctxT"], rs=rs, rs_rows=rs_rows, xT=xT[2], res=x[2], y=io["out"])]
    guards = [(1e-12, 1e-12, 1.1920929e-07), (1.1920929e-07, 1e-6, 1e-6), (1e-6, 1e-6, 1e-6)]
    attn = [Phase(nc, f"a{n}", setup, io) for n, setup in enumerate((setup_layer0, setup_layer1, setup_layer2, setup_layer3))]
    ffs = [Phase(nc, f"f{n}", partial(setup_feed_forward, n=n), io) for n in range(3)]

    attn[0].allocate()
    with cleared(nc), ExitStack() as ctx:
        ident = ctx.enter_context(nc.sbuf_tensor("c_ident", [P, P], F32))
        own = Fetch(nc, "ident")
        own.loads.append((ident[:, :], io["ident"]))
        context_pass(nc, ctx, ident, dict(ctx=io["ctx"], rs=rs, rs_rows=rs_rows, ident=own, ahead=attn[0].fetch))
    for n, L in enumerate(LAYERS):
        if n in (1, 2):
            ffs[n].allocate()
        with cleared(nc), ExitStack() as ctx:
            W = attn[n].finish()
            attention(nc, ctx, L, W, dict(streams[n], ahead=ffs[n].fetch if n in (1, 2) else None))
        attn[n].keep.close()
        if n == 3:
            break
        if n == 0:
            ffs[n].allocate()
        attn[n + 1].allocate()
        with cleared(nc), ExitStack() as ctx:
            W = ffs[n].finish()
            feed_forward(nc, ctx, n, W["ident"], W, dict(y=y, x_next=x[n], xT_next=xT[n], ahead=attn[n + 1].fetch),
                         *guards[n], F_TILES[n])
        ffs[n].keep.close()


def kernel(**inputs):
    import numpy as _np
    import concourse.bacc as _bacc
    from concourse import mybir as _mybir
    from concourse.bass_utils import run_bass_kernel_spmd as _run

    a = {k.replace("_xattn", ""): _np.asarray(v) for k, v in inputs.items()}
    f32 = _np.float32
    pairs = _np.concatenate([h * 64 + _np.r_[0:64:2, 1:64:2] for h in range(16)])
    qkv = a["L1_to_qkv_w"]
    per_row = lambda v: v.reshape(KT, P).T
    per_unit = lambda v: _np.pad(v, (0, -len(v) % P)).reshape(-1, P).T
    E = _np.zeros((P, 8, 4), a["L0_segment_encoding"].dtype)
    for s in range(2):
        for r in range(2):
            E[64 * r:64 * r + 64, :, 2 * s + r] = a["L0_segment_encoding"][s].reshape(8, 2, 64)[:, r, :].T
    doubled = lambda w: _np.repeat(w.T.reshape(H, 16, 1, 16), 2, axis=2).reshape(H, 512)
    freq = (f32(1.0) / f32(10000.0) ** (_np.arange(0, 64, 2, dtype=f32) / f32(64)))[_np.arange(P) % 32]
    angle = _np.arange(C, dtype=f32)[None, :] * freq[:, None]
    side = _np.where(_np.arange(P) // 32 % 2 == 0, f32(-1), f32(1))[:, None]
    cos, sin = _np.cos(angle).astype(f32), (_np.sin(angle) * side).astype(f32)
    causal = _np.concatenate([_np.where(_np.arange(T)[:, None] >= _np.arange(T)[None, :], f32(0), f32(NEG)), _np.zeros((T, 32), f32)], 1)
    arrays = {
        "ident": _np.eye(P, dtype=f32), "zeros": _np.zeros((P, 8), f32),
        "neg": _np.where(_np.arange(P) % 32 >= 16, f32(-1), f32(0))[:, None],
        "cos": cos, "sin": sin, "cos8": (cos / 8).astype(f32), "sin8": (sin / 8).astype(f32), "causal": causal.astype(f32),
        "x": a["x"], "xT": a["x"].transpose(0, 2, 1), "ctx": a["ctx_1024"], "ctxT": a["ctx_1024"].transpose(0, 2, 1),
        "cmask": a["mask_1x1xSxS2_ff0"][0, 0], "seg": a["mask_1xSxS2_bk1"][0], "mask": a["mask_Bx1xSxS2_ff0"][:, 0],
        "L0_Wq": a["L0_Wq"].reshape(H, 1024), "L0_WqT": a["L0_Wq"].reshape(H, 1024).T, "L0_Wk": a["L0_Wk"].reshape(H, 1024),
        "L0_Wv": a["L0_Wv"].reshape(H, 1024), "L0_Wr": a["L0_Wr"].reshape(H, 1024), "L0_WoT": a["L0_Wo"].reshape(H, 1024).T,
        "L0_posT": a["L0_position_encoding"][0].T[:, 1:1 + NR], "L0_segE": E, "L0_segb": a["L0_segment_bias"].reshape(8, P).T,
        "L0_posb": a["L0_position_bias"].reshape(8, P).T, "L0_contb": a["L0_content_bias"].reshape(8, P).T,
        "F0_W1": a["L0_W1"], "F0_b1": per_unit(a["L0_b1"]), "F0_W2": a["L0_W2"], "F0_b2": a["L0_b2"],
        "F0_gamma1": a["L0_ln1_gamma"], "F0_beta1": a["L0_ln1_beta"], "F0_gamma2": a["L0_ln2_gamma"], "F0_beta2": a["L0_ln2_beta"],
        "L1_Wq": qkv[:, 0:1024][:, pairs], "L1_Wk": qkv[:, 1024:2048][:, pairs], "L1_Wv": qkv[:, 2048:3072],
        "L1_Wo": a["L1_to_out_w"], "L1_gain": per_row(a["L1_attn_norm_w"]), "L1_Wm": a["L1_to_mem_tokens_w"],
        "L1_poolw": per_row(a["L1_mem_pool_norm_w"]),
        "L1_perk": a["L1_persist_mem"].transpose(0, 2, 1).reshape(1024, 16)[pairs].reshape(8, P, 16).transpose(1, 0, 2),
        "L1_perv": a["L1_persist_mem"].transpose(1, 0, 2),
        "F1_W1": a["L1_ff_w1"], "F1_b1": per_unit(a["L1_ff_b1"][:682]), "F1_bg": per_unit(a["L1_ff_b1"][682:]), "F1_W2": a["L1_ff_w2"], "F1_b2": a["L1_ff_b2"], "F1_gain": per_row(a["L1_ff_norm_w"]),
        "L2_Wq": a["L2_Wq"], "L2_Wk": a["L2_Wk"], "L2_Wv": a["L2_Wv"], "L2_Wo": a["L2_Wo"], "L2_gain": per_row(a["L2_ln1_w"]),
        "L2_Wup": a["L2_Wup"], "L2_Wgate": a["L2_Wgate"], "F2_W2": a["L2_Wdown"], "F2_gain": per_row(a["L2_ln2_w"]),
        "L3_Wq": doubled(a["L3_wq"]), "L3_Wk": doubled(a["L3_wk"]), "L3_Wv": a["L3_wv"].T, "L3_Wo": a["L3_wo"].T,
        "L3_gq": per_row(a["L3_gq"]), "L3_gkv": per_row(a["L3_gkv"]), "L3_gq_row": a["L3_gq"], "L3_bo": a["L3_bo"],
    }
    arrays = {f"in_{k}": _np.ascontiguousarray(v) for k, v in arrays.items()}
    nc = _bacc.Bacc("TRN2", target_bir_lowering=False, num_devices=1)
    io = {k[3:]: nc.dram_tensor(k, v.shape, _mybir.dt.from_np(v.dtype), kind="ExternalInput").ap() for k, v in arrays.items()}
    io["out"] = nc.dram_tensor("out", (B, T, H), F32, kind="ExternalOutput").ap()
    program(nc, io)
    return _run(nc, [arrays], core_ids=[0]).results[0]["out"]
```
